# Optimizing a Trainium2 kernel written in Bass

```python
import numpy as np
import jax
import jax.numpy as jnp

def _softmax(x, axis=-1):
    return jax.nn.softmax(x, axis=axis)

def _gelu(x):
    return jax.nn.gelu(x, approximate=True)

def _silu(x):
    return jax.nn.silu(x)

def _sigmoid(x):
    return jax.nn.sigmoid(x)

def _layernorm(x, axis=-1, eps=1e-05):
    m = jnp.mean(x, axis=axis, keepdims=True)
    v = jnp.var(x, axis=axis, keepdims=True)
    return (x - m) / jnp.sqrt(v + eps)

def _scatter_add(tgt, idx, src, axis=0):
    return tgt.at[idx].add(src)

def _segment_sum(src, seg, n):
    return jax.ops.segment_sum(src, seg, n)
kernel_name = 'mk_conv_preact_d2_conv_nchw512_r2_ba38c7'

def setup_inputs(seed: int=0):
    np.random.seed(seed)
    _w = jnp.asarray

    def _rec_inputs():
        import jax
        import jax.numpy as jnp
        _gk = jax.random.key(seed)
        x = 7.22e-05 + 1 * jax.random.normal(jax.random.fold_in(_gk, 1), (4, 256, 32, 32), jnp.float32)
        return x
    x = _rec_inputs()

    def _L0_conv_setup():
        import jax, jax.numpy as jnp
        import numpy as np
        B, DIM, H, W = (4, 256, 32, 32)
        NH = 8
        HD = DIM // NH
        CS = 16
        BASE_LR = 1.0
        EPS_IN = 1e-06
        EPS_OUT = 1e-05

        def _ln(x, g, b, eps):
            mu = x.mean(-1, keepdims=True)
            var = ((x - mu) ** 2).mean(-1, keepdims=True)
            return (x - mu) / jnp.sqrt(var + eps) * g + b

        def _ln_l2_bwd(Z, tgt, g, b):
            D = Z.shape[-1]
            mu = Z.mean(-1, keepdims=True)
            var = ((Z - mu) ** 2).mean(-1, keepdims=True)
            std = jnp.sqrt(var + EPS_IN)
            xh = (Z - mu) / std
            gxh = (g * xh + b - tgt) * g
            return (D * gxh - gxh.sum(-1, keepdims=True) - xh * (gxh * xh).sum(-1, keepdims=True)) / (D * std)

        def _rope(x, L):
            inv = 1.0 / 10000.0 ** (jnp.arange(0, HD, 2, dtype=jnp.float32) / HD)
            fr = jnp.arange(L, dtype=jnp.float32)[:, None] * inv[None, :]
            emb = jnp.concatenate([fr, fr], axis=-1)
            cos, sin = (jnp.cos(emb), jnp.sin(emb))
            x1, x2 = jnp.split(x, 2, axis=-1)
            return x * cos + jnp.concatenate([-x2, x1], axis=-1) * sin

        def _ttt_linear(xn, q_w, k_w, v_w, o_w, W1, b1, ttt_ln_w, ttt_ln_b, lr_w, lr_b, tok_idx_delta, post_w, post_b):
            Bsz, L, _ = xn.shape
            NC = L // CS
            heads = lambda t: t.reshape(Bsz, L, NH, HD).transpose(0, 2, 1, 3)
            XQ = _rope(heads(xn @ q_w.T), L)
            XK = _rope(heads(xn @ k_w.T), L)
            XV = heads(xn @ v_w.T)
            Xc = xn.reshape(Bsz, NC, CS, DIM)
            ttt_lr = jax.nn.sigmoid(jnp.einsum('bnkc,hdc->bhnkd', Xc, lr_w) + lr_b.reshape(1, NH, 1, 1, 1))
            ttt_lr_eta = BASE_LR / HD * ttt_lr.transpose(0, 1, 2, 4, 3)
            token_idx = jnp.maximum(1.0 / jnp.arange(1, CS + 1, dtype=jnp.float32) + tok_idx_delta, 0.0)
            eta = token_idx.reshape(1, 1, 1, CS, 1) * ttt_lr_eta
            g = ttt_ln_w[None, :, None, :]
            bb = ttt_ln_b[None, :, None, :]

            def step(carry, inp):
                W1c, b1c = carry
                xq, xk, xv, et = inp
                Z1 = xk @ W1c + b1c
                grad = _ln_l2_bwd(Z1, xv - xk, g, bb)
                Attn1 = jnp.tril(xq @ xk.swapaxes(-1, -2))
                b1_bar = b1c - jnp.tril(et) @ grad
                Z1_bar = xq @ W1c - et * Attn1 @ grad + b1_bar
                last_eta = et[..., -1, :, None]
                W1n = W1c - (last_eta * xk).swapaxes(-1, -2) @ grad
                b1n = b1c - (last_eta * grad).sum(-2, keepdims=True)
                return ((W1n, b1n), xq + _ln(Z1_bar, g, bb, EPS_IN))
            W1_0 = jnp.broadcast_to(W1[None], (Bsz, NH, HD, HD)) + 0.0
            b1_0 = jnp.broadcast_to(b1[None], (Bsz, NH, 1, HD)) + 0.0
            chunk = lambda t: t.reshape(Bsz, NH, NC, CS, HD).transpose(2, 0, 1, 3, 4)
            _, out = jax.lax.scan(step, (W1_0, b1_0), (chunk(XQ), chunk(XK), chunk(XV), eta.transpose(2, 0, 1, 3, 4)))
            out = out.transpose(1, 2, 0, 3, 4).reshape(Bsz, NH, L, HD).transpose(0, 2, 1, 3).reshape(Bsz, L, DIM)
            return _ln(out, post_w, post_b, EPS_IN) @ o_w.T
        key = jax.random.key(seed)
        ks = jax.random.split(key, 8)
        r = lambda k, s: 0.02 * jax.random.normal(k, s, dtype=jnp.float32)
        return {'x': jax.random.normal(ks[0], (B, DIM, H, W), dtype=jnp.float32), 'ln_w': jnp.ones((DIM,), jnp.float32), 'ln_b': jnp.zeros((DIM,), jnp.float32), 'q_w': r(ks[1], (DIM, DIM)), 'k_w': r(ks[2], (DIM, DIM)), 'v_w': r(ks[3], (DIM, DIM)), 'o_w': r(ks[4], (DIM, DIM)), 'W1': r(ks[5], (NH, HD, HD)), 'b1': jnp.zeros((NH, 1, HD), jnp.float32), 'ttt_ln_w': jnp.ones((NH, HD), jnp.float32), 'ttt_ln_b': jnp.zeros((NH, HD), jnp.float32), 'lr_w': r(ks[6], (NH, 1, DIM)), 'lr_b': jnp.zeros((NH, 1, 1), jnp.float32), 'tok_idx_delta': jnp.zeros((CS,), jnp.float32), 'post_w': jnp.ones((DIM,), jnp.float32), 'post_b': jnp.zeros((DIM,), jnp.float32)}
    _L0_conv_all = _L0_conv_setup()
    _L0_conv_in = {k: v for k, v in _L0_conv_all.items() if k in ('ln_w', 'ln_b', 'q_w', 'k_w', 'v_w', 'o_w', 'W1', 'b1', 'ttt_ln_w', 'ttt_ln_b', 'lr_w', 'lr_b', 'tok_idx_delta', 'post_w', 'post_b')}
    del _L0_conv_all

    def _L1_conv_setup():
        import jax, jax.numpy as jnp
        import numpy as np
        KERNEL_SIZE = 5
        EPS = 1e-06

        def spatial_descriptor(x, k):
            b, c, h, w = x.shape
            p = k // 2
            xp = jnp.pad(x, ((0, 0), (0, 0), (p, p), (p, p)))
            corrs = [jnp.sum(x * jax.lax.dynamic_slice(xp, (0, 0, di, dj), (b, c, h, w)), axis=1) for di in range(k) for dj in range(k)]
            return jnp.stack(corrs, axis=1)
        key = jax.random.key(seed)
        k1, k2 = jax.random.split(key)
        b, c, h, w = (16, 256, 32, 32)
        hidden = 256
        input_dim = c + KERNEL_SIZE * KERNEL_SIZE
        x = jax.random.normal(k1, (b, c, h, w), dtype=jnp.float32)
        W = jax.random.normal(k2, (hidden, input_dim), dtype=jnp.float32) * (1.0 / np.sqrt(input_dim))
        bias = jnp.zeros((hidden,), dtype=jnp.float32)
        return {'x': x, 'W': W, 'bias': bias}
    _L1_conv_all = _L1_conv_setup()
    _L1_conv_in = {k: v for k, v in _L1_conv_all.items() if k in ('W', 'bias')}
    del _L1_conv_all
    return {'x': x, 'L0_conv_ln_w': _L0_conv_in['ln_w'], 'L0_conv_ln_b': _L0_conv_in['ln_b'], 'L0_conv_q_w': _L0_conv_in['q_w'], 'L0_conv_k_w': _L0_conv_in['k_w'], 'L0_conv_v_w': _L0_conv_in['v_w'], 'L0_conv_o_w': _L0_conv_in['o_w'], 'L0_conv_W1': _L0_conv_in['W1'], 'L0_conv_b1': _L0_conv_in['b1'], 'L0_conv_ttt_ln_w': _L0_conv_in['ttt_ln_w'], 'L0_conv_ttt_ln_b': _L0_conv_in['ttt_ln_b'], 'L0_conv_lr_w': _L0_conv_in['lr_w'], 'L0_conv_lr_b': _L0_conv_in['lr_b'], 'L0_conv_tok_idx_delta': _L0_conv_in['tok_idx_delta'], 'L0_conv_post_w': _L0_conv_in['post_w'], 'L0_conv_post_b': _L0_conv_in['post_b'], 'L1_conv_W': _L1_conv_in['W'], 'L1_conv_bias': _L1_conv_in['bias']}

def reference(x, L0_conv_ln_w, L0_conv_ln_b, L0_conv_q_w, L0_conv_k_w, L0_conv_v_w, L0_conv_o_w, L0_conv_W1, L0_conv_b1, L0_conv_ttt_ln_w, L0_conv_ttt_ln_b, L0_conv_lr_w, L0_conv_lr_b, L0_conv_tok_idx_delta, L0_conv_post_w, L0_conv_post_b, L1_conv_W, L1_conv_bias):
    import jax
    import jax.numpy as jnp

    def _L0_conv_ref(x, ln_w, ln_b, q_w, k_w, v_w, o_w, W1, b1, ttt_ln_w, ttt_ln_b, lr_w, lr_b, tok_idx_delta, post_w, post_b):
        import jax, jax.numpy as jnp
        import numpy as np
        B, DIM, H, W = (4, 256, 32, 32)
        NH = 8
        HD = DIM // NH
        CS = 16
        BASE_LR = 1.0
        EPS_IN = 1e-06
        EPS_OUT = 1e-05

        def _ln(x, g, b, eps):
            mu = x.mean(-1, keepdims=True)
            var = ((x - mu) ** 2).mean(-1, keepdims=True)
            return (x - mu) / jnp.sqrt(var + eps) * g + b

        def _ln_l2_bwd(Z, tgt, g, b):
            D = Z.shape[-1]
            mu = Z.mean(-1, keepdims=True)
            var = ((Z - mu) ** 2).mean(-1, keepdims=True)
            std = jnp.sqrt(var + EPS_IN)
            xh = (Z - mu) / std
            gxh = (g * xh + b - tgt) * g
            return (D * gxh - gxh.sum(-1, keepdims=True) - xh * (gxh * xh).sum(-1, keepdims=True)) / (D * std)

        def _rope(x, L):
            inv = 1.0 / 10000.0 ** (jnp.arange(0, HD, 2, dtype=jnp.float32) / HD)
            fr = jnp.arange(L, dtype=jnp.float32)[:, None] * inv[None, :]
            emb = jnp.concatenate([fr, fr], axis=-1)
            cos, sin = (jnp.cos(emb), jnp.sin(emb))
            x1, x2 = jnp.split(x, 2, axis=-1)
            return x * cos + jnp.concatenate([-x2, x1], axis=-1) * sin

        def _ttt_linear(xn, q_w, k_w, v_w, o_w, W1, b1, ttt_ln_w, ttt_ln_b, lr_w, lr_b, tok_idx_delta, post_w, post_b):
            Bsz, L, _ = xn.shape
            NC = L // CS
            heads = lambda t: t.reshape(Bsz, L, NH, HD).transpose(0, 2, 1, 3)
            XQ = _rope(heads(xn @ q_w.T), L)
            XK = _rope(heads(xn @ k_w.T), L)
            XV = heads(xn @ v_w.T)
            Xc = xn.reshape(Bsz, NC, CS, DIM)
            ttt_lr = jax.nn.sigmoid(jnp.einsum('bnkc,hdc->bhnkd', Xc, lr_w) + lr_b.reshape(1, NH, 1, 1, 1))
            ttt_lr_eta = BASE_LR / HD * ttt_lr.transpose(0, 1, 2, 4, 3)
            token_idx = jnp.maximum(1.0 / jnp.arange(1, CS + 1, dtype=jnp.float32) + tok_idx_delta, 0.0)
            eta = token_idx.reshape(1, 1, 1, CS, 1) * ttt_lr_eta
            g = ttt_ln_w[None, :, None, :]
            bb = ttt_ln_b[None, :, None, :]

            def step(carry, inp):
                W1c, b1c = carry
                xq, xk, xv, et = inp
                Z1 = xk @ W1c + b1c
                grad = _ln_l2_bwd(Z1, xv - xk, g, bb)
                Attn1 = jnp.tril(xq @ xk.swapaxes(-1, -2))
                b1_bar = b1c - jnp.tril(et) @ grad
                Z1_bar = xq @ W1c - et * Attn1 @ grad + b1_bar
                last_eta = et[..., -1, :, None]
                W1n = W1c - (last_eta * xk).swapaxes(-1, -2) @ grad
                b1n = b1c - (last_eta * grad).sum(-2, keepdims=True)
                return ((W1n, b1n), xq + _ln(Z1_bar, g, bb, EPS_IN))
            W1_0 = jnp.broadcast_to(W1[None], (Bsz, NH, HD, HD)) + 0.0
            b1_0 = jnp.broadcast_to(b1[None], (Bsz, NH, 1, HD)) + 0.0
            chunk = lambda t: t.reshape(Bsz, NH, NC, CS, HD).transpose(2, 0, 1, 3, 4)
            _, out = jax.lax.scan(step, (W1_0, b1_0), (chunk(XQ), chunk(XK), chunk(XV), eta.transpose(2, 0, 1, 3, 4)))
            out = out.transpose(1, 2, 0, 3, 4).reshape(Bsz, NH, L, HD).transpose(0, 2, 1, 3).reshape(Bsz, L, DIM)
            return _ln(out, post_w, post_b, EPS_IN) @ o_w.T
        Bsz, d = x.shape[:2]
        n_tok = x.shape[2] * x.shape[3]
        xf = x.reshape(Bsz, d, n_tok).transpose(0, 2, 1)
        xn = _ln(xf, ln_w, ln_b, EPS_OUT)
        y = _ttt_linear(xn, q_w, k_w, v_w, o_w, W1, b1, ttt_ln_w, ttt_ln_b, lr_w, lr_b, tok_idx_delta, post_w, post_b)
        return y.transpose(0, 2, 1).reshape(x.shape)

    def _L1_conv_ref(x, W, bias):
        import jax, jax.numpy as jnp
        import numpy as np
        KERNEL_SIZE = 5
        EPS = 1e-06

        def spatial_descriptor(x, k):
            b, c, h, w = x.shape
            p = k // 2
            xp = jnp.pad(x, ((0, 0), (0, 0), (p, p), (p, p)))
            corrs = [jnp.sum(x * jax.lax.dynamic_slice(xp, (0, 0, di, dj), (b, c, h, w)), axis=1) for di in range(k) for dj in range(k)]
            return jnp.stack(corrs, axis=1)
        k = KERNEL_SIZE
        gs = spatial_descriptor(x, k)
        norm = jnp.sqrt(jnp.sum(gs * gs, axis=1, keepdims=True) + EPS)
        gs = gs / norm
        feat = jnp.concatenate([x, gs], axis=1)
        out = jnp.einsum('bchw,oc->bohw', feat, W) + bias[None, :, None, None]
        return jax.nn.relu(out)

    def _gn(v, G=32, eps=1e-05):
        B_, C_, H_, W_ = v.shape
        g = v.reshape(B_, G, C_ // G, H_, W_)
        m = jnp.mean(g, axis=(2, 3, 4), keepdims=True)
        s = jnp.var(g, axis=(2, 3, 4), keepdims=True)
        return ((g - m) / jnp.sqrt(s + eps)).reshape(v.shape)

    def _ln_c(v, eps=1e-06):
        m = jnp.mean(v, axis=1, keepdims=True)
        s = jnp.var(v, axis=1, keepdims=True)
        return (v - m) / jnp.sqrt(s + eps)

    def _ln_t(v, eps=1e-05):
        m = jnp.mean(v, axis=-1, keepdims=True)
        s = jnp.var(v, axis=-1, keepdims=True)
        return (v - m) / jnp.sqrt(s + eps)

    def _to_tokens(v):
        B_, C_, H_, W_ = v.shape
        return v.reshape(B_, C_, H_ * W_).transpose(0, 2, 1)

    def _from_tokens(t, like):
        B_, C_, H_, W_ = like.shape
        return t.transpose(0, 2, 1).reshape(B_, C_, H_, W_)
    x = x + _L0_conv_ref(_gn(x), L0_conv_ln_w, L0_conv_ln_b, L0_conv_q_w, L0_conv_k_w, L0_conv_v_w, L0_conv_o_w, L0_conv_W1, L0_conv_b1, L0_conv_ttt_ln_w, L0_conv_ttt_ln_b, L0_conv_lr_w, L0_conv_lr_b, L0_conv_tok_idx_delta, L0_conv_post_w, L0_conv_post_b)
    x = x + _L1_conv_ref(_gn(x), L1_conv_W, L1_conv_bias)
    return x

_drawn_inputs = setup_inputs


def setup_inputs(seed=0):
    import zlib

    import numpy as np

    out = dict(_drawn_inputs(seed))
    spreads = {'L0_conv_ln_w': (1.0, 0.2),
     'L0_conv_ln_b': (0.0, 0.1),
     'L0_conv_b1': (0.0, 0.1),
     'L0_conv_ttt_ln_w': (1.0, 0.2),
     'L0_conv_ttt_ln_b': (0.0, 0.1),
     'L0_conv_lr_b': (0.0, 2.0),
     'L0_conv_tok_idx_delta': (0.0, 0.1),
     'L0_conv_post_w': (1.0, 0.2),
     'L0_conv_post_b': (0.0, 0.1),
     'L1_conv_bias': (0.0, 0.1)}
    factors = {'L0_conv_lr_w': 3.07}
    for name, (base, spread) in spreads.items():
        noise = np.random.default_rng([zlib.crc32(name.encode()), seed]).standard_normal(out[name].shape)
        drawn = base * np.exp(spread * noise) if base else spread * noise
        out[name] = jnp.asarray(drawn.astype(out[name].dtype))
    for name, factor in factors.items():
        out[name] = (out[name] * factor).astype(out[name].dtype)
    return out
```

```python
from contextlib import ExitStack

import numpy as np

import concourse.bass as bass
from concourse import mybir

F32 = mybir.dt.float32
ALU = mybir.AluOpType
ACT = mybir.ActivationFunctionType
AX = mybir.AxisListType
ds = bass.ds

P = 128
B, C, H, W_ = 4, 256, 32, 32
N = H * W_
NT = B * N
J = C // P
NH, HD, CS = 8, 32, 16
NC = N // CS
E = 2
BLK = 512
NBLK = NT // BLK
PER = N // BLK
GROUP = 8
KS = 5
S = KS * KS
PAD = KS // 2
RB = 4
NRB = H // RB
RW = RB + 2 * PAD
XW = W_ + 2 * PAD

EPS_GN, EPS_LN, EPS_IN, EPS_NORM = 1e-5, 1e-5, 1e-6, 1e-6

CONST = dict(ident=P, mean_c=P, mean_g=P, chunk_ones=P, emask=E, emask_k=E, causal=E * CS, headmask=NH, inv_t=CS,
             shift_on=7, shift_off=7, spread=8 * P)
PARAM = dict(ln_w=J, ln_b=J, post_w=J, post_b=J, conv_b=J, g=E, bb=E, g_row=HD, b1_row=HD,
             delta=CS, lr_b=1, w1=J * HD)


def columns(widths):
    at, out = 0, {}
    for name, w in widths.items():
        out[name] = (at, w)
        at += w
    return out, at


CONST_AT, NCONST = columns(CONST)
PARAM_AT, NPARAM = columns(PARAM)


def build(nc, x, out, wq, wk, wv, wo, wlr, wx, ws, params, consts, rope):
    ctx = ExitStack()
    with ctx:
        def sb(name, shape):
            return ctx.enter_context(nc.sbuf_tensor(name, shape, F32))

        def sem(name):
            return ctx.enter_context(nc.semaphore(name))

        X = sb("X", [P, J, NT])
        KP = sb("KP", [P, J, NT])
        QP = sb("QP", [P, J, NT])
        KN = sb("KN", [P, J, NT])
        TT = sb("TT", [P, J, NT])
        par = sb("par", [P, NPARAM])
        small = sb("small", [P, 512])
        lrh = sb("lrh", [P, NC, B])
        wsm = sb("wsm", [P, J, C])
        work = sb("work", [P, 6720])

        def pcol(name, i=0, n=1, rows=P):
            at = PARAM_AT[name][0] + i
            return par[0:rows, at:at + n]

        used = [0]

        def scol(n):
            used[0] += n
            assert used[0] <= 512
            return small[:, used[0] - n:used[0]]

        gn_a, gn_c = scol(B * J), scol(B * J)
        eps5, eps6 = scol(1), scol(1)
        neg_g, bbg = scol(E), scol(E)
        g2row = scol(HD)
        amask = scol(E * CS)
        upd_mask = scol(E)
        w0 = scol(J * HD)
        b0 = scol(HD)
        stat = scol(J * B * 2 * 6)
        mv = scol(J * B * 2)
        gm = scol(J * B * 2)
        gdev = scol(J * B)
        tok = scol(CS)
        neg_mean = scol(B)

        counts = []

        def value(eng, v):
            if isinstance(v, int):
                return v
            r = eng.alloc_register(f"count{len(counts)}")
            counts.append(r)
            eng.reg_mov(r, v)
            return eng.snap(r, min_val=1, max_val=1 << 12)

        class Carve:
            def __init__(self):
                self.at = 0

            def __call__(self, *dims):
                n = int(np.prod(dims))
                v = work[:, self.at:self.at + n]
                self.at += n
                assert self.at <= work.shape[1], self.at
                if len(dims) == 1:
                    return v
                names = "abcdef"[:len(dims)]
                return v.rearrange(f"p ({' '.join(names)}) -> p {' '.join(names)}",
                                   **dict(zip(names, dims)))

        PS = ctx.enter_context(nc.psum_tensor("PS", [P, 8, BLK], F32))

        cst = sb("cst", [P, NCONST])
        ones_blk = sb("ones_blk", [P, P])

        def ccol(name, i=0, n=None, rows=P):
            at, w = CONST_AT[name]
            n = w - i if n is None else n
            return cst[0:rows, at + i:at + i + n]

        ident, mean_c, mean_g = ccol("ident"), ccol("mean_c"), ccol("mean_g")

        def group_norm(block, src, tag, extra_vector=None, extra_loads=None):
            s_bn, s_mv, s_g1, s_gc, s_dev, s_g2, s_var, s_sd, s_r, s_a = (
                sem(f"{tag}_{n}") for n in ("bn", "mv", "g1", "gc", "dev", "g2", "var", "sd", "r", "a"))
            s_in = [sem(f"{tag}_in{b}") for b in range(B)]
            s_par = sem(f"{tag}_par")
            st = stat.rearrange("p (k s) -> p k s", s=6)

            @block.sync
            def _(sp):
                if extra_loads:
                    extra_loads(sp, s_in, s_par)

            @block.vector
            def _(dve):
                for b in range(B):
                    for j in range(J):
                        k = b * J + j
                        if extra_loads:
                            dve.wait_ge(s_in[b], 16)
                        for h in range(PER):
                            nc.vector.bn_stats(
                                st[:, PER * k + h, :],
                                src[:, j, b * N + h * BLK:b * N + (h + 1) * BLK]).then_inc(s_bn, 1)
                dve.wait_ge(s_bn, B * J * PER)
                for k in range(B * J):
                    nc.vector.bn_aggr(mv[:, 2 * k:2 * k + 2], st[:, PER * k:PER * k + PER, :]
                                      ).then_inc(s_mv, 1)
                dve.wait_ge(s_g1, 1)
                nc.vector.tensor_copy(gm, PS[:, 0, 0:2 * B * J]).then_inc(s_gc, 1)
                dve.wait_ge(s_gc, 1)
                dve.wait_ge(s_mv, B * J)
                m2 = mv.rearrange("p (k t) -> p k t", t=2)
                g2 = gm.rearrange("p (k t) -> p k t", t=2)
                nc.vector.tensor_tensor(gdev, m2[:, :, 0], g2[:, :, 0], ALU.subtract).then_inc(s_dev, 1)
                dve.wait_ge(s_dev, 1)
                nc.vector.tensor_tensor(gdev, gdev, gdev, ALU.mult).then_inc(s_dev, 1)
                dve.wait_ge(s_g2, 1)
                nc.vector.tensor_tensor(gdev, PS[:, 1, 0:B * J], g2[:, :, 1], ALU.add).then_inc(s_var, 1)
                dve.wait_ge(s_sd, 1)
                nc.vector.reciprocal(gn_a, gn_a).then_inc(s_r, 1)
                dve.wait_ge(s_r, 1)
                nc.vector.scalar_tensor_tensor(gn_c, g2[:, :, 0], -1.0, gn_a, ALU.mult, ALU.mult
                                               ).then_inc(s_a, 1)
                if extra_vector:
                    extra_vector(dve, s_par)

            @block.tensor
            def _(pe):
                if extra_loads:
                    pe.wait_ge(s_par, 32)
                pe.wait_ge(s_mv, B * J)
                nc.tensor.matmul(PS[:, 0, 0:2 * B * J], mean_g, mv, start=True, stop=True).then_inc(s_g1, 1)
                pe.wait_ge(s_dev, 2)
                nc.tensor.matmul(PS[:, 1, 0:B * J], mean_g, gdev, start=True, stop=True).then_inc(s_g2, 1)

            @block.scalar
            def _(act):
                if extra_loads:
                    act.wait_ge(s_k0, 2)
                act.wait_ge(s_var, 1)
                nc.scalar.activation(gn_a, gdev, ACT.Sqrt, bias=eps5).then_inc(s_sd, 1)

        xv = x.rearrange("b (j p) n -> p j b n", p=P)
        s_k0 = sem("s_k0")
        s_w = sem("s_w")

        def first_loads(sp, s_in, s_par):
            sp.dma_start(par[:, :], params).then_inc(s_par, 16)
            sp.dma_start(cst[:, :], consts).then_inc(s_par, 16)
            for b in range(B):
                sp.dma_start(X[:, :, b * N:(b + 1) * N], xv[:, :, b, :]).then_inc(s_in[b], 16)

        with nc.Block() as block:
            s_d = sem("derive")

            def derive(dve, s_par):
                n = [0]

                def link(ins):
                    n[0] += 1
                    ins.then_inc(s_d, 1)
                    dve.wait_ge(s_d, n[0])

                dve.wait_ge(s_par, 32)
                nc.vector.tensor_scalar(neg_g, pcol("g", 0, E), -1.0, None, ALU.mult).then_inc(s_d, 1)
                nc.vector.tensor_tensor(bbg, pcol("bb", 0, E), pcol("g", 0, E), ALU.mult).then_inc(s_d, 1)
                nc.vector.tensor_tensor(g2row, pcol("g_row", 0, HD), pcol("g_row", 0, HD), ALU.mult
                                        ).then_inc(s_d, 1)
                n[0] = 3
                link(nc.vector.tensor_tensor(tok, ccol("inv_t"), pcol("delta", 0, CS), ALU.add))
                link(nc.vector.tensor_scalar(tok, tok, 0.0, None, ALU.max))
                link(nc.vector.tensor_tensor(
                    amask.rearrange("p (e t) -> p e t", e=E),
                    ccol("causal").rearrange("p (e t) -> p e t", e=E),
                    tok.unsqueeze(1).broadcast_to([P, E, CS]), ALU.mult))
                link(nc.vector.tensor_scalar(amask, amask, -1.0, None, ALU.mult))
                link(nc.vector.tensor_scalar(upd_mask, ccol("emask"), tok[:, CS - 1:CS], -1.0,
                                             ALU.mult, ALU.mult))
                link(nc.vector.tensor_scalar(ones_blk[:, :], ccol("chunk_ones"), tok[:, CS - 1:CS], -1.0,
                                             ALU.mult, ALU.mult))
                w1 = pcol("w1", 0, J * HD).rearrange("p (j d) -> p j d", d=HD)
                link(nc.vector.tensor_reduce(gdev[:, 0:J], w1, AX.X, ALU.add))
                link(nc.vector.tensor_reduce(gdev[:, J:J + 1], pcol("b1_row", 0, HD), AX.X, ALU.add))
                link(nc.vector.scalar_tensor_tensor(
                    w0.rearrange("p (j d) -> p j d", d=HD),
                    gdev[:, 0:J].unsqueeze(2).broadcast_to([P, J, HD]), -1.0 / HD, w1, ALU.mult, ALU.add))
                link(nc.vector.scalar_tensor_tensor(
                    b0, gdev[:, J:J + 1].broadcast_to([P, HD]), -1.0 / HD, pcol("b1_row", 0, HD),
                    ALU.mult, ALU.add))

            @block.gpsimd
            def _(pool):
                pool.memset(eps5, EPS_GN).then_inc(s_k0, 1)
                pool.memset(eps6, EPS_IN).then_inc(s_k0, 1)
                pool.memset(neg_mean, -1.0 / HD).then_inc(s_k0, 1)

            group_norm(block, X, "gn1", derive, first_loads)

        carve = Carve()
        cosT, sinT = carve(N), carve(N)
        sq = carve(J, BLK)
        sd = carve(BLK)
        kc, ksw = carve(2, BLK), carve(2, BLK)
        wkv = carve(J, 2 * C)
        wl = carve(J, NH)
        wvw = wsm
        swap = [(i + HD // 2) % HD for i in range(HD)]

        def blk_of(t, i):
            return t[:, ds(i * BLK, BLK)]

        def layer_norm(tag, src, sq, sd, eps, w, b, scale):
            q = {n: sem(f"{tag}_{n}") for n in ("in", "mean", "xc", "sq", "var", "sd", "rs", "xh", "xn")}

            def tile(i, j):
                return src[:, j, ds(i * BLK, BLK)]

            def act_a(act, i):
                for j in range(J):
                    scale(act, i, j).then_inc(q["in"], 1)

            def pe_mean(pe, i, first):
                pe.wait_ge(q["in"], i * J + J)
                if not first:
                    pe.wait_ge(q["xc"], i * J)
                for j in range(J):
                    m = nc.tensor.matmul(PS[:, 0, :], mean_c, tile(i, j), start=(j == 0), stop=(j == J - 1))
                m.then_inc(q["mean"], 1)

            def dve_center(dve, i):
                dve.wait_ge(q["mean"], i + 1)
                for j in range(J):
                    nc.vector.tensor_tensor(tile(i, j), tile(i, j), PS[:, 0, :], ALU.subtract
                                            ).then_inc(q["xc"], 1)

            def act_square(act, i, first):
                if not first:
                    act.wait_ge(q["var"], i + 0)
                for j in range(J):
                    act.wait_ge(s_k0, 2)
                    act.wait_ge(q["xc"], i * J + j + 1)
                    nc.scalar.activation(sq[:, j, :], tile(i, j), ACT.Square).then_inc(q["sq"], 1)

            def pe_var(pe, i, first):
                pe.wait_ge(q["sq"], i * J + J)
                if not first:
                    pe.wait_ge(q["sd"], i + 0)
                for j in range(J):
                    m = nc.tensor.matmul(PS[:, 1, :], mean_c, sq[:, j, :], start=(j == 0), stop=(j == J - 1))
                m.then_inc(q["var"], 1)

            def act_sd(act, i, first):
                act.wait_ge(q["var"], i + 1)
                if not first:
                    act.wait_ge(q["xh"], i * J)
                nc.scalar.activation(sd, PS[:, 1, :], ACT.Sqrt, bias=eps).then_inc(q["sd"], 1)

            def dve_scale(dve, i):
                dve.wait_ge(q["sd"], i + 1)
                nc.vector.reciprocal(sd, sd).then_inc(q["rs"], 1)
                dve.wait_ge(q["rs"], i + 1)
                for j in range(J):
                    nc.vector.tensor_tensor(tile(i, j), tile(i, j), sd, ALU.mult).then_inc(q["xh"], 1)

            def act_affine(act, i):
                for j in range(J):
                    act.wait_ge(s_k0, 2)
                    act.wait_ge(q["xh"], i * J + j + 1)
                    nc.scalar.activation(tile(i, j), tile(i, j), ACT.Identity, scale=pcol(w, j),
                                         bias=pcol(b, j)).then_inc(q["xn"], 1)

            return q, tile, act_a, pe_mean, dve_center, act_square, pe_var, act_sd, dve_scale, act_affine

        ga8 = sb("ga8", [P, 2, J, NBLK])

        def spread_gn(dve, s):
            for k, src in enumerate((gn_a, gn_c)):
                for j in range(J):
                    nc.vector.tensor_copy(
                        ga8[:, k, j, :].rearrange("p (b h) -> p b h", h=PER),
                        src.rearrange("p (b j) -> p b j", j=J)[:, :, j].unsqueeze(2).broadcast_to([P, B, PER])
                    ).then_inc(s, 1)

        s_sp = sem("gn_spread")
        with nc.Block() as block:
            q1, xt, act_a, pe_mean, dve_center, act_square, pe_var, act_sd, dve_scale, act_affine = \
                layer_norm("ln1", X, sq, sd, eps5, "ln_w", "ln_b",
                           lambda act, i, j: nc.scalar.activation(
                               X[:, j, ds(i * BLK, BLK)], X[:, j, ds(i * BLK, BLK)], ACT.Identity,
                               scale=ga8[:, 0, j, ds(i, 1)], bias=ga8[:, 1, j, ds(i, 1)]))
            s_proj, s_kc, s_ksw, s_ksin, s_rope, s_tt, s_lr, s_kperm, s_ttf, s_rt = (
                sem(n) for n in ("proj", "kc", "ksw", "ksin", "rope", "tt", "lr", "kperm", "ttf", "ropetab"))
            NPJ = 7

            @block.sync
            def _(sp):
                sp.dma_start(wkv[:, :, 0:C], wk).then_inc(s_w, 16)
                sp.dma_start(wkv[:, :, C:2 * C], wq).then_inc(s_w, 16)
                sp.dma_start(wvw[:, :, :], wv).then_inc(s_w, 16)
                sp.dma_start(wl, wlr).then_inc(s_w, 16)
                sp.dma_start(cosT, rope[:, 0, :]).then_inc(s_rt, 16)
                sp.dma_start(sinT, rope[:, 1, :]).then_inc(s_rt, 16)

                def permute(i, first):
                    if not first:
                        sp.wait_ge(s_kperm, i * 128)
                    sp.wait_ge(s_rope, i * 2 * J + J)
                    for k in range(J):
                        for a2 in range(2):
                            for e in range(E):
                                a = 2 * k + a2
                                r = 2 * HD * a2 + HD * e
                                sp.dma_start(KN[HD * a:HD * a + HD, e, ds(i * BLK, BLK)],
                                             KP[r:r + HD, k, ds(i * BLK, BLK)]).then_inc(s_kperm, 16)
                permute(0, True)
                with sp.Fori(1, NBLK) as i:
                    permute(i, False)
                sp.wait_ge(s_kperm, NBLK * 128)

            @block.tensor
            def _(pe):
                pe.wait_ge(s_w, 64)

                def proj(i, m, first):
                    if m < 2 * J:
                        lhs = lambda j: wkv[:, j, m * P:(m + 1) * P]
                    elif m < 3 * J:
                        lhs = lambda j: wvw[:, j, (m - 2 * J) * P:(m - 2 * J + 1) * P]
                    else:
                        lhs = lambda j: wl[:, j, :]
                    if m == NPJ - 1:
                        first_tile = value(pe, i * (2 * J) + 1)
                        pe.wait_ge(s_w, 64)
                        pe.wait_ge(s_ksw, first_tile)
                        o = PS[0:NH, 2, :]
                    else:
                        o = PS[:, 2 + m, :]
                        if not first:
                            if m < 2 * J:
                                pe.wait_ge(s_ksw, (i - 1) * (2 * J) + m + 1)
                            else:
                                pe.wait_ge(s_tt, (i - 1) * J + m - 2 * J + 1)
                            if m == 0:
                                pe.wait_ge(s_lr, i + 0)
                    for j in range(J):
                        mm = nc.tensor.matmul(o, lhs(j), xt(i, j), start=(j == 0), stop=(j == J - 1))
                    mm.then_inc(s_proj, 1)

                def body(i, first, last):
                    pe.wait_ge(q1["xn"], i * J + J)
                    if not last:
                        pe_mean(pe, i + 1, False)
                    for m in range(3):
                        proj(i, m, first)
                    if not last:
                        pe_var(pe, i + 1, False)
                    for m in range(3, NPJ):
                        proj(i, m, first)

                pe_mean(pe, 0, True)
                pe_var(pe, 0, True)
                body(0, True, False)
                with pe.Fori(1, NBLK - 1) as i:
                    body(i, False, False)
                body(NBLK - 1, False, True)

            @block.vector
            def _(dve):
                def rope_in(i, m, first):
                    t = m % 2
                    dve.wait_ge(s_proj, i * NPJ + m + 1)
                    if not (first and m < 2):
                        dve.wait_ge(s_rope, i * (2 * J) + m - 1)
                    h = ds((i % PER) * BLK, BLK)
                    nc.vector.tensor_tensor(kc[:, t, :], PS[:, 2 + m, :], cosT[:, h], ALU.mult).then_inc(s_kc, 1)
                    nc.vector.stream_shuffle(ksw[:, t, :], PS[:, 2 + m, :], swap).then_inc(s_ksw, 1)

                def finish_target(i):
                    dve.wait_ge(s_kperm, i * 128 + 128)
                    for j in range(J):
                        dve.wait_ge(s_tt, i * J + j + 1)
                        nc.vector.scalar_tensor_tensor(TT[:, j, ds(i * BLK, BLK)], KN[:, j, ds(i * BLK, BLK)],
                                                       pcol("g", j), TT[:, j, ds(i * BLK, BLK)],
                                                       ALU.mult, ALU.add).then_inc(s_ttf, 1)

                def body(i, first, last):
                    if not last:
                        dve_center(dve, i + 1)
                    for m in range(2):
                        rope_in(i, m, first)
                    if not last:
                        dve_scale(dve, i + 1)
                    for m in range(2, 2 * J):
                        rope_in(i, m, first)
                    if not first:
                        finish_target(i - 1)

                spread_gn(dve, s_sp)
                dve.wait_ge(s_rt, 32)
                dve_center(dve, 0)
                dve_scale(dve, 0)
                body(0, True, False)
                with dve.Fori(1, NBLK - 1) as i:
                    body(i, False, False)
                body(NBLK - 1, False, True)
                finish_target(NBLK - 1)

            @block.gpsimd
            def _(pool):
                def rope_out(i, m):
                    t = m % 2
                    dst = (KP if m < J else QP)[:, m % J, ds(i * BLK, BLK)]
                    h = ds((i % PER) * BLK, BLK)
                    done = value(pool, i * (2 * J) + (m + 1))
                    pool.wait_ge(s_rt, 32)
                    pool.wait_ge(s_ksw, done)
                    nc.gpsimd.tensor_tensor(ksw[:, t, :], ksw[:, t, :], sinT[:, h], ALU.mult).then_inc(s_ksin, 1)
                    pool.wait_ge(s_rt, 32)
                    pool.wait_ge(s_ksin, done)
                    nc.gpsimd.tensor_tensor(dst, ksw[:, t, :], kc[:, t, :], ALU.add).then_inc(s_rope, 1)
                pool.wait_ge(s_rt, 32)
                with pool.Fori(0, NBLK) as i:
                    for m in range(2 * J):
                        rope_out(i, m)

            @block.scalar
            def _(act):
                def v_out(i, j):
                    act.wait_ge(s_proj, i * NPJ + 2 * J + j + 1)
                    nc.scalar.activation(TT[:, j, ds(i * BLK, BLK)], PS[:, 2 + 2 * J + j, :], ACT.Identity,
                                         scale=neg_g[:, j:j + 1], bias=bbg[:, j:j + 1]).then_inc(s_tt, 1)

                def lr_out(i):
                    act.wait_ge(s_proj, i * NPJ + NPJ)
                    nc.scalar.activation(X[0:NH, 0, ds(i * BLK, BLK)], PS[0:NH, 2, :], ACT.Identity,
                                         bias=pcol("lr_b", rows=NH)).then_inc(s_lr, 1)

                def norm(i, first):
                    act_square(act, i, first)
                    act_sd(act, i, first)
                    act_affine(act, i)

                def body(i, last):
                    if not last:
                        norm(i + 1, False)
                    for j in range(J):
                        v_out(i, j)
                    lr_out(i)

                act.wait_ge(s_sp, 2 * J)
                act_a(act, 0)
                act_a(act, 1)
                norm(0, True)
                with act.Fori(0, NBLK - 2) as i:
                    act_a(act, i + 2)
                    body(i, False)
                body(NBLK - 2, False)
                body(NBLK - 1, True)

        lrt = work[:, 0:NBLK * B * NH].rearrange("p (s b h) -> p s b h", s=8, b=B)
        lrm = work[:, 256:512]
        with nc.Block() as block:
            s_sig, s_tr, s_cp, s_spread, s_mask, s_lrh, s_qperm = (
                sem(n) for n in ("sig", "lr_tr", "lr_cp", "lr_spread", "lr_mask", "lr_h", "qperm"))

            @block.scalar
            def _(act):
                nc.scalar.activation(X[0:NH, 0, :], X[0:NH, 0, :], ACT.Sigmoid).then_inc(s_sig, 1)

            @block.tensor
            def _(pe):
                pe.wait_ge(s_sig, 1)
                for b in range(B):
                    for s in range(8):
                        tr = nc.tensor.transpose(PS[:, 0, (s * B + b) * NH:(s * B + b + 1) * NH],
                                                 X[0:NH, 0, b * N + s * P:b * N + (s + 1) * P],
                                                 ident[0:NH, 0:NH])
                tr.then_inc(s_tr, 1)
                pe.wait_ge(s_cp, 1)
                for n in range(8):
                    if n >= 2:
                        pe.wait_ge(s_mask, n - 1)
                    nc.tensor.matmul(PS[:, 1 + n % 2, 0:256], ccol("spread", n * P, P),
                                     lrt.rearrange("p s b h -> p (s b h)"), start=True, stop=True
                                     ).then_inc(s_spread, 1)

            @block.vector
            def _(dve):
                dve.wait_ge(s_tr, 1)
                nc.vector.tensor_copy(lrt.rearrange("p s b h -> p (s b h)"), PS[:, 0, 0:256]).then_inc(s_cp, 1)
                for n in range(8):
                    dve.wait_ge(s_spread, n + 1)
                    if n:
                        dve.wait_ge(s_lrh, n)
                    nc.vector.tensor_tensor(
                        lrm.rearrange("p (k h) -> p k h", h=NH),
                        PS[:, 1 + n % 2, 0:256].rearrange("p (k h) -> p k h", h=NH),
                        ccol("headmask").unsqueeze(1).broadcast_to([P, 8 * B, NH]), ALU.mult).then_inc(s_mask, 1)
                    dve.wait_ge(s_mask, n + 1)
                    nc.vector.tensor_reduce(
                        lrh.rearrange("p (s n) b -> p s n b", n=8)[:, :, n, :],
                        lrm.rearrange("p (s b h) -> p s b h", b=B, h=NH), AX.X, ALU.add).then_inc(s_lrh, 1)

            @block.sync
            def _(sp):
                sp.wait_ge(s_tr, 1)
                for k in range(J):
                    for a2 in range(2):
                        for e in range(E):
                            a = 2 * k + a2
                            r = 2 * HD * a2 + HD * e
                            sp.dma_start(X[HD * a:HD * a + HD, e, :], QP[r:r + HD, k, :]).then_inc(s_qperm, 16)

        carve = Carve()
        KT2 = [carve(J * B, E, CS) for _ in range(2)]
        QT2 = [carve(J * B, E, CS) for _ in range(2)]
        R = [carve(J, B, HD + CS) for _ in range(2)]
        TK = [carve(2, B, E, CS) for _ in range(2)]
        TKH = [carve(2, B, HD) for _ in range(2)]
        KHX = [carve(E, B, HD) for _ in range(2)]
        AM = [carve(B, E, CS) for _ in range(2)]
        Bs = [carve(B, HD) for _ in range(2)]
        Z, SQ, XH, GR = (carve(B, HD) for _ in range(4))
        GL = [carve(B, HD) for _ in range(2)]
        Y = carve(2, B, HD)
        ZQ, SQQ, ZN, ZT = (carve(B, HD) for _ in range(4))
        ss, sd1, rl, m12 = carve(B), carve(B), carve(B), carve(2, B)
        sz, mx, mcor = carve(B), carve(B), carve(B)
        ssq, sdq = carve(B), carve(B)

        def bc(v, n=HD):
            return v.unsqueeze(2).broadcast_to([P, v.shape[1], n])

        def grow(v):
            return v.unsqueeze(1).broadcast_to([P, B, HD])

        WB, BB, ZB, QB = 0, 2, (3, 4), (5, 6)

        with nc.Block() as block:
            names = ("init wcopy bcopy kt2 qt2 qr stage tkh khx base qbase am z sq ss sd r xh y1 y yp m w v u "
                     "rl gl upd attn sz mx mx2 mc mcor zq sqq ssq sdq rq zn zt ot").split()
            q = {n: sem(f"scan_{n}") for n in names}

            def chunk(t, c):
                return t.rearrange("p j (b n) -> p (j b) n", b=B)[:, :, ds(c * CS, CS)]

            @block.tensor
            def _(pe):
                for k in range(J):
                    nc.tensor.matmul(PS[:, WB + k, 0:B * HD].rearrange("p (b d) -> p b d", b=B), ident,
                                     grow(w0[:, k * HD:(k + 1) * HD]), start=True, stop=True,
                                     skip_group_check=True)
                nc.tensor.matmul(PS[:, BB, 0:B * HD].rearrange("p (b d) -> p b d", b=B), ident,
                                 grow(b0), start=True, stop=True, skip_group_check=True).then_inc(q["init"], 1)

                def body(c, p, early):
                    last_but_one, now = value(pe, c - 1), value(pe, c + 1)
                    pe.wait_ge(q["init"], 1)
                    pe.wait_ge(q["kt2"], now)
                    pe.wait_ge(q["qr"], c + 1)
                    pe.wait_ge(q["wcopy"], c + 1)
                    if not early:
                        pe.wait_ge(q["am"], last_but_one)
                    for b in range(B):
                        for k in range(J):
                            for a2 in range(2):
                                r, a = 2 * HD * a2, 2 * k + a2
                                mm = nc.tensor.matmul(
                                    PS[HD * a:HD * a + HD, ZB[p], b * 48:b * 48 + 48],
                                    KT2[p][r:r + 64, k * B + b, :, :].rearrange("p e t -> p (e t)"),
                                    R[p][r:r + 64, k, b, :], start=True, stop=True, skip_group_check=True)
                    mm.then_inc(q["base"], 1)
                    pe.wait_ge(q["init"], 1)
                    pe.wait_ge(q["qt2"], now)
                    if not early:
                        pe.wait_ge(q["zq"], last_but_one)
                    for b in range(B):
                        for k in range(J):
                            for a2 in range(2):
                                r, a = 2 * HD * a2, 2 * k + a2
                                mm = nc.tensor.matmul(
                                    PS[HD * a:HD * a + HD, QB[p], b * HD:b * HD + HD],
                                    QT2[p][r:r + 64, k * B + b, :, :].rearrange("p e t -> p (e t)"),
                                    R[p][r:r + 64, k, b, 0:HD], start=(b == 0), stop=False,
                                    skip_group_check=True)
                    mm.then_inc(q["qbase"], 1)
                    pe.wait_ge(q["init"], 1)
                    pe.wait_ge(q["khx"], now)
                    pe.wait_ge(q["gl"], now)
                    for k in range(J):
                        for a2 in range(2):
                            a = 2 * k + a2
                            for e in range(E):
                                o = 2 * HD * a2 + HD * e
                                for b in range(B):
                                    nc.tensor.matmul(PS[o:o + HD, WB + k, b * HD:b * HD + HD],
                                                     KHX[p][HD * a:HD * a + HD, e, b, :],
                                                     GL[p][HD * a:HD * a + HD, b, :],
                                                     start=False, stop=True, skip_group_check=True)
                    nc.tensor.matmul(PS[:, BB, 0:B * HD], ones_blk[:, :], GL[p].rearrange("p b d -> p (b d)"),
                                     start=False, stop=True, skip_group_check=True).then_inc(q["upd"], 1)
                    pe.wait_ge(q["init"], 1)
                    pe.wait_ge(q["am"], now)
                    for a in range(4):
                        for b in range(B):
                            mm = nc.tensor.matmul(PS[HD * a:HD * a + HD, QB[p], b * HD:b * HD + HD],
                                                  AM[p][HD * a:HD * a + HD, b, :, :].rearrange("p e t -> p (e t)"),
                                                  GL[p][HD * a:HD * a + HD, b, :],
                                                  start=False, stop=True, skip_group_check=True)
                    mm.then_inc(q["attn"], 1)

                body(0, 0, True)
                body(1, 1, True)
                with pe.Fori(1, NC // 2) as pair:
                    c = pair * 2
                    body(c, 0, False)
                    body(c + 1, 1, False)

            @block.vector
            def _(dve):
                def rows_of(c, p):
                    dve.wait_ge(q["stage"], c + 1)
                    nc.vector.transpose(TKH[p].rearrange("p s b d -> p (s b d)"),
                                        TK[p].rearrange("p s b e t -> p (s b e t)")).then_inc(q["tkh"], 1)

                def out_rows(c, p):
                    dve.wait_ge(q["attn"], c + 1)
                    nc.vector.tensor_tensor(ZQ, PS[:, QB[p], 0:B * HD].rearrange("p (b d) -> p b d", b=B),
                                            Bs[p], ALU.add).then_inc(q["zq"], 1)

                def out_norm(c, first):
                    dve.wait_ge(q["sqq"], c + 1)
                    nc.vector.tensor_reduce(ssq, SQQ, AX.X, ALU.add).then_inc(q["ssq"], 1)
                    dve.wait_ge(q["sdq"], c + 1)
                    nc.vector.reciprocal(sdq, sdq).then_inc(q["rq"], 1)
                    dve.wait_ge(q["rq"], c + 1)
                    nc.vector.tensor_tensor(ZN, ZQ, bc(sdq), ALU.mult).then_inc(q["zn"], 1)
                    dve.wait_ge(q["zn"], c + 1)
                    if not first:
                        dve.wait_ge(q["ot"], c + 0)
                    nc.vector.transpose(ZT.rearrange("p b d -> p (b d)"), ZN.rearrange("p b d -> p (b d)")
                                        ).then_inc(q["zt"], 1)

                def body(c, p, first, last):
                    T = TKH[p][:, 0, :, :]
                    zb = PS[:, ZB[p], 0:B * 48].rearrange("p (b n) -> p b n", b=B)
                    dve.wait_ge(q["base"], c + 1)
                    dve.wait_ge(q["bcopy"], c + 1)
                    nc.vector.tensor_tensor(Z, zb[:, :, 0:HD], Bs[p], ALU.add).then_inc(q["z"], 1)
                    if not first:
                        dve.wait_ge(q["attn"], c + 0)
                    for e in range(E):
                        a = nc.vector.scalar_tensor_tensor(
                            AM[p][:, :, e, :], zb[:, :, HD:HD + CS], 1.0,
                            amask[:, e * CS:(e + 1) * CS].unsqueeze(1).broadcast_to([P, B, CS]),
                            ALU.add, ALU.mult)
                    a.then_inc(q["am"], 1)
                    dve.wait_ge(q["z"], c + 1)
                    if not first:
                        dve.wait_ge(q["mx"], c + 0)
                    nc.vector.tensor_reduce(sz, Z, AX.X, ALU.add).then_inc(q["sz"], 1)
                    dve.wait_ge(q["sq"], c + 1)
                    nc.vector.tensor_reduce(ss, SQ, AX.X, ALU.add).then_inc(q["ss"], 1)
                    if not first:
                        out_rows(c - 1, 1 - p)
                    dve.wait_ge(q["sd"], c + 1)
                    nc.vector.reciprocal(sd1, sd1).then_inc(q["r"], 1)
                    dve.wait_ge(q["r"], c + 1)
                    nc.vector.tensor_tensor(XH, Z, bc(sd1), ALU.mult).then_inc(q["xh"], 1)
                    dve.wait_ge(q["xh"], c + 1)
                    nc.vector.tensor_tensor(GR, XH, grow(g2row), ALU.mult).then_inc(q["y1"], 1)
                    dve.wait_ge(q["y1"], c + 1)
                    nc.vector.tensor_tensor(Y[:, 0, :, :], GR, T, ALU.add).then_inc(q["y"], 1)
                    dve.wait_ge(q["y"], c + 1)
                    nc.vector.tensor_tensor(Y[:, 1, :, :], Y[:, 0, :, :], XH, ALU.mult).then_inc(q["yp"], 1)
                    dve.wait_ge(q["yp"], c + 1)
                    nc.vector.tensor_reduce(m12, Y, AX.X, ALU.add).then_inc(q["m"], 1)
                    dve.wait_ge(q["m"], c + 1)
                    nc.vector.scalar_tensor_tensor(GR, XH, -1.0 / HD, bc(m12[:, 1, :]), ALU.mult, ALU.mult
                                                   ).then_inc(q["w"], 1)
                    dve.wait_ge(q["w"], c + 1)
                    nc.vector.tensor_tensor(GR, GR, Y[:, 0, :, :], ALU.add).then_inc(q["v"], 1)
                    dve.wait_ge(q["v"], c + 1)
                    dve.wait_ge(q["mcor"], c + 1)
                    nc.vector.scalar_tensor_tensor(GR, bc(m12[:, 0, :]), -1.0 / HD, GR, ALU.mult, ALU.add
                                                   ).then_inc(q["u"], 1)
                    dve.wait_ge(q["u"], c + 1)
                    nc.vector.tensor_tensor(GL[p], GR, bc(rl), ALU.mult).then_inc(q["gl"], 1)
                    if not last:
                        rows_of(c + 1, 1 - p)
                    if not first:
                        out_norm(c - 1, early_out(c))

                early_out = lambda c: isinstance(c, int) and c == 1
                rows_of(0, 0)
                body(0, 0, True, False)
                body(1, 1, False, False)
                with dve.Fori(1, NC // 2 - 1) as pair:
                    c = pair * 2
                    body(c, 0, False, False)
                    body(c + 1, 1, False, False)
                body(NC - 2, 0, False, False)
                body(NC - 1, 1, False, True)
                out_rows(NC - 1, 1)
                out_norm(NC - 1, False)

            @block.gpsimd
            def _(pool):
                def prepare(c, p, early):
                    if not early:
                        pool.wait_ge(q["qbase"], c - 1)
                    nc.gpsimd.tensor_tensor(
                        KT2[p], chunk(KP, c).unsqueeze(2).broadcast_to([P, J * B, E, CS]),
                        ccol("emask_k").unsqueeze(1).unsqueeze(3).broadcast_to([P, J * B, E, CS]),
                        ALU.mult).then_inc(q["kt2"], 1)
                    nc.gpsimd.tensor_copy(R[p].rearrange("p k b n -> p (k b) n")[:, :, HD:HD + CS],
                                          chunk(QP, c)).then_inc(q["qr"], 1)
                    if not early:
                        pool.wait_ge(q["tkh"], c - 1)
                    nc.gpsimd.tensor_copy(TK[p][:, 0, :, :, :].rearrange("p b e t -> p e b t"),
                                          TT.rearrange("p e (b n) -> p e b n", b=B)[:, :, :, ds(c * CS, CS)])
                    nc.gpsimd.tensor_copy(TK[p][:, 1, :, :, :].rearrange("p b e t -> p e b t"),
                                          KN.rearrange("p e (b n) -> p e b n", b=B)[:, :, :, ds(c * CS, CS)]
                                          ).then_inc(q["stage"], 1)

                def khx(c, p, early):
                    pool.wait_ge(q["tkh"], c + 1)
                    if not early:
                        pool.wait_ge(q["upd"], c - 1)
                    nc.gpsimd.tensor_tensor(
                        KHX[p], TKH[p][:, 1, :, :].unsqueeze(1).broadcast_to([P, E, B, HD]),
                        upd_mask.unsqueeze(2).unsqueeze(3).broadcast_to([P, E, B, HD]), ALU.mult
                    ).then_inc(q["khx"], 1)

                def body(c, p, first, last, early):
                    khx(c, p, early)
                    pool.wait_ge(q["r"], c + 1)
                    if not first:
                        pool.wait_ge(q["gl"], c + 0)
                    nc.gpsimd.tensor_tensor(rl, sd1, lrh[:, ds(c, 1), :].squeeze(1), ALU.mult
                                            ).then_inc(q["rl"], 1)
                    pool.wait_ge(q["sz"], c + 1)
                    nc.gpsimd.tensor_tensor(mx, sz, sd1, ALU.mult).then_inc(q["mx"], 1)
                    pool.wait_ge(q["mx"], c + 1)
                    nc.gpsimd.tensor_tensor(mx, mx, neg_mean, ALU.mult).then_inc(q["mx2"], 1)
                    pool.wait_ge(q["mx2"], c + 1)
                    pool.wait_ge(q["m"], c + 1)
                    nc.gpsimd.tensor_tensor(mcor, mx, m12[:, 1, :], ALU.mult).then_inc(q["mc"], 1)
                    pool.wait_ge(q["mc"], c + 1)
                    nc.gpsimd.tensor_tensor(m12[:, 0, :], mcor, m12[:, 0, :], ALU.add).then_inc(q["mcor"], 1)
                    if not first:
                        pool.wait_ge(q["zq"], c + 0)
                        nc.gpsimd.tensor_tensor(SQQ, ZQ, ZQ, ALU.mult).then_inc(q["sqq"], 1)
                    if not last:
                        prepare(c + 2, p, False)

                prepare(0, 0, True)
                prepare(1, 1, True)
                body(0, 0, True, False, True)
                body(1, 1, False, False, True)
                with pool.Fori(1, NC // 2 - 1) as pair:
                    c = pair * 2
                    body(c, 0, False, False, False)
                    body(c + 1, 1, False, False, False)
                body(NC - 2, 0, False, True, False)
                body(NC - 1, 1, False, True, False)
                pool.wait_ge(q["zq"], NC)
                nc.gpsimd.tensor_tensor(SQQ, ZQ, ZQ, ALU.mult).then_inc(q["sqq"], 1)

            @block.scalar
            def _(act):
                wb = PS[:, WB:WB + J, 0:B * HD].rearrange("p k (b d) -> p k b d", b=B)

                def state(c, p):
                    for k in range(J):
                        w = nc.scalar.activation(R[p][:, k, :, 0:HD], wb[:, k, :, :], ACT.Copy)
                    w.then_inc(q["wcopy"], 1)
                    nc.scalar.activation(Bs[p], PS[:, BB, 0:B * HD].rearrange("p (b d) -> p b d", b=B),
                                         ACT.Copy).then_inc(q["bcopy"], 1)

                def qt2(c, p, early):
                    if not early:
                        act.wait_ge(q["qbase"], c - 1)
                    for e in range(E):
                        a = nc.scalar.activation(QT2[p][:, :, e, :], chunk(QP, c), ACT.Copy,
                                                 scale=ccol("emask_k", e, 1))
                    a.then_inc(q["qt2"], 1)

                def out_sd(c):
                    act.wait_ge(q["ssq"], c + 1)
                    nc.scalar.activation(sdq, ssq, ACT.Sqrt, bias=eps6, scale=1.0 / HD).then_inc(q["sdq"], 1)

                def out_store(c):
                    act.wait_ge(q["zt"], c + 1)
                    nc.scalar.activation(
                        TT.rearrange("p e (b n) -> p e b n", b=B)[:, :, :, ds(c * CS, CS)],
                        ZT.rearrange("p b (e t) -> p e b t", e=E), ACT.Copy).then_inc(q["ot"], 1)

                def body(c, p, first, last):
                    act.wait_ge(q["z"], c + 1)
                    nc.scalar.activation(SQ, Z, ACT.Square).then_inc(q["sq"], 1)
                    act.wait_ge(q["ss"], c + 1)
                    nc.scalar.activation(sd1, ss, ACT.Sqrt, bias=eps6, scale=1.0 / HD).then_inc(q["sd"], 1)
                    if not last:
                        qt2(c + 1, 1 - p, early_q(c))
                    if not last:
                        act.wait_ge(q["upd"], c + 1)
                        if not first:
                            act.wait_ge(q["zq"], c + 0)
                        state(c + 1, 1 - p)
                    if not first:
                        out_sd(c - 1)
                        out_store(c - 1)

                early_q = lambda c: isinstance(c, int) and c == 0
                act.wait_ge(q["init"], 1)
                state(0, 0)
                qt2(0, 0, True)
                body(0, 0, True, False)
                body(1, 1, False, False)
                with act.Fori(1, NC // 2 - 1) as pair:
                    c = pair * 2
                    body(c, 0, False, False)
                    body(c + 1, 1, False, False)
                body(NC - 2, 0, False, False)
                body(NC - 1, 1, False, True)
                out_sd(NC - 1)
                out_store(NC - 1)

            @block.sync
            def _(sp):
                sp.wait_ge(s_qperm, 16 * 2 * J * E)

        carve = Carve()
        sq, sd = carve(J, BLK), carve(BLK)
        with nc.Block() as block:
            s_pre, s_wo, s_o, s_x1 = (sem(n) for n in ("pre", "wo", "o", "x1"))
            s_xr = [sem(f"xr{b}") for b in range(B)]

            def add_bias(act, i, j):
                act.wait_ge(s_pre, i * J + j + 1)
                return nc.scalar.activation(blk_of(TT[:, j, :], i), blk_of(TT[:, j, :], i), ACT.Identity,
                                            bias=pcol("bb", j))

            q2, ot, act_a, pe_mean, dve_center, act_square, pe_var, act_sd, dve_scale, act_affine = \
                layer_norm("ln2", TT, sq, sd, eps6, "post_w", "post_b", add_bias)

            @block.sync
            def _(sp):
                sp.dma_start(wsm[:, :, :], wo).then_inc(s_wo, 16)
                for b in range(B):
                    sp.dma_start(KN[:, :, b * N:(b + 1) * N], xv[:, :, b, :]).then_inc(s_xr[b], 16)

            @block.tensor
            def _(pe):
                pe.wait_ge(s_wo, 16)

                def body(i, first, last):
                    pe.wait_ge(q2["xn"], i * J + J)
                    if not last:
                        pe_mean(pe, i + 1, False)
                    for m in range(J):
                        if m == J - 1 and not last:
                            pe_var(pe, i + 1, False)
                        if not first:
                            pe.wait_ge(s_x1, (i - 1) * J + m + 1)
                        for j in range(J):
                            mm = nc.tensor.matmul(PS[:, 2 + m, :], wsm[:, j, m * P:(m + 1) * P], ot(i, j),
                                                  start=(j == 0), stop=(j == J - 1))
                        mm.then_inc(s_o, 1)

                pe_mean(pe, 0, True)
                pe_var(pe, 0, True)
                body(0, True, False)
                with pe.Fori(1, NBLK - 1) as i:
                    body(i, False, False)
                body(NBLK - 1, False, True)

            @block.vector
            def _(dve):
                def pre(i):
                    for j in range(J):
                        nc.vector.scalar_tensor_tensor(blk_of(TT[:, j, :], i), blk_of(TT[:, j, :], i),
                                                       pcol("g", j), blk_of(X[:, j, :], i),
                                                       ALU.mult, ALU.add).then_inc(s_pre, 1)

                def residual(i):
                    for m in range(J):
                        dve.wait_ge(s_o, i * J + m + 1)
                        nc.vector.tensor_tensor(blk_of(KN[:, m, :], i), PS[:, 2 + m, :],
                                                blk_of(KN[:, m, :], i), ALU.add).then_inc(s_x1, 1)

                for b in range(B):
                    dve.wait_ge(s_xr[b], 16)
                pre(0)
                pre(1)
                dve_center(dve, 0)
                dve_scale(dve, 0)
                with dve.Fori(0, NBLK - 2) as i:
                    pre(i + 2)
                    dve_center(dve, i + 1)
                    dve_scale(dve, i + 1)
                    residual(i)
                dve_center(dve, NBLK - 1)
                dve_scale(dve, NBLK - 1)
                residual(NBLK - 2)
                residual(NBLK - 1)

            @block.scalar
            def _(act):
                def norm(i, first):
                    act_square(act, i, first)
                    act_sd(act, i, first)
                    act_affine(act, i)

                act_a(act, 0)
                act_a(act, 1)
                norm(0, True)
                with act.Fori(0, NBLK - 2) as i:
                    act_a(act, i + 2)
                    norm(i + 1, False)
                norm(NBLK - 1, False)

        with nc.Block() as block:
            group_norm(block, KN, "gn2")

        flat = lambda t: t[:, :, :].rearrange("p j n -> p (j n)")
        NXP = J * XW * W_
        XP = [flat(KP)[:, s * NXP:(s + 1) * NXP].rearrange("p (j r x) -> p j r x", j=J, x=W_)
              for s in range(2)]
        NG = NRB * RW * XW
        G = flat(QP)[:, 0:NG]
        STAGES = [(NRB, RW * XW, 2 * XW, (RW - 2) * XW), (NRB, (RW - 2) * XW, XW, KS * XW),
                  (NRB * KS, XW, 16, 20), (NRB * KS, 20, 8, 12), (NRB * KS, 12, 4, 8),
                  (NRB * KS, 8, 2, 6), (NRB * KS, 6, 1, KS)]
        carve = Carve()
        DST, SRC = [], [G.rearrange("p (r w) -> p r w", w=RW * XW)]
        at = [flat(QP), NG]
        for k, (r, w, _, kept) in enumerate(STAGES):
            n = r * kept
            if at[1] + n > J * NT:
                at = [flat(TT), 0]
            DST.append(at[0][:, at[1]:at[1] + n].rearrange("p (r w) -> p r w", w=kept))
            if k + 1 < len(STAGES):
                SRC.append(at[0][:, at[1]:at[1] + n].rearrange("p (r w) -> p r w", w=STAGES[k + 1][1]))
            at[1] += n
        TMP = [flat(X)[:, k * 2048:k * 2048 + r * kept].rearrange("p (r w) -> p r w", w=kept)
               for k, (r, w, _, kept) in zip((0, 1, 2, 0, 1, 2, 0), STAGES)]
        YB = [flat(TT)[:, 4096 + s * 2048:4096 + (s + 1) * 2048].rearrange("p (k n) -> p k n", k=PER * J)
              for s in range(2)]
        DN = carve(NRB, S)
        DSQ = carve(NRB, S)
        nrm = carve(NRB)
        DT = carve(N)
        wsw = carve(C)
        ov = out.rearrange("b (j p) n -> p j b n", p=P)

        with nc.Block() as block:
            (s_w2, s_pad, s_xg, s_gram, s_gs, s_tmp, s_st, s_dsq, s_dss, s_dsd, s_dr, s_dn, s_dt, s_dtc,
             s_conv, s_relu, s_y) = (
                sem(n) for n in ("w2", "pad", "xg", "gram", "gs", "btmp", "bstage", "dsq", "dss", "dsd", "dr",
                                 "dn", "dt", "dtc", "conv", "relu", "yfin"))
            s_out = [sem(f"out{s}") for s in range(2)]
            NS = len(STAGES)
            CV = PER * J

            @block.sync
            def _(sp):
                sp.dma_start(wsm[:, :, :], wx).then_inc(s_w2, 16)
                sp.dma_start(wsw[0:S, :], ws).then_inc(s_w2, 16)

                def store(b, p, h):
                    sp.wait_ge(s_y, b * CV + (h + 1) * J)
                    for o in range(J):
                        sp.dma_start(ov[:, o, ds(b, 1), h * BLK:(h + 1) * BLK].rearrange("p b n -> p (b n)"),
                                     YB[p][:, h * J + o, :]).then_inc(s_out[p], 16)
                with sp.Fori(0, B // 2) as pair:
                    b = pair * 2
                    for p in range(2):
                        for h in range(PER):
                            store(b + p, p, h)
                for p in range(2):
                    sp.wait_ge(s_out[p], 16 * CV * B // 2)

            @block.gpsimd
            def _(pool):
                for p in range(2):
                    nc.gpsimd.memset(XP[p][:, :, 0:PAD, :], 0.0)
                    nc.gpsimd.memset(XP[p][:, :, XW - PAD:XW, :], 0.0)
                g3 = G.rearrange("p (r x) -> p r x", x=XW)
                nc.gpsimd.memset(g3[:, :, 0:PAD], 0.0)
                nc.gpsimd.memset(g3[:, :, XW - PAD:XW], 0.0).then_inc(s_pad, 1)

                def fin(b, p, k):
                    h, o = divmod(k, J)
                    pool.wait_ge(s_relu, b * CV + k + 1)
                    nc.gpsimd.tensor_tensor(YB[p][:, k, :], YB[p][:, k, :],
                                            KN[:, o, ds(b * N + h * BLK, BLK)], ALU.add).then_inc(s_y, 1)
                with pool.Fori(0, B // 2) as pair:
                    b = pair * 2
                    for p in range(2):
                        for k in range(CV):
                            fin(b + p, p, k)

            @block.tensor
            def _(pe):
                pe.wait_ge(s_w2, 32)
                pe.wait_ge(s_pad, 1)

                def gram(b, p, first):
                    pe.wait_ge(s_xg, b * J + J)
                    for rb in range(NRB):
                        if not (first and rb < 4):
                            pe.wait_ge(s_gs, b * NRB + rb - 3)
                        for j in range(J):
                            mm = nc.tensor.matmul(
                                PS[:, rb % 4, 0:RW * W_],
                                XP[p][:, j, PAD + RB * rb:PAD + RB * rb + RB, :].rearrange("p r x -> p (r x)"),
                                XP[p][:, j, RB * rb:RB * rb + RW, :].rearrange("p r x -> p (r x)"),
                                start=(j == 0), stop=(j == J - 1))
                        mm.then_inc(s_gram, 1)

                def conv(b, p, first):
                    pe.wait_ge(s_dn, b + 1)
                    if not first:
                        pe.wait_ge(s_dtc, b * 2)
                    for rb in range(NRB):
                        tr = nc.tensor.transpose(PS[0:S, 4 + rb // 4, (rb % 4) * P:(rb % 4 + 1) * P],
                                                 DN[:, rb, :], ident)
                    tr.then_inc(s_dt, 1)
                    pe.wait_ge(s_dtc, b * 2 + 2)
                    for k in range(CV):
                        h, o = divmod(k, J)
                        if not (first and k < 2):
                            pe.wait_ge(s_relu, b * CV + k - 1)
                        bank = 6 + k % 2
                        for j in range(J):
                            nc.tensor.matmul(PS[:, bank, :], wsm[:, j, o * P:(o + 1) * P],
                                             XP[p][:, j, PAD + 16 * h:PAD + 16 * h + 16, :].rearrange(
                                                 "p r x -> p (r x)"), start=(j == 0), stop=False)
                        nc.tensor.matmul(PS[:, bank, :], wsw[0:S, o * P:(o + 1) * P],
                                         DT[0:S, h * BLK:(h + 1) * BLK], start=False, stop=True
                                         ).then_inc(s_conv, 1)

                gram(0, 0, True)
                gram(1, 1, False)
                conv(0, 0, True)
                for b in range(2, B):
                    gram(b, b % 2, False)
                    conv(b - 1, (b - 1) % 2, False)
                conv(B - 1, 1, False)

            @block.vector
            def _(dve):
                def body(b, first):
                    for k, (r, w, sh, kept) in enumerate(STAGES):
                        dve.wait_ge(s_tmp, b * NS + k + 1)
                        nc.vector.scalar_tensor_tensor(DST[k], SRC[k][:, :, 0:kept], ccol("shift_off", k, 1),
                                                       TMP[k], ALU.mult, ALU.add).then_inc(s_st, 1)
                    dve.wait_ge(s_st, b * NS + NS)
                    D = DST[-1].rearrange("p (a r) w -> p a (r w)", r=KS)
                    nc.vector.tensor_tensor(DSQ, D, D, ALU.mult).then_inc(s_dsq, 1)
                    dve.wait_ge(s_dsq, b + 1)
                    nc.vector.tensor_reduce(nrm, DSQ, AX.X, ALU.add).then_inc(s_dss, 1)
                    dve.wait_ge(s_dsd, b + 1)
                    nc.vector.reciprocal(nrm, nrm).then_inc(s_dr, 1)
                    dve.wait_ge(s_dr, b + 1)
                    if not first:
                        dve.wait_ge(s_dt, b + 0)
                    nc.vector.tensor_tensor(DN, D, nrm.unsqueeze(2).broadcast_to([P, NRB, S]), ALU.mult
                                            ).then_inc(s_dn, 1)

                body(0, True)
                with dve.Fori(1, B) as b:
                    body(b, False)

            @block.scalar
            def _(act):
                def scale(b, p, first):
                    if not first:
                        act.wait_ge(s_conv, (b - 1) * CV)
                    for j in range(J):
                        nc.scalar.activation(
                            XP[p][:, j, PAD:PAD + H, :].rearrange("p r x -> p (r x)"), KN[:, j, ds(b * N, N)],
                            ACT.Identity, scale=gn_a[:, ds(b * J + j, 1)], bias=gn_c[:, ds(b * J + j, 1)]
                        ).then_inc(s_xg, 1)

                def evacuate(b, first):
                    if not first:
                        act.wait_ge(s_st, (b - 1) * NS + 1)
                    for rb in range(NRB):
                        act.wait_ge(s_gram, b * NRB + rb + 1)
                        nc.scalar.activation(
                            G.rearrange("p (a r x) -> p a r x", a=NRB, x=XW)[:, rb, :, PAD:PAD + W_],
                            PS[:, rb % 4, 0:RW * W_].rearrange("p (r x) -> p r x", x=W_), ACT.Copy
                        ).then_inc(s_gs, 1)

                def stages(b):
                    for k, (r, w, sh, kept) in enumerate(STAGES):
                        if k == 0:
                            act.wait_ge(s_gs, b * NRB + NRB)
                        else:
                            act.wait_ge(s_st, b * NS + k)
                        nc.scalar.activation(TMP[k], SRC[k][:, :, sh:sh + kept], ACT.Copy,
                                             scale=ccol("shift_on", k, 1)).then_inc(s_tmp, 1)
                    act.wait_ge(s_dss, b + 1)
                    nc.scalar.activation(nrm, nrm, ACT.Sqrt, bias=eps6).then_inc(s_dsd, 1)

                def dt_copy(b, first):
                    act.wait_ge(s_dt, b + 1)
                    if not first:
                        act.wait_ge(s_conv, b * CV)
                    for h in range(2):
                        nc.scalar.activation(DT[0:S, h * BLK:(h + 1) * BLK], PS[0:S, 4 + h, :], ACT.Copy
                                             ).then_inc(s_dtc, 1)

                def relu(b, p, first):
                    if not first:
                        act.wait_ge(s_out[p], (b - p) * (CV * 8))
                    for k in range(CV):
                        h, o = divmod(k, J)
                        act.wait_ge(s_conv, b * CV + k + 1)
                        nc.scalar.activation(YB[p][:, k, :], PS[:, 6 + k % 2, :], ACT.Relu,
                                             bias=pcol("conv_b", o)).then_inc(s_relu, 1)

                scale(0, 0, True)
                evacuate(0, True)
                scale(1, 1, True)
                stages(0)
                evacuate(1, False)
                dt_copy(0, True)
                relu(0, 0, True)
                for b in range(2, B):
                    scale(b, b % 2, False)
                    stages(b - 1)
                    evacuate(b, False)
                    dt_copy(b - 1, False)
                    relu(b - 1, (b - 1) % 2, b == 2)
                stages(B - 1)
                dt_copy(B - 1, False)
                relu(B - 1, 1, False)


def constants():
    p = np.arange(P)
    row_e, row_t, row_head = (p // CS) % E, p % CS, 4 * ((p // CS) % E) + p // HD
    c = {}
    c["ident"] = np.eye(P)
    c["mean_c"] = np.full((P, P), 1.0 / C)
    c["mean_g"] = (p[:, None] // GROUP == p[None, :] // GROUP) / GROUP
    c["chunk_ones"] = p[:, None] // CS == p[None, :] // CS
    c["emask"] = row_e[:, None] == np.arange(E)
    c["emask_k"] = ((p // HD) % E)[:, None] == np.arange(E)
    col_e, col_t = np.divmod(np.arange(E * CS), CS)
    c["causal"] = (row_e[:, None] == col_e) & (row_t[:, None] <= col_t)
    c["headmask"] = (row_head[:, None] == np.arange(NH)) / HD
    c["inv_t"] = np.broadcast_to((1.0 / np.arange(1, CS + 1, dtype=np.float32)), (P, CS))
    r, xx = np.divmod(p, W_)
    bits = np.stack([(r >> 1) & 1, r & 1] + [(xx >> k) & 1 for k in (4, 3, 2, 1, 0)], 1)
    c["shift_on"], c["shift_off"] = bits, 1 - bits
    c["spread"] = np.concatenate([p[:, None] == n * CS + row_t[None, :] for n in range(8)], 1)
    table = np.concatenate([np.asarray(c[k], np.float32).reshape(P, w) for k, w in CONST.items()], 1)
    inv = (1.0 / 10000.0 ** (np.arange(0, HD, 2, dtype=np.float32) / np.float32(HD))).astype(np.float32)
    angle = np.arange(N, dtype=np.float32)[None, :] * inv[:, None]
    cos, sin = np.cos(angle), np.sin(angle)
    rope = np.stack([np.tile(np.concatenate([cos, cos]), (P // HD, 1)),
                     np.tile(np.concatenate([-sin, sin]), (P // HD, 1))], 1)
    return np.ascontiguousarray(table), np.ascontiguousarray(rope.astype(np.float32))


def kernel(x, L0_conv_ln_w, L0_conv_ln_b, L0_conv_q_w, L0_conv_k_w, L0_conv_v_w, L0_conv_o_w, L0_conv_W1,
           L0_conv_b1, L0_conv_ttt_ln_w, L0_conv_ttt_ln_b, L0_conv_lr_w, L0_conv_lr_b,
           L0_conv_tok_idx_delta, L0_conv_post_w, L0_conv_post_b, L1_conv_W, L1_conv_bias):
    import concourse.bacc as bacc
    from concourse.bass_utils import run_bass_kernel_spmd

    a = np.asarray
    paired = [4 * e + 2 * k + a2 for k in range(J) for a2 in range(2) for e in range(E)]
    rows = [4 * e + g for g in range(4) for e in range(E)]

    def stationary(w):
        return np.ascontiguousarray(a(w).T.reshape(J, P, -1).transpose(1, 0, 2))

    def by_head(w):
        return a(w).reshape(NH, HD, C)[paired].reshape(C, C)

    def channels(v):
        return a(v).reshape(J, P).T

    pars = dict(
        ln_w=channels(L0_conv_ln_w), ln_b=channels(L0_conv_ln_b), post_w=channels(L0_conv_post_w),
        post_b=channels(L0_conv_post_b), conv_b=channels(L1_conv_bias),
        g=channels(a(L0_conv_ttt_ln_w).reshape(C)), bb=channels(a(L0_conv_ttt_ln_b).reshape(C)),
        g_row=np.repeat(a(L0_conv_ttt_ln_w)[rows], CS, 0),
        b1_row=np.repeat(a(L0_conv_b1).reshape(NH, HD)[rows], CS, 0),
        delta=np.tile(a(L0_conv_tok_idx_delta)[None], (P, 1)),
        lr_b=np.tile(a(L0_conv_lr_b).reshape(NH, 1), (P // NH, 1)),
        w1=a(L0_conv_W1)[paired].reshape(J, P, HD).transpose(1, 0, 2).reshape(P, J * HD),
    )
    table, rope = constants()
    arrays = dict(
        x=np.ascontiguousarray(a(x).reshape(B, C, N)),
        wq=stationary(by_head(L0_conv_q_w)), wk=stationary(by_head(L0_conv_k_w)),
        wv=stationary(L0_conv_v_w), wo=stationary(L0_conv_o_w),
        wlr=stationary(a(L0_conv_lr_w).reshape(NH, C)),
        wx=stationary(a(L1_conv_W)[:, :C]), ws=np.ascontiguousarray(a(L1_conv_W)[:, C:].T),
        params=np.ascontiguousarray(np.concatenate([pars[k] for k in PARAM], 1)),
        consts=table, rope=rope)

    nc = bacc.Bacc("TRN2", target_bir_lowering=False, num_devices=1)
    order = ["x", "wq", "wk", "wv", "wo", "wlr", "wx", "ws", "params", "consts", "rope"]
    aps = {k: nc.dram_tensor(f"in_{k}", arrays[k].shape, F32, kind="ExternalInput").ap() for k in order}
    o = nc.dram_tensor("out_0", (B, C, N), F32, kind="ExternalOutput").ap()
    build(nc, aps["x"], o, aps["wq"], aps["wk"], aps["wv"], aps["wo"], aps["wlr"], aps["wx"], aps["ws"],
          aps["params"], aps["consts"], aps["rope"])
    r = run_bass_kernel_spmd(nc, [{f"in_{k}": arrays[k] for k in order}], core_ids=[0])
    return r.results[0]["out_0"].reshape(B, C, H, W_)
```

```python
from contextlib import ExitStack

import numpy as np

import concourse.bass as bass
from concourse import mybir

F32 = mybir.dt.float32
ALU = mybir.AluOpType
ACT = mybir.ActivationFunctionType
AX = mybir.AxisListType
ds = bass.ds

P = 128
B, C, H, W_ = 4, 256, 32, 32
N = H * W_
NT = B * N
J = C // P
NH, HD, CS = 8, 32, 16
NC = N // CS
E = 2
BLK = 512
NBLK = NT // BLK
PER = N // BLK
GROUP = 8
KS = 5
S = KS * KS
PAD = KS // 2
RB = 4
NRB = H // RB
RW = RB + 2 * PAD
XW = W_ + 2 * PAD

EPS_GN, EPS_LN, EPS_IN, EPS_NORM = 1e-5, 1e-5, 1e-6, 1e-6

CONST = dict(ident=P, center_h=P, mean_c=P, mean_g=P, chunk_ones=P, emask=E, emask_k=E, causal=E * CS, headmask=NH, inv_t=CS,
             shift_on=7, shift_off=7, spread=8 * P)
PARAM = dict(ln_w=J, ln_b=J, post_w=J, post_b=J, conv_b=J, g=E, bb=E, g_row=HD, b1_row=HD,
             delta=CS, lr_b=1, w1=J * HD)


def columns(widths):
    at, out = 0, {}
    for name, w in widths.items():
        out[name] = (at, w)
        at += w
    return out, at


CONST_AT, NCONST = columns(CONST)
PARAM_AT, NPARAM = columns(PARAM)


def build(nc, x, out, wq, wk, wv, wo, wlr, wx, ws, params, consts, rope):
    ctx = ExitStack()
    with ctx:
        def sb(name, shape):
            return ctx.enter_context(nc.sbuf_tensor(name, shape, F32))

        def sem(name):
            return ctx.enter_context(nc.semaphore(name))

        X = sb("X", [P, J, NT])
        KP = sb("KP", [P, J, NT])
        QP = sb("QP", [P, J, NT])
        KN = sb("KN", [P, J, NT])
        TT = sb("TT", [P, J, NT])
        par = sb("par", [P, NPARAM])
        small = sb("small", [P, 512])
        lrh = sb("lrh", [P, NC, B])
        wsm = sb("wsm", [P, J, C])
        work = sb("work", [P, 7424])

        def pcol(name, i=0, n=1, rows=P):
            at = PARAM_AT[name][0] + i
            return par[0:rows, at:at + n]

        used = [0]

        def scol(n):
            used[0] += n
            assert used[0] <= 512
            return small[:, used[0] - n:used[0]]

        gn_a, gn_c = scol(B * J), scol(B * J)
        eps5, eps6 = scol(1), scol(1)
        neg_g, bbg = scol(E), scol(E)
        gpair = scol(2 * HD)
        g2row = gpair[:, HD:2 * HD]
        amask = scol(E * CS)
        upd_mask = scol(E)
        w0 = scol(J * HD)
        b0 = scol(HD)
        stat = scol(J * B * 2 * 6)
        mv = scol(J * B * 2)
        gm = scol(J * B * 2)
        gdev = scol(J * B)
        tok = scol(CS)
        one = scol(1)

        counts = []

        def value(eng, v):
            if isinstance(v, int):
                return v
            r = eng.alloc_register(f"count{len(counts)}")
            counts.append(r)
            eng.reg_mov(r, v)
            return eng.snap(r, min_val=1, max_val=1 << 12)

        class Carve:
            def __init__(self):
                self.at = 0

            def __call__(self, *dims):
                n = int(np.prod(dims))
                v = work[:, self.at:self.at + n]
                self.at += n
                assert self.at <= work.shape[1], self.at
                if len(dims) == 1:
                    return v
                names = "abcdef"[:len(dims)]
                return v.rearrange(f"p ({' '.join(names)}) -> p {' '.join(names)}",
                                   **dict(zip(names, dims)))

        PS = ctx.enter_context(nc.psum_tensor("PS", [P, 8, BLK], F32))

        cst = sb("cst", [P, NCONST])
        ones_blk = sb("ones_blk", [P, P])
        mask2 = sb("mask2", [P, B * 2 * E * CS])

        def ccol(name, i=0, n=None, rows=P):
            at, w = CONST_AT[name]
            n = w - i if n is None else n
            return cst[0:rows, at + i:at + i + n]

        ident, mean_c, mean_g = ccol("ident"), ccol("mean_c"), ccol("mean_g")

        def group_norm(block, src, tag, extra_vector=None, extra_loads=None):
            s_bn, s_mv, s_g1, s_gc, s_dev, s_g2, s_var, s_sd, s_r, s_a = (
                sem(f"{tag}_{n}") for n in ("bn", "mv", "g1", "gc", "dev", "g2", "var", "sd", "r", "a"))
            s_in = [sem(f"{tag}_in{b}") for b in range(B)]
            s_par = sem(f"{tag}_par")
            st = stat.rearrange("p (k s) -> p k s", s=6)

            @block.sync
            def _(sp):
                if extra_loads:
                    extra_loads(sp, s_in, s_par)

            @block.vector
            def _(dve):
                for b in range(B):
                    for j in range(J):
                        k = b * J + j
                        if extra_loads:
                            dve.wait_ge(s_in[b], 16)
                        for h in range(PER):
                            nc.vector.bn_stats(
                                st[:, PER * k + h, :],
                                src[:, j, b * N + h * BLK:b * N + (h + 1) * BLK]).then_inc(s_bn, 1)
                dve.wait_ge(s_bn, B * J * PER)
                for k in range(B * J):
                    nc.vector.bn_aggr(mv[:, 2 * k:2 * k + 2], st[:, PER * k:PER * k + PER, :]
                                      ).then_inc(s_mv, 1)
                dve.wait_ge(s_g1, 1)
                nc.vector.tensor_copy(gm, PS[:, 0, 0:2 * B * J]).then_inc(s_gc, 1)
                dve.wait_ge(s_gc, 1)
                dve.wait_ge(s_mv, B * J)
                m2 = mv.rearrange("p (k t) -> p k t", t=2)
                g2 = gm.rearrange("p (k t) -> p k t", t=2)
                nc.vector.tensor_tensor(gdev, m2[:, :, 0], g2[:, :, 0], ALU.subtract).then_inc(s_dev, 1)
                dve.wait_ge(s_dev, 1)
                nc.vector.tensor_tensor(gdev, gdev, gdev, ALU.mult).then_inc(s_dev, 1)
                dve.wait_ge(s_g2, 1)
                nc.vector.tensor_tensor(gdev, PS[:, 1, 0:B * J], g2[:, :, 1], ALU.add).then_inc(s_var, 1)
                dve.wait_ge(s_sd, 1)
                nc.vector.reciprocal(gn_a, gn_a).then_inc(s_r, 1)
                dve.wait_ge(s_r, 1)
                nc.vector.scalar_tensor_tensor(gn_c, g2[:, :, 0], -1.0, gn_a, ALU.mult, ALU.mult
                                               ).then_inc(s_a, 1)
                if extra_vector:
                    extra_vector(dve, s_par)

            @block.tensor
            def _(pe):
                if extra_loads:
                    pe.wait_ge(s_par, 32)
                pe.wait_ge(s_mv, B * J)
                nc.tensor.matmul(PS[:, 0, 0:2 * B * J], mean_g, mv, start=True, stop=True).then_inc(s_g1, 1)
                pe.wait_ge(s_dev, 2)
                nc.tensor.matmul(PS[:, 1, 0:B * J], mean_g, gdev, start=True, stop=True).then_inc(s_g2, 1)

            @block.scalar
            def _(act):
                if extra_loads:
                    act.wait_ge(s_k0, 2)
                act.wait_ge(s_var, 1)
                nc.scalar.activation(gn_a, gdev, ACT.Sqrt, bias=eps5).then_inc(s_sd, 1)

        xv = x.rearrange("b (j p) n -> p j b n", p=P)
        s_k0 = sem("s_k0")
        s_w = sem("s_w")

        def first_loads(sp, s_in, s_par):
            sp.dma_start(par[:, :], params).then_inc(s_par, 16)
            sp.dma_start(cst[:, :], consts).then_inc(s_par, 16)
            for b in range(B):
                sp.dma_start(X[:, :, b * N:(b + 1) * N], xv[:, :, b, :]).then_inc(s_in[b], 16)

        with nc.Block() as block:
            s_d = sem("derive")

            def derive(dve, s_par):
                n = [0]

                def link(ins):
                    n[0] += 1
                    ins.then_inc(s_d, 1)
                    dve.wait_ge(s_d, n[0])

                dve.wait_ge(s_par, 32)
                nc.vector.tensor_scalar(neg_g, pcol("g", 0, E), -1.0, None, ALU.mult).then_inc(s_d, 1)
                nc.vector.tensor_tensor(bbg, pcol("bb", 0, E), pcol("g", 0, E), ALU.mult).then_inc(s_d, 1)
                nc.vector.tensor_tensor(g2row, pcol("g_row", 0, HD), pcol("g_row", 0, HD), ALU.mult
                                        ).then_inc(s_d, 1)
                n[0] = 3
                link(nc.vector.tensor_tensor(tok, ccol("inv_t"), pcol("delta", 0, CS), ALU.add))
                link(nc.vector.tensor_scalar(tok, tok, 0.0, None, ALU.max))
                link(nc.vector.tensor_tensor(
                    amask.rearrange("p (e t) -> p e t", e=E),
                    ccol("causal").rearrange("p (e t) -> p e t", e=E),
                    tok.unsqueeze(1).broadcast_to([P, E, CS]), ALU.mult))
                link(nc.vector.tensor_scalar(amask, amask, -1.0, None, ALU.mult))
                link(nc.vector.tensor_scalar(upd_mask, ccol("emask"), tok[:, CS - 1:CS], -1.0,
                                             ALU.mult, ALU.mult))
                link(nc.vector.tensor_scalar(ones_blk[:, :], ccol("chunk_ones"), tok[:, CS - 1:CS], -1.0,
                                             ALU.mult, ALU.mult))
                w1 = pcol("w1", 0, J * HD).rearrange("p (j d) -> p j d", d=HD)
                link(nc.vector.tensor_reduce(gdev[:, 0:J], w1, AX.X, ALU.add))
                link(nc.vector.tensor_reduce(gdev[:, J:J + 1], pcol("b1_row", 0, HD), AX.X, ALU.add))
                link(nc.vector.scalar_tensor_tensor(
                    w0.rearrange("p (j d) -> p j d", d=HD),
                    gdev[:, 0:J].unsqueeze(2).broadcast_to([P, J, HD]), -1.0 / HD, w1, ALU.mult, ALU.add))
                link(nc.vector.scalar_tensor_tensor(
                    b0, gdev[:, J:J + 1].broadcast_to([P, HD]), -1.0 / HD, pcol("b1_row", 0, HD),
                    ALU.mult, ALU.add))

            @block.gpsimd
            def _(pool):
                pool.memset(eps5, EPS_GN).then_inc(s_k0, 1)
                pool.memset(eps6, EPS_IN).then_inc(s_k0, 1)
                pool.memset(one, 1.0).then_inc(s_k0, 1)
                pool.memset(gpair[:, 0:HD], 1.0).then_inc(s_k0, 1)

            group_norm(block, X, "gn1", derive, first_loads)

        carve = Carve()
        cosT, sinT = carve(N), carve(N)
        sq = carve(J, BLK)
        sd = carve(BLK)
        kc, ksw = carve(2, BLK), carve(2, BLK)
        wkv = carve(J, 2 * C)
        wl = carve(J, NH)
        wvw = wsm
        swap = [(i + HD // 2) % HD for i in range(HD)]

        def blk_of(t, i):
            return t[:, ds(i * BLK, BLK)]

        def has(i, n):
            return not isinstance(i, int) or i + n < NBLK

        def layer_norm(tag, src, sq, sd, eps, w, b, scale, ready=None):
            q = {n: sem(f"{tag}_{n}") for n in ("in", "mean", "xc", "sq", "var", "sd", "rs", "xh", "xn")}

            def tile(i, j):
                return src[:, j, ds(i * BLK, BLK)]

            def act_a(act, i):
                for j in range(J):
                    scale(act, i, j).then_inc(q["in"], 1)

            def pe_mean(pe, i, first):
                pe.wait_ge(ready or q["in"], i * J + J)
                if not first:
                    pe.wait_ge(q["xc"], i * J)
                for j in range(J):
                    m = nc.tensor.matmul(PS[:, 0, :], mean_c, tile(i, j), start=(j == 0), stop=(j == J - 1))
                m.then_inc(q["mean"], 1)

            def dve_center(dve, i):
                dve.wait_ge(q["mean"], i + 1)
                for j in range(J):
                    nc.vector.tensor_tensor(tile(i, j), tile(i, j), PS[:, 0, :], ALU.subtract
                                            ).then_inc(q["xc"], 1)

            def act_square(act, i, first):
                if not first:
                    act.wait_ge(q["var"], i + 0)
                for j in range(J):
                    act.wait_ge(s_k0, 2)
                    act.wait_ge(q["xc"], i * J + j + 1)
                    nc.scalar.activation(sq[:, j, :], tile(i, j), ACT.Square).then_inc(q["sq"], 1)

            def pe_var(pe, i, first):
                pe.wait_ge(q["sq"], i * J + J)
                if not first:
                    pe.wait_ge(q["sd"], i + 0)
                for j in range(J):
                    m = nc.tensor.matmul(PS[:, 1, :], mean_c, sq[:, j, :], start=(j == 0), stop=(j == J - 1))
                m.then_inc(q["var"], 1)

            def act_sd(act, i, first):
                act.wait_ge(q["var"], i + 1)
                if not first:
                    act.wait_ge(q["xh"], i * J)
                nc.scalar.activation(sd, PS[:, 1, :], ACT.Sqrt, bias=eps).then_inc(q["sd"], 1)

            def dve_scale(dve, i):
                dve.wait_ge(q["sd"], i + 1)
                nc.vector.reciprocal(sd, sd).then_inc(q["rs"], 1)
                dve.wait_ge(q["rs"], i + 1)
                for j in range(J):
                    nc.vector.tensor_tensor(tile(i, j), tile(i, j), sd, ALU.mult).then_inc(q["xh"], 1)

            def act_affine(act, i):
                for j in range(J):
                    act.wait_ge(s_k0, 2)
                    act.wait_ge(q["xh"], i * J + j + 1)
                    nc.scalar.activation(tile(i, j), tile(i, j), ACT.Identity, scale=pcol(w, j),
                                         bias=pcol(b, j)).then_inc(q["xn"], 1)

            return q, tile, act_a, pe_mean, dve_center, act_square, pe_var, act_sd, dve_scale, act_affine

        ga8 = sb("ga8", [P, 2, J, NBLK])

        def spread_gn(dve, s):
            for k, src in enumerate((gn_a, gn_c)):
                for j in range(J):
                    nc.vector.tensor_copy(
                        ga8[:, k, j, :].rearrange("p (b h) -> p b h", h=PER),
                        src.rearrange("p (b j) -> p b j", j=J)[:, :, j].unsqueeze(2).broadcast_to([P, B, PER])
                    ).then_inc(s, 1)

        s_sp = sem("gn_spread")
        with nc.Block() as block:
            q1, xt, act_a, pe_mean, dve_center, act_square, pe_var, act_sd, dve_scale, act_affine = \
                layer_norm("ln1", X, sq, sd, eps5, "ln_w", "ln_b",
                           lambda act, i, j: nc.scalar.activation(
                               X[:, j, ds(i * BLK, BLK)], X[:, j, ds(i * BLK, BLK)], ACT.Identity,
                               scale=ga8[:, 0, j, ds(i, 1)], bias=ga8[:, 1, j, ds(i, 1)]))
            s_proj, s_kc, s_ksw, s_ksin, s_rope, s_tt, s_lr, s_kperm, s_ttf, s_rt = (
                sem(n) for n in ("proj", "kc", "ksw", "ksin", "rope", "tt", "lr", "kperm", "ttf", "ropetab"))
            NPJ = 7

            @block.sync
            def _(sp):
                sp.dma_start(wkv[:, :, 0:C], wk).then_inc(s_w, 16)
                sp.dma_start(wkv[:, :, C:2 * C], wq).then_inc(s_w, 16)
                sp.dma_start(wvw[:, :, :], wv).then_inc(s_w, 16)
                sp.dma_start(wl, wlr).then_inc(s_w, 16)
                sp.dma_start(cosT, rope[:, 0, :]).then_inc(s_rt, 16)
                sp.dma_start(sinT, rope[:, 1, :]).then_inc(s_rt, 16)

                def permute(i, first):
                    if not first:
                        sp.wait_ge(s_kperm, i * 128)
                    sp.wait_ge(s_rope, i * 2 * J + J)
                    for k in range(J):
                        for a2 in range(2):
                            for e in range(E):
                                a = 2 * k + a2
                                r = 2 * HD * a2 + HD * e
                                sp.dma_start(KN[HD * a:HD * a + HD, e, ds(i * BLK, BLK)],
                                             KP[r:r + HD, k, ds(i * BLK, BLK)]).then_inc(s_kperm, 16)
                permute(0, True)
                with sp.Fori(1, NBLK) as i:
                    permute(i, False)
                sp.wait_ge(s_kperm, NBLK * 128)

            @block.tensor
            def _(pe):
                pe.wait_ge(s_w, 64)

                def proj(i, m, first):
                    if m < 2 * J:
                        lhs = lambda j: wkv[:, j, m * P:(m + 1) * P]
                    elif m < 3 * J:
                        lhs = lambda j: wvw[:, j, (m - 2 * J) * P:(m - 2 * J + 1) * P]
                    else:
                        lhs = lambda j: wl[:, j, :]
                    if m == NPJ - 1:
                        first_tile = value(pe, i * (2 * J) + 1)
                        pe.wait_ge(s_w, 64)
                        pe.wait_ge(s_ksw, first_tile)
                        o = PS[0:NH, 2, :]
                    else:
                        o = PS[:, 2 + m, :]
                        if not first:
                            if m < 2 * J:
                                pe.wait_ge(s_ksw, (i - 1) * (2 * J) + m + 1)
                            else:
                                pe.wait_ge(s_tt, (i - 1) * J + m - 2 * J + 1)
                            if m == 0:
                                pe.wait_ge(s_lr, i + 0)
                    for j in range(J):
                        mm = nc.tensor.matmul(o, lhs(j), xt(i, j), start=(j == 0), stop=(j == J - 1))
                    mm.then_inc(s_proj, 1)

                def body(i, first):
                    pe.wait_ge(q1["xn"], i * J + J)
                    if has(i, 1):
                        pe_var(pe, i + 1, False)
                    if has(i, 2):
                        pe_mean(pe, i + 2, False)
                    for m in range(NPJ):
                        proj(i, m, first)

                pe_mean(pe, 0, True)
                pe_mean(pe, 1, False)
                pe_var(pe, 0, True)
                body(0, True)
                with pe.Fori(1, NBLK - 2) as i:
                    body(i, False)
                body(NBLK - 2, False)
                body(NBLK - 1, False)

            @block.vector
            def _(dve):
                def rope_in(i, m, first):
                    t = m % 2
                    dve.wait_ge(s_proj, i * NPJ + m + 1)
                    if not (first and m < 2):
                        dve.wait_ge(s_rope, i * (2 * J) + m - 1)
                    h = ds((i % PER) * BLK, BLK)
                    nc.vector.tensor_tensor(kc[:, t, :], PS[:, 2 + m, :], cosT[:, h], ALU.mult).then_inc(s_kc, 1)
                    nc.vector.stream_shuffle(ksw[:, t, :], PS[:, 2 + m, :], swap).then_inc(s_ksw, 1)

                def finish_target(i):
                    dve.wait_ge(s_kperm, i * 128 + 128)
                    for j in range(J):
                        dve.wait_ge(s_tt, i * J + j + 1)
                        nc.vector.scalar_tensor_tensor(TT[:, j, ds(i * BLK, BLK)], KN[:, j, ds(i * BLK, BLK)],
                                                       pcol("g", j), TT[:, j, ds(i * BLK, BLK)],
                                                       ALU.mult, ALU.add).then_inc(s_ttf, 1)

                def body(i, first):
                    if has(i, 1):
                        dve_scale(dve, i + 1)
                    if has(i, 2):
                        dve_center(dve, i + 2)
                    for m in range(2 * J):
                        rope_in(i, m, first)
                    if not first:
                        finish_target(i - 1)

                spread_gn(dve, s_sp)
                dve.wait_ge(s_rt, 32)
                dve_center(dve, 0)
                dve_center(dve, 1)
                dve_scale(dve, 0)
                body(0, True)
                with dve.Fori(1, NBLK - 2) as i:
                    body(i, False)
                body(NBLK - 2, False)
                body(NBLK - 1, False)
                finish_target(NBLK - 1)

            @block.gpsimd
            def _(pool):
                def rope_out(i, m):
                    t = m % 2
                    dst = (KP if m < J else QP)[:, m % J, ds(i * BLK, BLK)]
                    h = ds((i % PER) * BLK, BLK)
                    done = value(pool, i * (2 * J) + (m + 1))
                    pool.wait_ge(s_rt, 32)
                    pool.wait_ge(s_ksw, done)
                    nc.gpsimd.tensor_tensor(ksw[:, t, :], ksw[:, t, :], sinT[:, h], ALU.mult).then_inc(s_ksin, 1)
                    pool.wait_ge(s_rt, 32)
                    pool.wait_ge(s_ksin, done)
                    nc.gpsimd.tensor_tensor(dst, ksw[:, t, :], kc[:, t, :], ALU.add).then_inc(s_rope, 1)
                pool.wait_ge(s_rt, 32)
                with pool.Fori(0, NBLK) as i:
                    for m in range(2 * J):
                        rope_out(i, m)

            @block.scalar
            def _(act):
                def v_out(i, j):
                    act.wait_ge(s_proj, i * NPJ + 2 * J + j + 1)
                    nc.scalar.activation(TT[:, j, ds(i * BLK, BLK)], PS[:, 2 + 2 * J + j, :], ACT.Identity,
                                         scale=neg_g[:, j:j + 1], bias=bbg[:, j:j + 1]).then_inc(s_tt, 1)

                def lr_out(i):
                    act.wait_ge(s_proj, i * NPJ + NPJ)
                    nc.scalar.activation(X[0:NH, 0, ds(i * BLK, BLK)], PS[0:NH, 2, :], ACT.Identity,
                                         bias=pcol("lr_b", rows=NH)).then_inc(s_lr, 1)

                def body(i):
                    if has(i, 1):
                        act_sd(act, i + 1, False)
                        act_affine(act, i + 1)
                    if has(i, 2):
                        act_square(act, i + 2, False)
                    if has(i, 3):
                        act_a(act, i + 3)
                    for j in range(J):
                        v_out(i, j)
                    lr_out(i)

                act.wait_ge(s_sp, 2 * J)
                for i in range(3):
                    act_a(act, i)
                    if i == 0:
                        act_square(act, 0, True)
                act_sd(act, 0, True)
                act_affine(act, 0)
                act_square(act, 1, False)
                with act.Fori(0, NBLK - 3) as i:
                    body(i)
                for i in range(NBLK - 3, NBLK):
                    body(i)

        lrt = work[:, 0:NBLK * B * NH].rearrange("p (s b h) -> p s b h", s=8, b=B)
        lrm = work[:, 256:512]
        with nc.Block() as block:
            s_sig, s_tr, s_cp, s_spread, s_mask, s_lrh, s_qperm, s_ct, s_ctc = (
                sem(n) for n in ("sig", "lr_tr", "lr_cp", "lr_spread", "lr_mask", "lr_h", "qperm", "center",
                                 "centered"))
            NCT = 4

            @block.scalar
            def _(act):
                nc.scalar.activation(X[0:NH, 0, :], X[0:NH, 0, :], ACT.Sigmoid).then_inc(s_sig, 1)
                for n in range(J * NBLK):
                    act.wait_ge(s_ct, n + 1)
                    nc.scalar.activation(TT[:, n % J, (n // J) * BLK:(n // J + 1) * BLK], PS[:, 3 + n % NCT, :],
                                         ACT.Copy).then_inc(s_ctc, 1)

            @block.tensor
            def _(pe):
                def center(n):
                    if n >= NCT:
                        pe.wait_ge(s_ctc, n - NCT + 1)
                    nc.tensor.matmul(PS[:, 3 + n % NCT, :], ccol("center_h"),
                                     TT[:, n % J, (n // J) * BLK:(n // J + 1) * BLK], start=True, stop=True
                                     ).then_inc(s_ct, 1)

                for n in range(NCT):
                    center(n)
                pe.wait_ge(s_sig, 1)
                for b in range(B):
                    for s in range(8):
                        tr = nc.tensor.transpose(PS[:, 0, (s * B + b) * NH:(s * B + b + 1) * NH],
                                                 X[0:NH, 0, b * N + s * P:b * N + (s + 1) * P],
                                                 ident[0:NH, 0:NH])
                tr.then_inc(s_tr, 1)
                pe.wait_ge(s_cp, 1)
                for n in range(8):
                    if n >= 2:
                        pe.wait_ge(s_mask, n - 1)
                    nc.tensor.matmul(PS[:, 1 + n % 2, 0:256], ccol("spread", n * P, P),
                                     lrt.rearrange("p s b h -> p (s b h)"), start=True, stop=True
                                     ).then_inc(s_spread, 1)
                    if NCT + n < J * NBLK:
                        center(NCT + n)
                for n in range(NCT + 8, J * NBLK):
                    center(n)

            @block.vector
            def _(dve):
                m4 = mask2.rearrange("p (b s m) -> p b s m", b=B, s=2)
                nc.vector.tensor_copy(m4[:, :, 0, :], amask.unsqueeze(1).broadcast_to([P, B, E * CS]))
                nc.vector.tensor_copy(m4[:, :, 1, :].rearrange("p b (e t) -> p b e t", e=E),
                                      upd_mask.unsqueeze(1).unsqueeze(3).broadcast_to([P, B, E, CS]))
                dve.wait_ge(s_tr, 1)
                nc.vector.tensor_copy(lrt.rearrange("p s b h -> p (s b h)"), PS[:, 0, 0:256]).then_inc(s_cp, 1)
                for n in range(8):
                    dve.wait_ge(s_spread, n + 1)
                    if n:
                        dve.wait_ge(s_lrh, n)
                    nc.vector.tensor_tensor(
                        lrm.rearrange("p (k h) -> p k h", h=NH),
                        PS[:, 1 + n % 2, 0:256].rearrange("p (k h) -> p k h", h=NH),
                        ccol("headmask").unsqueeze(1).broadcast_to([P, 8 * B, NH]), ALU.mult).then_inc(s_mask, 1)
                    dve.wait_ge(s_mask, n + 1)
                    nc.vector.tensor_reduce(
                        lrh.rearrange("p (s n) b -> p s n b", n=8)[:, :, n, :],
                        lrm.rearrange("p (s b h) -> p s b h", b=B, h=NH), AX.X, ALU.add).then_inc(s_lrh, 1)

            @block.sync
            def _(sp):
                sp.wait_ge(s_tr, 1)
                for k in range(J):
                    for a2 in range(2):
                        for e in range(E):
                            a = 2 * k + a2
                            r = 2 * HD * a2 + HD * e
                            sp.dma_start(X[HD * a:HD * a + HD, e, :], QP[r:r + HD, k, :]).then_inc(s_qperm, 16)

        carve = Carve()
        KT2 = [carve(J * B, E, CS) for _ in range(2)]
        QT2 = [carve(J * B, E, CS) for _ in range(2)]
        R = [carve(J, B, HD + 2 * CS) for _ in range(2)]
        TK = [carve(2, B, E, CS) for _ in range(2)]
        TKH = [carve(2, B, HD) for _ in range(2)]
        KHX = [carve(E, B, HD) for _ in range(2)]
        S1 = [carve(B * 2, CS) for _ in range(2)]
        AM = [carve(B, 2, E, CS) for _ in range(2)]
        Bs = [carve(B, HD) for _ in range(2)]
        ZP, XP = carve(2, B, HD), carve(2, B, HD)
        SQ, Y0, Y1, YL, WX = (carve(B, HD) for _ in range(5))
        GL = [carve(B, HD) for _ in range(2)]
        ZQ = [carve(B, HD) for _ in range(2)]
        SQQ, ZN, ZT = (carve(B, HD) for _ in range(3))
        sz = carve(2 * B)
        ss, ssq, rl, m2, m2r = (carve(B) for _ in range(5))
        sds = carve(2 * B)
        sd1, sdq = sds[:, 0:B], sds[:, B:2 * B]

        def bc(v, n=HD):
            return v.unsqueeze(2).broadcast_to([P, v.shape[1], n])

        WB, BB, ZB, QB = 0, 2, (3, 4), (5, 6)
        ZW = HD + 2 * CS

        with nc.Block() as block:
            names = ("init wcopy bcopy kt2 qt2 qr kr stage tkh khx base qbase corr s1 am z p sq sz zc ss sd r xp "
                     "y yl yp m mr w rl gl upd attn zq sqq ssq sdq rq zn zt ot").split()
            q = {n: sem(f"scan_{n}") for n in names}

            def chunk(t, c):
                return t.rearrange("p j (b n) -> p (j b) n", b=B)[:, :, ds(c * CS, CS)]

            def past(c, n):
                return c >= n if isinstance(c, int) else n <= 2

            def run_chunks(eng, body):
                body(0, 0)
                body(1, 1)
                with eng.Fori(1, NC // 2 - 2) as pair:
                    c = pair * 2
                    body(c, 0)
                    body(c + 1, 1)
                for c in range(NC - 4, NC):
                    body(c, c % 2)

            is_last = lambda c: isinstance(c, int) and c == NC - 1
            near_end = lambda c: isinstance(c, int) and c >= NC - 2

            @block.tensor
            def _(pe):
                for k in range(J):
                    nc.tensor.matmul(PS[:, WB + k, 0:B * HD].rearrange("p (b d) -> p b d", b=B), ident,
                                     w0[:, k * HD:(k + 1) * HD].unsqueeze(1).broadcast_to([P, B, HD]),
                                     start=True, stop=True, skip_group_check=True)
                nc.tensor.matmul(PS[:, BB, 0:B * HD].rearrange("p (b d) -> p b d", b=B), ident,
                                 b0.unsqueeze(1).broadcast_to([P, B, HD]), start=True, stop=True,
                                 skip_group_check=True).then_inc(q["init"], 1)

                def base(n, p, ready, state):
                    pe.wait_ge(q["init"], 1)
                    pe.wait_ge(q["kt2"], ready)
                    pe.wait_ge(q["qr"], ready)
                    pe.wait_ge(q["kr"], min(n + 1, NC - 1) if isinstance(n, int) else ready)
                    pe.wait_ge(q["wcopy"], state)
                    for b in range(B):
                        for k in range(J):
                            for a2 in range(2):
                                r, a = 2 * HD * a2, 2 * k + a2
                                mm = nc.tensor.matmul(
                                    PS[HD * a:HD * a + HD, ZB[p], b * ZW:b * ZW + ZW],
                                    KT2[p][r:r + 64, k * B + b, :, :].rearrange("p e t -> p (e t)"),
                                    R[p][r:r + 64, k, b, :], start=(b == 0), stop=False,
                                    skip_group_check=True)
                    mm.then_inc(q["base"], 1)

                def grads(o, width, bank, p, part):
                    for a in range(4):
                        for b in range(B):
                            mm = nc.tensor.matmul(PS[HD * a:HD * a + HD, bank, b * width:b * width + HD],
                                                  AM[p][HD * a:HD * a + HD, b, part, :, :].rearrange(
                                                      "p e t -> p (e t)"),
                                                  GL[p][HD * a:HD * a + HD, b, :],
                                                  start=False, stop=True, skip_group_check=True)
                    return mm

                def update(p):
                    for k in range(J):
                        for a2 in range(2):
                            a = 2 * k + a2
                            for e in range(E):
                                o = 2 * HD * a2 + HD * e
                                for b in range(B):
                                    nc.tensor.matmul(PS[o:o + HD, WB + k, b * HD:b * HD + HD],
                                                     KHX[p][HD * a:HD * a + HD, e, b, :],
                                                     GL[p][HD * a:HD * a + HD, b, :],
                                                     start=False, stop=True, skip_group_check=True)
                    nc.tensor.matmul(PS[:, BB, 0:B * HD], ones_blk[:, :], GL[p].rearrange("p b d -> p (b d)"),
                                     start=False, stop=True, skip_group_check=True).then_inc(q["upd"], 1)

                def body(c, p):
                    o = 1 - p
                    done, now, nxt = value(pe, c), value(pe, c + 1), value(pe, c + 2)
                    before = value(pe, c - 1) if past(c, 2) else None
                    if past(c, 1):
                        pe.wait_ge(q["init"], 1)
                        pe.wait_ge(q["gl"], done)
                        pe.wait_ge(q["am"], done)
                        pe.wait_ge(q["s1"], now)
                        grads(c, ZW, ZB[p], o, 1).then_inc(q["corr"], 1)
                        pe.wait_ge(q["init"], 1)
                        pe.wait_ge(q["khx"], done)
                        pe.wait_ge(q["bcopy"], done)
                        update(o)
                        grads(c, HD, QB[o], o, 0).then_inc(q["attn"], 1)
                    else:
                        base(0, 0, 1, 1)
                    if not is_last(c):
                        base(c + 1, o, nxt, now)
                    pe.wait_ge(q["init"], 1)
                    pe.wait_ge(q["qt2"], now)
                    pe.wait_ge(q["wcopy"], now)
                    if past(c, 2):
                        pe.wait_ge(q["zq"], before)
                    for b in range(B):
                        for k in range(J):
                            for a2 in range(2):
                                r, a = 2 * HD * a2, 2 * k + a2
                                mm = nc.tensor.matmul(
                                    PS[HD * a:HD * a + HD, QB[p], b * HD:b * HD + HD],
                                    QT2[p][r:r + 64, k * B + b, :, :].rearrange("p e t -> p (e t)"),
                                    R[o][r:r + 64, k, b, 0:HD], start=(b == 0), stop=False,
                                    skip_group_check=True)
                    mm.then_inc(q["qbase"], 1)

                run_chunks(pe, body)
                pe.wait_ge(q["gl"], NC)
                pe.wait_ge(q["am"], NC)
                grads(NC, HD, QB[1], 1, 0).then_inc(q["attn"], 1)

            @block.vector
            def _(dve):
                def rows_of(c, p):
                    dve.wait_ge(q["stage"], c + 1)
                    if past(c, 2) and not (isinstance(c, int) and c == 2):
                        dve.wait_ge(q["khx"], c - 1)
                    elif past(c, 2):
                        dve.wait_ge(q["khx"], 1)
                    nc.vector.transpose(TKH[p].rearrange("p s b d -> p (s b d)"),
                                        TK[p].rearrange("p s b e t -> p (s b e t)")).then_inc(q["tkh"], 1)

                def out_rows(c, p):
                    dve.wait_ge(q["attn"], c + 1)
                    nc.vector.tensor_tensor(ZQ[p], PS[:, QB[p], 0:B * HD].rearrange("p (b d) -> p b d", b=B),
                                            Bs[p], ALU.add).then_inc(q["zq"], 1)

                def out_var(c):
                    dve.wait_ge(q["sqq"], c + 1)
                    nc.vector.tensor_reduce(ssq, SQQ, AX.X, ALU.add).then_inc(q["ssq"], 1)

                def out_r(c):
                    dve.wait_ge(q["sdq"], c + 1)
                    nc.vector.reciprocal(sdq, sdq).then_inc(q["rq"], 1)

                def out_turn(c):
                    dve.wait_ge(q["zn"], c + 1)
                    nc.vector.transpose(ZT.rearrange("p b d -> p (b d)"), ZN.rearrange("p b d -> p (b d)")
                                        ).then_inc(q["zt"], 1)

                def body(c, p):
                    zb = PS[:, ZB[p], 0:B * ZW].rearrange("p (b n) -> p b n", b=B)[:, :, 0:HD]
                    flat2 = lambda v: v.rearrange("p s b d -> p (s b) d")
                    if past(c, 1):
                        dve.wait_ge(q["corr"], c + 0)
                    else:
                        dve.wait_ge(q["s1"], 1)
                    dve.wait_ge(q["bcopy"], max(c, 1) if isinstance(c, int) else c + 0)
                    nc.vector.tensor_tensor(ZP[:, 0, :, :], zb, Bs[1 - p] if past(c, 1) else Bs[0], ALU.add
                                            ).then_inc(q["z"], 1)
                    dve.wait_ge(q["z"], c + 1)
                    nc.vector.tensor_tensor(ZP[:, 1, :, :], ZP[:, 0, :, :],
                                            g2row.unsqueeze(1).broadcast_to([P, B, HD]), ALU.mult
                                            ).then_inc(q["p"], 1)
                    dve.wait_ge(q["sq"], c + 1)
                    nc.vector.tensor_reduce(ss, SQ, AX.X, ALU.add).then_inc(q["ss"], 1)
                    dve.wait_ge(q["p"], c + 1)
                    nc.vector.tensor_reduce(sz, flat2(ZP), AX.X, ALU.add).then_inc(q["sz"], 1)
                    dve.wait_ge(q["sd"], c + 1)
                    if past(c, 2):
                        dve.wait_ge(q["sdq"], c - 1)
                        nc.vector.reciprocal(sds, sds).then_inc(q["r"], 1)
                    else:
                        nc.vector.reciprocal(sd1, sd1).then_inc(q["r"], 1)
                    dve.wait_ge(q["sz"], c + 1)
                    nc.vector.scalar_tensor_tensor(
                        flat2(ZP), sz.unsqueeze(2).broadcast_to([P, 2 * B, HD]), -1.0 / HD, flat2(ZP),
                        ALU.mult, ALU.add).then_inc(q["zc"], 1)
                    dve.wait_ge(q["r"], c + 1)
                    dve.wait_ge(q["zc"], c + 1)
                    nc.vector.tensor_tensor(XP, ZP, sd1.unsqueeze(1).unsqueeze(3).broadcast_to([P, 2, B, HD]),
                                            ALU.mult).then_inc(q["xp"], 1)
                    dve.wait_ge(q["xp"], c + 1)
                    nc.vector.tensor_tensor(Y0, XP[:, 1, :, :], TKH[p][:, 0, :, :], ALU.add).then_inc(q["y"], 1)
                    dve.wait_ge(q["y"], c + 1)
                    nc.vector.tensor_tensor(Y1, Y0, XP[:, 0, :, :], ALU.mult).then_inc(q["yp"], 1)
                    dve.wait_ge(q["yp"], c + 1)
                    nc.vector.tensor_reduce(m2, Y1, AX.X, ALU.add).then_inc(q["m"], 1)
                    dve.wait_ge(q["m"], c + 1)
                    dve.wait_ge(q["rl"], c + 1)
                    nc.vector.scalar_tensor_tensor(m2r, m2, -1.0 / HD, rl, ALU.mult, ALU.mult
                                                   ).then_inc(q["mr"], 1)
                    dve.wait_ge(q["mr"], c + 1)
                    nc.vector.tensor_tensor(WX, XP[:, 0, :, :], bc(m2r), ALU.mult).then_inc(q["w"], 1)
                    dve.wait_ge(q["w"], c + 1)
                    dve.wait_ge(q["yl"], c + 1)
                    nc.vector.tensor_tensor(GL[p], WX, YL, ALU.add).then_inc(q["gl"], 1)
                    if past(c, 1):
                        out_rows(c - 1, 1 - p)
                    if past(c, 2):
                        out_turn(c - 2)
                    if not is_last(c):
                        rows_of(c + 1, 1 - p)
                    if past(c, 1):
                        out_var(c - 1)

                rows_of(0, 0)
                run_chunks(dve, body)
                out_rows(NC - 1, 1)
                out_r(NC - 2)
                dve.wait_ge(q["ot"], NC - 2)
                out_turn(NC - 2)
                out_var(NC - 1)
                out_r(NC - 1)
                dve.wait_ge(q["ot"], NC - 1)
                out_turn(NC - 1)

            @block.gpsimd
            def _(pool):
                def prepare(c, p):
                    if past(c, 2):
                        pool.wait_ge(q["base"], c - 1)
                    nc.gpsimd.tensor_tensor(
                        KT2[p], chunk(KP, c).unsqueeze(2).broadcast_to([P, J * B, E, CS]),
                        ccol("emask_k").unsqueeze(1).unsqueeze(3).broadcast_to([P, J * B, E, CS]),
                        ALU.mult).then_inc(q["kt2"], 1)
                    nc.gpsimd.tensor_copy(R[p].rearrange("p k b n -> p (k b) n")[:, :, HD:HD + CS],
                                          chunk(QP, c)).then_inc(q["qr"], 1)
                    if past(c, 2):
                        pool.wait_ge(q["tkh"], c - 1)
                    nc.gpsimd.tensor_copy(TK[p][:, 0, :, :, :].rearrange("p b e t -> p e b t"),
                                          TT.rearrange("p e (b n) -> p e b n", b=B)[:, :, :, ds(c * CS, CS)])
                    nc.gpsimd.tensor_copy(TK[p][:, 1, :, :, :].rearrange("p b e t -> p e b t"),
                                          KN.rearrange("p e (b n) -> p e b n", b=B)[:, :, :, ds(c * CS, CS)]
                                          ).then_inc(q["stage"], 1)

                def khx(c, p):
                    pool.wait_ge(q["tkh"], c + 1)
                    if past(c, 2):
                        pool.wait_ge(q["upd"], c - 1)
                    nc.gpsimd.tensor_tensor(
                        KHX[p], TKH[p][:, 1, :, :].unsqueeze(1).broadcast_to([P, E, B, HD]),
                        upd_mask.unsqueeze(2).unsqueeze(3).broadcast_to([P, E, B, HD]), ALU.mult
                    ).then_inc(q["khx"], 1)

                def masks(c, p):
                    pool.wait_ge(q["s1"], c + 1)
                    if past(c, 2):
                        pool.wait_ge(q["attn"], c - 1)
                    nc.gpsimd.tensor_tensor(
                        AM[p].rearrange("p b s e t -> p (b s) e t"),
                        S1[p].unsqueeze(2).broadcast_to([P, 2 * B, E, CS]),
                        mask2.rearrange("p (k e t) -> p k e t", e=E, t=CS), ALU.mult).then_inc(q["am"], 1)

                def out_norm(c, p):
                    nc.gpsimd.tensor_tensor(ZN, ZQ[p], bc(sdq), ALU.mult).then_inc(q["zn"], 1)

                def body(c, p):
                    if not near_end(c):
                        prepare(c + 2, p)
                    pool.wait_ge(q["r"], c + 1)
                    nc.gpsimd.tensor_tensor(rl, sd1, lrh[:, ds(c, 1), :].squeeze(1), ALU.mult
                                            ).then_inc(q["rl"], 1)
                    pool.wait_ge(q["rl"], c + 1)
                    pool.wait_ge(q["y"], c + 1)
                    nc.gpsimd.tensor_tensor(YL, Y0, bc(rl), ALU.mult).then_inc(q["yl"], 1)
                    if past(c, 2):
                        out_norm(c - 2, p)
                    khx(c, p)
                    if not is_last(c):
                        masks(c + 1, 1 - p)

                prepare(0, 0)
                prepare(1, 1)
                masks(0, 0)
                run_chunks(pool, body)
                for c in (NC - 2, NC - 1):
                    pool.wait_ge(q["rq"], c - NC + 3)
                    out_norm(c, c % 2)

            @block.scalar
            def _(act):
                wb = PS[:, WB:WB + J, 0:B * HD].rearrange("p k (b d) -> p k b d", b=B)

                def state_w(p):
                    for k in range(J):
                        w = nc.scalar.activation(R[p][:, k, :, 0:HD], wb[:, k, :, :], ACT.Copy)
                    return w

                def state_b(p):
                    nc.scalar.activation(Bs[p], PS[:, BB, 0:B * HD].rearrange("p (b d) -> p b d", b=B),
                                         ACT.Copy).then_inc(q["bcopy"], 1)

                def next_k(c, p):
                    if past(c, 2):
                        act.wait_ge(q["base"], c - 1)
                    nc.scalar.activation(R[p].rearrange("p k b n -> p (k b) n")[:, :, HD + CS:ZW],
                                         chunk(KP, c + 1), ACT.Copy).then_inc(q["kr"], 1)

                def qt2(c, p):
                    if past(c, 2):
                        act.wait_ge(q["qbase"], c - 1)
                    for e in range(E):
                        a = nc.scalar.activation(QT2[p][:, :, e, :], chunk(QP, c), ACT.Copy,
                                                 scale=ccol("emask_k", e, 1))
                    a.then_inc(q["qt2"], 1)

                def products(c, p):
                    act.wait_ge(q["base"], c + 1)
                    nc.scalar.activation(
                        S1[p].rearrange("p (b s) t -> p b (s t)", b=B),
                        PS[:, ZB[p], 0:B * ZW].rearrange("p (b n) -> p b n", b=B)[:, :, HD:ZW],
                        ACT.Identity, bias=one).then_inc(q["s1"], 1)

                def out_square(c, p):
                    act.wait_ge(q["zq"], c + 1)
                    nc.scalar.activation(SQQ, ZQ[p], ACT.Square).then_inc(q["sqq"], 1)

                def out_sd(c):
                    act.wait_ge(q["ssq"], c + 1)
                    nc.scalar.activation(sdq, ssq, ACT.Sqrt, bias=eps6, scale=1.0 / HD).then_inc(q["sdq"], 1)

                def out_store(c):
                    act.wait_ge(q["zt"], c + 1)
                    nc.scalar.activation(
                        TT.rearrange("p e (b n) -> p e b n", b=B)[:, :, :, ds(c * CS, CS)],
                        ZT.rearrange("p b (e t) -> p e b t", e=E), ACT.Copy).then_inc(q["ot"], 1)

                def body(c, p):
                    act.wait_ge(q["z"], c + 1)
                    nc.scalar.activation(SQ, ZP[:, 0, :, :], ACT.Square).then_inc(q["sq"], 1)
                    act.wait_ge(q["ss"], c + 1)
                    nc.scalar.activation(sd1, ss, ACT.Sqrt, bias=eps6, scale=1.0 / HD).then_inc(q["sd"], 1)
                    if past(c, 1):
                        act.wait_ge(q["upd"], c + 0)
                        state_w(1 - p).then_inc(q["wcopy"], 1)
                        state_b(p)
                    if not is_last(c):
                        products(c + 1, 1 - p)
                        qt2(c + 1, 1 - p)
                    if not isinstance(c, int) or c + 3 < NC:
                        next_k(c + 2, p)
                    if past(c, 1):
                        out_square(c - 1, 1 - p)
                        out_sd(c - 1)
                    if past(c, 2):
                        out_store(c - 2)

                next_k(0, 0)
                next_k(1, 1)
                act.wait_ge(q["init"], 1)
                state_w(0)
                state_w(1).then_inc(q["wcopy"], 1)
                state_b(0)
                products(0, 0)
                qt2(0, 0)
                run_chunks(act, body)
                out_square(NC - 1, 1)
                out_sd(NC - 1)
                out_store(NC - 2)
                out_store(NC - 1)

            @block.sync
            def _(sp):
                sp.wait_ge(s_qperm, 16 * 2 * J * E)

        carve = Carve()
        sq, sd = carve(J, BLK), carve(BLK)
        with nc.Block() as block:
            s_pre, s_wo, s_o, s_x1 = (sem(n) for n in ("pre", "wo", "o", "x1"))
            s_xr = [sem(f"xr{b}") for b in range(B)]

            def gain(act, i, j):
                return nc.scalar.activation(blk_of(TT[:, j, :], i), blk_of(TT[:, j, :], i), ACT.Identity,
                                            scale=pcol("g", j), bias=pcol("bb", j))

            q2, ot, act_a, pe_mean, dve_center, act_square, pe_var, act_sd, dve_scale, act_affine = \
                layer_norm("ln2", TT, sq, sd, eps6, "post_w", "post_b", gain,
                           ready=s_pre)

            def residual(dve, i):
                for m in range(J):
                    dve.wait_ge(s_o, i * J + m + 1)
                    nc.vector.tensor_tensor(blk_of(KN[:, m, :], i), PS[:, 2 + m, :],
                                            blk_of(KN[:, m, :], i), ALU.add).then_inc(s_x1, 1)

            @block.sync
            def _(sp):
                sp.dma_start(wsm[:, :, :], wo).then_inc(s_wo, 16)
                for b in range(B):
                    sp.dma_start(KN[:, :, b * N:(b + 1) * N], xv[:, :, b, :]).then_inc(s_xr[b], 16)

            @block.tensor
            def _(pe):
                pe.wait_ge(s_wo, 16)

                def body(i, first):
                    pe.wait_ge(q2["xn"], i * J + J)
                    if has(i, 1):
                        pe_var(pe, i + 1, False)
                    if has(i, 2):
                        pe_mean(pe, i + 2, False)
                    for m in range(J):
                        if not first:
                            pe.wait_ge(s_x1, (i - 1) * J + m + 1)
                        for j in range(J):
                            mm = nc.tensor.matmul(PS[:, 2 + m, :], wsm[:, j, m * P:(m + 1) * P], ot(i, j),
                                                  start=(j == 0), stop=(j == J - 1))
                        mm.then_inc(s_o, 1)

                pe_mean(pe, 0, True)
                pe_mean(pe, 1, False)
                pe_var(pe, 0, True)
                body(0, True)
                with pe.Fori(1, NBLK - 2) as i:
                    body(i, False)
                body(NBLK - 2, False)
                body(NBLK - 1, False)

            @block.vector
            def _(dve):
                dve_center(dve, 0)
                dve_center(dve, 1)
                dve_scale(dve, 0)
                for b in range(B):
                    dve.wait_ge(s_xr[b], 16)
                with dve.Fori(0, NBLK - 2) as i:
                    dve_scale(dve, i + 1)
                    dve_center(dve, i + 2)
                    residual(dve, i)
                dve_scale(dve, NBLK - 1)
                for i in (NBLK - 2, NBLK - 1):
                    residual(dve, i)

            @block.gpsimd
            def _(pool):
                def pre(i):
                    for j in range(J):
                        gained = value(pool, i * J + (j + 1))
                        pool.wait_ge(s_k0, 2)
                        pool.wait_ge(q2["in"], gained)
                        nc.gpsimd.tensor_tensor(blk_of(TT[:, j, :], i), blk_of(TT[:, j, :], i),
                                                blk_of(X[:, j, :], i), ALU.add).then_inc(s_pre, 1)

                for i in range(3):
                    pre(i)
                with pool.Fori(0, NBLK - 3) as i:
                    pre(i + 3)

            @block.scalar
            def _(act):
                def body(i):
                    if has(i, 1):
                        act_sd(act, i + 1, False)
                        act_affine(act, i + 1)
                    if has(i, 2):
                        act_square(act, i + 2, False)
                    if has(i, 3):
                        act_a(act, i + 3)

                for i in range(3):
                    act_a(act, i)
                act_square(act, 0, True)
                act_sd(act, 0, True)
                act_affine(act, 0)
                act_square(act, 1, False)
                with act.Fori(0, NBLK - 3) as i:
                    body(i)
                for i in range(NBLK - 3, NBLK):
                    body(i)

        with nc.Block() as block:
            group_norm(block, KN, "gn2")

        flat = lambda t: t[:, :, :].rearrange("p j n -> p (j n)")
        NXP = J * XW * W_
        XP = [flat(KP)[:, s * NXP:(s + 1) * NXP].rearrange("p (j r x) -> p j r x", j=J, x=W_)
              for s in range(2)]
        NG = NRB * RW * XW
        G = flat(QP)[:, 0:NG]
        STAGES = [(NRB, RW * XW, 2 * XW, (RW - 2) * XW), (NRB, (RW - 2) * XW, XW, KS * XW),
                  (NRB * KS, XW, 16, 20), (NRB * KS, 20, 8, 12), (NRB * KS, 12, 4, 8),
                  (NRB * KS, 8, 2, 6), (NRB * KS, 6, 1, KS)]
        carve = Carve()
        DST, SRC = [], [G.rearrange("p (r w) -> p r w", w=RW * XW)]
        at = [flat(QP), NG]
        for k, (r, w, _, kept) in enumerate(STAGES):
            n = r * kept
            if at[1] + n > J * NT:
                at = [flat(TT), 0]
            DST.append(at[0][:, at[1]:at[1] + n].rearrange("p (r w) -> p r w", w=kept))
            if k + 1 < len(STAGES):
                SRC.append(at[0][:, at[1]:at[1] + n].rearrange("p (r w) -> p r w", w=STAGES[k + 1][1]))
            at[1] += n
        TMP = [flat(X)[:, k * 2048:k * 2048 + r * kept].rearrange("p (r w) -> p r w", w=kept)
               for k, (r, w, _, kept) in zip((0, 1, 2, 0, 1, 2, 0), STAGES)]
        YB = [flat(TT)[:, 4096 + s * 2048:4096 + (s + 1) * 2048].rearrange("p (k n) -> p k n", k=PER * J)
              for s in range(2)]
        DN = carve(NRB, S)
        DSQ = carve(NRB, S)
        nrm = carve(NRB)
        DT = carve(N)
        wsw = carve(C)
        ov = out.rearrange("b (j p) n -> p j b n", p=P)

        with nc.Block() as block:
            (s_w2, s_pad, s_xg, s_gram, s_gs, s_tmp, s_st, s_dsq, s_dss, s_dsd, s_dr, s_dn, s_dt, s_dtc,
             s_conv, s_relu, s_y) = (
                sem(n) for n in ("w2", "pad", "xg", "gram", "gs", "btmp", "bstage", "dsq", "dss", "dsd", "dr",
                                 "dn", "dt", "dtc", "conv", "relu", "yfin"))
            s_out = [sem(f"out{s}") for s in range(2)]
            NS = len(STAGES)
            CV = PER * J

            @block.sync
            def _(sp):
                sp.dma_start(wsm[:, :, :], wx).then_inc(s_w2, 16)
                sp.dma_start(wsw[0:S, :], ws).then_inc(s_w2, 16)

                def store(b, p, h):
                    sp.wait_ge(s_y, b * CV + (h + 1) * J)
                    for o in range(J):
                        sp.dma_start(ov[:, o, ds(b, 1), h * BLK:(h + 1) * BLK].rearrange("p b n -> p (b n)"),
                                     YB[p][:, h * J + o, :]).then_inc(s_out[p], 16)
                with sp.Fori(0, B // 2) as pair:
                    b = pair * 2
                    for p in range(2):
                        for h in range(PER):
                            store(b + p, p, h)
                for p in range(2):
                    sp.wait_ge(s_out[p], 16 * CV * B // 2)

            @block.gpsimd
            def _(pool):
                for p in range(2):
                    nc.gpsimd.memset(XP[p][:, :, 0:PAD, :], 0.0)
                    nc.gpsimd.memset(XP[p][:, :, XW - PAD:XW, :], 0.0)
                g3 = G.rearrange("p (r x) -> p r x", x=XW)
                nc.gpsimd.memset(g3[:, :, 0:PAD], 0.0)
                nc.gpsimd.memset(g3[:, :, XW - PAD:XW], 0.0).then_inc(s_pad, 1)

                def fin(b, p, k):
                    h, o = divmod(k, J)
                    pool.wait_ge(s_relu, b * CV + k + 1)
                    nc.gpsimd.tensor_tensor(YB[p][:, k, :], YB[p][:, k, :],
                                            KN[:, o, ds(b * N + h * BLK, BLK)], ALU.add).then_inc(s_y, 1)
                with pool.Fori(0, B // 2) as pair:
                    b = pair * 2
                    for p in range(2):
                        for k in range(CV):
                            fin(b + p, p, k)

            @block.tensor
            def _(pe):
                pe.wait_ge(s_w2, 32)
                pe.wait_ge(s_pad, 1)

                def gram(b, p, first):
                    pe.wait_ge(s_xg, b * J + J)
                    for rb in range(NRB):
                        if not (first and rb < 4):
                            pe.wait_ge(s_gs, b * NRB + rb - 3)
                        for j in range(J):
                            mm = nc.tensor.matmul(
                                PS[:, rb % 4, 0:RW * W_],
                                XP[p][:, j, PAD + RB * rb:PAD + RB * rb + RB, :].rearrange("p r x -> p (r x)"),
                                XP[p][:, j, RB * rb:RB * rb + RW, :].rearrange("p r x -> p (r x)"),
                                start=(j == 0), stop=(j == J - 1))
                        mm.then_inc(s_gram, 1)

                def conv(b, p, first):
                    pe.wait_ge(s_dn, b + 1)
                    if not first:
                        pe.wait_ge(s_dtc, b * 2)
                    for rb in range(NRB):
                        tr = nc.tensor.transpose(PS[0:S, 4 + rb // 4, (rb % 4) * P:(rb % 4 + 1) * P],
                                                 DN[:, rb, :], ident)
                    tr.then_inc(s_dt, 1)
                    pe.wait_ge(s_dtc, b * 2 + 2)
                    for k in range(CV):
                        h, o = divmod(k, J)
                        if not (first and k < 2):
                            pe.wait_ge(s_relu, b * CV + k - 1)
                        bank = 6 + k % 2
                        for j in range(J):
                            nc.tensor.matmul(PS[:, bank, :], wsm[:, j, o * P:(o + 1) * P],
                                             XP[p][:, j, PAD + 16 * h:PAD + 16 * h + 16, :].rearrange(
                                                 "p r x -> p (r x)"), start=(j == 0), stop=False)
                        nc.tensor.matmul(PS[:, bank, :], wsw[0:S, o * P:(o + 1) * P],
                                         DT[0:S, h * BLK:(h + 1) * BLK], start=False, stop=True
                                         ).then_inc(s_conv, 1)

                gram(0, 0, True)
                gram(1, 1, False)
                conv(0, 0, True)
                for b in range(2, B):
                    gram(b, b % 2, False)
                    conv(b - 1, (b - 1) % 2, False)
                conv(B - 1, 1, False)

            @block.vector
            def _(dve):
                def body(b, first):
                    for k, (r, w, sh, kept) in enumerate(STAGES):
                        dve.wait_ge(s_tmp, b * NS + k + 1)
                        nc.vector.scalar_tensor_tensor(DST[k], SRC[k][:, :, 0:kept], ccol("shift_off", k, 1),
                                                       TMP[k], ALU.mult, ALU.add).then_inc(s_st, 1)
                    dve.wait_ge(s_st, b * NS + NS)
                    D = DST[-1].rearrange("p (a r) w -> p a (r w)", r=KS)
                    nc.vector.tensor_tensor(DSQ, D, D, ALU.mult).then_inc(s_dsq, 1)
                    dve.wait_ge(s_dsq, b + 1)
                    nc.vector.tensor_reduce(nrm, DSQ, AX.X, ALU.add).then_inc(s_dss, 1)
                    dve.wait_ge(s_dsd, b + 1)
                    nc.vector.reciprocal(nrm, nrm).then_inc(s_dr, 1)
                    dve.wait_ge(s_dr, b + 1)
                    if not first:
                        dve.wait_ge(s_dt, b + 0)
                    nc.vector.tensor_tensor(DN, D, nrm.unsqueeze(2).broadcast_to([P, NRB, S]), ALU.mult
                                            ).then_inc(s_dn, 1)

                body(0, True)
                with dve.Fori(1, B) as b:
                    body(b, False)

            @block.scalar
            def _(act):
                def scale(b, p, first):
                    if not first:
                        act.wait_ge(s_conv, (b - 1) * CV)
                    for j in range(J):
                        nc.scalar.activation(
                            XP[p][:, j, PAD:PAD + H, :].rearrange("p r x -> p (r x)"), KN[:, j, ds(b * N, N)],
                            ACT.Identity, scale=gn_a[:, ds(b * J + j, 1)], bias=gn_c[:, ds(b * J + j, 1)]
                        ).then_inc(s_xg, 1)

                def evacuate(b, first):
                    if not first:
                        act.wait_ge(s_st, (b - 1) * NS + 1)
                    for rb in range(NRB):
                        act.wait_ge(s_gram, b * NRB + rb + 1)
                        nc.scalar.activation(
                            G.rearrange("p (a r x) -> p a r x", a=NRB, x=XW)[:, rb, :, PAD:PAD + W_],
                            PS[:, rb % 4, 0:RW * W_].rearrange("p (r x) -> p r x", x=W_), ACT.Copy
                        ).then_inc(s_gs, 1)

                def stages(b):
                    for k, (r, w, sh, kept) in enumerate(STAGES):
                        if k == 0:
                            act.wait_ge(s_gs, b * NRB + NRB)
                        else:
                            act.wait_ge(s_st, b * NS + k)
                        nc.scalar.activation(TMP[k], SRC[k][:, :, sh:sh + kept], ACT.Copy,
                                             scale=ccol("shift_on", k, 1)).then_inc(s_tmp, 1)
                    act.wait_ge(s_dss, b + 1)
                    nc.scalar.activation(nrm, nrm, ACT.Sqrt, bias=eps6).then_inc(s_dsd, 1)

                def dt_copy(b, first):
                    act.wait_ge(s_dt, b + 1)
                    if not first:
                        act.wait_ge(s_conv, b * CV)
                    for h in range(2):
                        nc.scalar.activation(DT[0:S, h * BLK:(h + 1) * BLK], PS[0:S, 4 + h, :], ACT.Copy
                                             ).then_inc(s_dtc, 1)

                def relu(b, p, first):
                    if not first:
                        act.wait_ge(s_out[p], (b - p) * (CV * 8))
                    for k in range(CV):
                        h, o = divmod(k, J)
                        act.wait_ge(s_conv, b * CV + k + 1)
                        nc.scalar.activation(YB[p][:, k, :], PS[:, 6 + k % 2, :], ACT.Relu,
                                             bias=pcol("conv_b", o)).then_inc(s_relu, 1)

                scale(0, 0, True)
                evacuate(0, True)
                scale(1, 1, True)
                stages(0)
                evacuate(1, False)
                dt_copy(0, True)
                relu(0, 0, True)
                for b in range(2, B):
                    scale(b, b % 2, False)
                    stages(b - 1)
                    evacuate(b, False)
                    dt_copy(b - 1, False)
                    relu(b - 1, (b - 1) % 2, b == 2)
                stages(B - 1)
                dt_copy(B - 1, False)
                relu(B - 1, 1, False)


def constants():
    p = np.arange(P)
    row_e, row_t, row_head = (p // CS) % E, p % CS, 4 * ((p // CS) % E) + p // HD
    c = {}
    c["ident"] = np.eye(P)
    c["center_h"] = np.eye(P) - (p[:, None] // HD == p[None, :] // HD) / HD
    c["mean_c"] = np.full((P, P), 1.0 / C)
    c["mean_g"] = (p[:, None] // GROUP == p[None, :] // GROUP) / GROUP
    c["chunk_ones"] = p[:, None] // CS == p[None, :] // CS
    c["emask"] = row_e[:, None] == np.arange(E)
    c["emask_k"] = ((p // HD) % E)[:, None] == np.arange(E)
    col_e, col_t = np.divmod(np.arange(E * CS), CS)
    c["causal"] = (row_e[:, None] == col_e) & (row_t[:, None] <= col_t)
    c["headmask"] = (row_head[:, None] == np.arange(NH)) / HD
    c["inv_t"] = np.broadcast_to((1.0 / np.arange(1, CS + 1, dtype=np.float32)), (P, CS))
    r, xx = np.divmod(p, W_)
    bits = np.stack([(r >> 1) & 1, r & 1] + [(xx >> k) & 1 for k in (4, 3, 2, 1, 0)], 1)
    c["shift_on"], c["shift_off"] = bits, 1 - bits
    c["spread"] = np.concatenate([p[:, None] == n * CS + row_t[None, :] for n in range(8)], 1)
    table = np.concatenate([np.asarray(c[k], np.float32).reshape(P, w) for k, w in CONST.items()], 1)
    inv = (1.0 / 10000.0 ** (np.arange(0, HD, 2, dtype=np.float32) / np.float32(HD))).astype(np.float32)
    angle = np.arange(N, dtype=np.float32)[None, :] * inv[:, None]
    cos, sin = np.cos(angle), np.sin(angle)
    rope = np.stack([np.tile(np.concatenate([cos, cos]), (P // HD, 1)),
                     np.tile(np.concatenate([-sin, sin]), (P // HD, 1))], 1)
    return np.ascontiguousarray(table), np.ascontiguousarray(rope.astype(np.float32))


def kernel(x, L0_conv_ln_w, L0_conv_ln_b, L0_conv_q_w, L0_conv_k_w, L0_conv_v_w, L0_conv_o_w, L0_conv_W1,
           L0_conv_b1, L0_conv_ttt_ln_w, L0_conv_ttt_ln_b, L0_conv_lr_w, L0_conv_lr_b,
           L0_conv_tok_idx_delta, L0_conv_post_w, L0_conv_post_b, L1_conv_W, L1_conv_bias):
    import concourse.bacc as bacc
    from concourse.bass_utils import run_bass_kernel_spmd

    a = np.asarray
    paired = [4 * e + 2 * k + a2 for k in range(J) for a2 in range(2) for e in range(E)]
    rows = [4 * e + g for g in range(4) for e in range(E)]

    def stationary(w):
        return np.ascontiguousarray(a(w).T.reshape(J, P, -1).transpose(1, 0, 2))

    def by_head(w):
        return a(w).reshape(NH, HD, C)[paired].reshape(C, C)

    def channels(v):
        return a(v).reshape(J, P).T

    pars = dict(
        ln_w=channels(L0_conv_ln_w), ln_b=channels(L0_conv_ln_b), post_w=channels(L0_conv_post_w),
        post_b=channels(L0_conv_post_b), conv_b=channels(L1_conv_bias),
        g=channels(a(L0_conv_ttt_ln_w).reshape(C)), bb=channels(a(L0_conv_ttt_ln_b).reshape(C)),
        g_row=np.repeat(a(L0_conv_ttt_ln_w)[rows], CS, 0),
        b1_row=np.repeat(a(L0_conv_b1).reshape(NH, HD)[rows], CS, 0),
        delta=np.tile(a(L0_conv_tok_idx_delta)[None], (P, 1)),
        lr_b=np.tile(a(L0_conv_lr_b).reshape(NH, 1), (P // NH, 1)),
        w1=a(L0_conv_W1)[paired].reshape(J, P, HD).transpose(1, 0, 2).reshape(P, J * HD),
    )
    table, rope = constants()
    arrays = dict(
        x=np.ascontiguousarray(a(x).reshape(B, C, N)),
        wq=stationary(by_head(L0_conv_q_w)), wk=stationary(by_head(L0_conv_k_w)),
        wv=stationary(L0_conv_v_w), wo=stationary(L0_conv_o_w),
        wlr=stationary(a(L0_conv_lr_w).reshape(NH, C)),
        wx=stationary(a(L1_conv_W)[:, :C]), ws=np.ascontiguousarray(a(L1_conv_W)[:, C:].T),
        params=np.ascontiguousarray(np.concatenate([pars[k] for k in PARAM], 1)),
        consts=table, rope=rope)

    nc = bacc.Bacc("TRN2", target_bir_lowering=False, num_devices=1)
    order = ["x", "wq", "wk", "wv", "wo", "wlr", "wx", "ws", "params", "consts", "rope"]
    aps = {k: nc.dram_tensor(f"in_{k}", arrays[k].shape, F32, kind="ExternalInput").ap() for k in order}
    o = nc.dram_tensor("out_0", (B, C, N), F32, kind="ExternalOutput").ap()
    build(nc, aps["x"], o, aps["wq"], aps["wk"], aps["wv"], aps["wo"], aps["wlr"], aps["wx"], aps["ws"],
          aps["params"], aps["consts"], aps["rope"])
    r = run_bass_kernel_spmd(nc, [{f"in_{k}": arrays[k] for k in order}], core_ids=[0])
    return r.results[0]["out_0"].reshape(B, C, H, W_)
```

```python
from contextlib import ExitStack

import numpy as np

import concourse.bass as bass
from concourse import mybir

F32 = mybir.dt.float32
ALU = mybir.AluOpType
ACT = mybir.ActivationFunctionType
AX = mybir.AxisListType
ds = bass.ds

P = 128
B, C, H, W_ = 4, 256, 32, 32
N = H * W_
NT = B * N
J = C // P
NH, HD, CS = 8, 32, 16
NC = N // CS
E = 2
BLK = 512
NBLK = NT // BLK
PER = N // BLK
GROUP = 8
KS = 5
S = KS * KS
PAD = KS // 2
RB = 4
NRB = H // RB
RW = RB + 2 * PAD
XW = W_ + 2 * PAD

EPS_GN, EPS_LN, EPS_IN, EPS_NORM = 1e-5, 1e-5, 1e-6, 1e-6

CONST = dict(ident=P, mean_c=P, mean_g=P, chunk_ones=P, emask=E, emask_k=E, causal=E * CS, inv_t=CS,
             shift_on=7, shift_off=7, spread=8 * E * HD)
PARAM = dict(ln_w=J, ln_b=J, post_w=J, post_b=J, conv_b=J, g=E, bb=E, g_row=HD, b1_row=HD,
             delta=CS, lr_b=1, w1=J * HD)


def columns(widths):
    at, out = 0, {}
    for name, w in widths.items():
        out[name] = (at, w)
        at += w
    return out, at


CONST_AT, NCONST = columns(CONST)
PARAM_AT, NPARAM = columns(PARAM)


def build(nc, x, out, wq, wk, wv, wo, wlr, wx, ws, params, consts, rope):
    ctx = ExitStack()
    with ctx:
        def sb(name, shape):
            return ctx.enter_context(nc.sbuf_tensor(name, shape, F32))

        def sem(name):
            return ctx.enter_context(nc.semaphore(name))

        X = sb("X", [P, J, NT])
        KP = sb("KP", [P, J, NT])
        QP = sb("QP", [P, J, NT])
        KN = sb("KN", [P, J, NT])
        TT = sb("TT", [P, J, NT])
        par = sb("par", [P, NPARAM])
        small = sb("small", [P, 512])
        lrh = sb("lrh", [P, NC, B])
        wsm = sb("wsm", [P, J, C])
        work = sb("work", [P, 7712])

        def pcol(name, i=0, n=1, rows=P):
            at = PARAM_AT[name][0] + i
            return par[0:rows, at:at + n]

        used = [0]

        def scol(n):
            used[0] += n
            assert used[0] <= 512
            return small[:, used[0] - n:used[0]]

        gn_a, gn_c = scol(B * J), scol(B * J)
        eps5, eps6 = scol(1), scol(1)
        neg_g, bbg = scol(E), scol(E)
        g2row = scol(HD)
        amask = scol(E * CS)
        upd_mask = scol(E)
        w0 = scol(J * HD)
        b0 = scol(HD)
        stat = scol(J * B * 2 * 6)
        mv = scol(J * B * 2)
        gm = scol(J * B * 2)
        gdev = scol(J * B)
        tok = scol(CS)
        one = scol(1)
        sqrt_warm = scol(1)

        counts = []

        def value(eng, v):
            if isinstance(v, int):
                return v
            r = eng.alloc_register(f"count{len(counts)}")
            counts.append(r)
            eng.reg_mov(r, v)
            return eng.snap(r, min_val=1, max_val=1 << 12)

        class Carve:
            def __init__(self):
                self.at = 0

            def __call__(self, *dims):
                n = int(np.prod(dims))
                v = work[:, self.at:self.at + n]
                self.at += n
                assert self.at <= work.shape[1], self.at
                if len(dims) == 1:
                    return v
                names = "abcdef"[:len(dims)]
                return v.rearrange(f"p ({' '.join(names)}) -> p {' '.join(names)}",
                                   **dict(zip(names, dims)))

        PS = ctx.enter_context(nc.psum_tensor("PS", [P, 8, BLK], F32))

        cst = sb("cst", [P, NCONST])
        ones_blk = sb("ones_blk", [P, P])
        mask2 = sb("mask2", [P, B * 2 * E * CS])

        def ccol(name, i=0, n=None, rows=P):
            at, w = CONST_AT[name]
            n = w - i if n is None else n
            return cst[0:rows, at + i:at + i + n]

        ident, mean_c, mean_g = ccol("ident"), ccol("mean_c"), ccol("mean_g")

        def group_norm(block, src, tag, extra_vector=None, extra_loads=None, have_stats=False):
            s_bn, s_mv, s_g1, s_gc, s_dev, s_g2, s_var, s_sd, s_r, s_a = (
                sem(f"{tag}_{n}") for n in ("bn", "mv", "g1", "gc", "dev", "g2", "var", "sd", "r", "a"))
            s_in = [sem(f"{tag}_in{b}") for b in range(B)]
            s_par = sem(f"{tag}_par")
            st = stat.rearrange("p (b h j s) -> p b h j s", b=B, h=PER, s=6)

            @block.sync
            def _(sp):
                if extra_loads:
                    extra_loads(sp, s_in, s_par)

            @block.vector
            def _(dve):
                for b in range(0 if have_stats else B):
                    for j in range(J):
                        if extra_loads:
                            dve.wait_ge(s_in[b], 16)
                        for h in range(PER):
                            nc.vector.bn_stats(
                                st[:, b, h, j, :],
                                src[:, j, b * N + h * BLK:b * N + (h + 1) * BLK]).then_inc(s_bn, 1)
                    if b == 0 and extra_vector:
                        extra_vector(dve, s_par)
                if not have_stats:
                    dve.wait_ge(s_bn, B * J * PER)
                for k in range(B * J):
                    nc.vector.bn_aggr(mv[:, 2 * k:2 * k + 2], st[:, k // J, :, k % J, :]).then_inc(s_mv, 1)
                dve.wait_ge(s_g1, 1)
                nc.vector.tensor_copy(gm, PS[:, 0, 0:2 * B * J]).then_inc(s_gc, 1)
                dve.wait_ge(s_gc, 1)
                dve.wait_ge(s_mv, B * J)
                m2 = mv.rearrange("p (k t) -> p k t", t=2)
                g2 = gm.rearrange("p (k t) -> p k t", t=2)
                nc.vector.tensor_tensor(gdev, m2[:, :, 0], g2[:, :, 0], ALU.subtract).then_inc(s_dev, 1)
                dve.wait_ge(s_dev, 1)
                nc.vector.tensor_tensor(gdev, gdev, gdev, ALU.mult).then_inc(s_dev, 1)
                dve.wait_ge(s_g2, 1)
                nc.vector.tensor_tensor(gdev, PS[:, 1, 0:B * J], g2[:, :, 1], ALU.add).then_inc(s_var, 1)
                dve.wait_ge(s_sd, 1)
                nc.vector.reciprocal(gn_a, gn_a).then_inc(s_r, 1)
                dve.wait_ge(s_r, 1)
                nc.vector.scalar_tensor_tensor(gn_c, g2[:, :, 0], -1.0, gn_a, ALU.mult, ALU.mult
                                               ).then_inc(s_a, 1)

            @block.tensor
            def _(pe):
                if extra_loads:
                    pe.wait_ge(s_par, 32)
                pe.wait_ge(s_mv, B * J)
                nc.tensor.matmul(PS[:, 0, 0:2 * B * J], mean_g, mv, start=True, stop=True).then_inc(s_g1, 1)
                pe.wait_ge(s_dev, 2)
                nc.tensor.matmul(PS[:, 1, 0:B * J], mean_g, gdev, start=True, stop=True).then_inc(s_g2, 1)

            @block.scalar
            def _(act):
                if extra_loads:
                    act.wait_ge(s_k0, 3)
                    nc.scalar.activation(sqrt_warm, eps5, ACT.Sqrt)
                act.wait_ge(s_var, 1)
                nc.scalar.activation(gn_a, gdev, ACT.Sqrt, bias=eps5).then_inc(s_sd, 1)

        xv = x.rearrange("b (j p) n -> p j b n", p=P)
        carve = Carve()
        cosT, sinT = carve(N), carve(N)
        sq = carve(J, BLK)
        sd = carve(BLK)
        kc, ksw = carve(2, BLK), carve(2, BLK)
        wkv = carve(J, 2 * C)
        wl = carve(J, NH)
        sum_x, sum_sq = carve(BLK), carve(BLK)
        wvw = wsm
        lrt = sb("lrt", [P, 8 * B * NH])
        s_k0 = sem("s_k0")
        s_w, s_rt, s_sp2 = sem("s_w"), sem("ropetab"), sem("spread_table")

        FIRST = CONST_AT["spread"][0]

        def first_loads(sp, s_in, s_par):
            sp.dma_start(X[:, :, 0:N], xv[:, :, 0, :]).then_inc(s_in[0], 16)
            sp.dma_start(par[:, :], params).then_inc(s_par, 16)
            sp.dma_start(cst[:, 0:FIRST], consts[:, 0:FIRST]).then_inc(s_par, 16)
            for b in range(1, B):
                sp.dma_start(X[:, :, b * N:(b + 1) * N], xv[:, :, b, :]).then_inc(s_in[b], 16)
            sp.dma_start(wkv[:, :, 0:C], wk).then_inc(s_w, 16)
            sp.dma_start(wkv[:, :, C:2 * C], wq).then_inc(s_w, 16)
            sp.dma_start(wvw[:, :, :], wv).then_inc(s_w, 16)
            sp.dma_start(wl, wlr).then_inc(s_w, 16)
            sp.dma_start(cosT, rope[:, 0, :]).then_inc(s_rt, 16)
            sp.dma_start(sinT, rope[:, 1, :]).then_inc(s_rt, 16)
            sp.dma_start(cst[:, FIRST:], consts[:, FIRST:]).then_inc(s_sp2, 16)

        with nc.Block() as block:
            s_d = sem("derive")

            def derive(dve, s_par):
                n = [0]

                def link(ins):
                    n[0] += 1
                    ins.then_inc(s_d, 1)
                    dve.wait_ge(s_d, n[0])

                dve.wait_ge(s_par, 32)
                nc.vector.tensor_scalar(neg_g, pcol("g", 0, E), -1.0, None, ALU.mult).then_inc(s_d, 1)
                nc.vector.tensor_tensor(bbg, pcol("bb", 0, E), pcol("g", 0, E), ALU.mult).then_inc(s_d, 1)
                nc.vector.tensor_tensor(g2row, pcol("g_row", 0, HD), pcol("g_row", 0, HD), ALU.mult
                                        ).then_inc(s_d, 1)
                n[0] = 3
                link(nc.vector.tensor_tensor(tok, ccol("inv_t"), pcol("delta", 0, CS), ALU.add))
                link(nc.vector.tensor_scalar(tok, tok, 0.0, None, ALU.max))
                link(nc.vector.tensor_tensor(
                    amask.rearrange("p (e t) -> p e t", e=E),
                    ccol("causal").rearrange("p (e t) -> p e t", e=E),
                    tok.unsqueeze(1).broadcast_to([P, E, CS]), ALU.mult))
                link(nc.vector.tensor_scalar(amask, amask, -1.0, None, ALU.mult))
                link(nc.vector.tensor_scalar(upd_mask, ccol("emask"), tok[:, CS - 1:CS], -1.0,
                                             ALU.mult, ALU.mult))
                link(nc.vector.tensor_scalar(ones_blk[:, :], ccol("chunk_ones"), tok[:, CS - 1:CS], -1.0,
                                             ALU.mult, ALU.mult))
                w1 = pcol("w1", 0, J * HD).rearrange("p (j d) -> p j d", d=HD)
                link(nc.vector.tensor_reduce(gdev[:, 0:J], w1, AX.X, ALU.add))
                link(nc.vector.tensor_reduce(gdev[:, J:J + 1], pcol("b1_row", 0, HD), AX.X, ALU.add))
                link(nc.vector.scalar_tensor_tensor(
                    w0.rearrange("p (j d) -> p j d", d=HD),
                    gdev[:, 0:J].unsqueeze(2).broadcast_to([P, J, HD]), -1.0 / HD, w1, ALU.mult, ALU.add))
                link(nc.vector.scalar_tensor_tensor(
                    b0, gdev[:, J:J + 1].broadcast_to([P, HD]), -1.0 / HD, pcol("b1_row", 0, HD),
                    ALU.mult, ALU.add))

            @block.gpsimd
            def _(pool):
                pool.memset(eps5, EPS_GN).then_inc(s_k0, 1)
                pool.memset(eps6, EPS_IN).then_inc(s_k0, 1)
                pool.memset(one, 1.0).then_inc(s_k0, 1)

            group_norm(block, X, "gn1", derive, first_loads)

        swap = [(i + HD // 2) % HD for i in range(HD)]

        def blk_of(t, i):
            return t[:, ds(i * BLK, BLK)]

        def has(i, n):
            return not isinstance(i, int) or i + n < NBLK

        def layer_norm(tag, src, sq, sd, eps, w, b, scale, ready=None, sums=None):
            q = {n: sem(f"{tag}_{n}") for n in ("in", "mean", "xc", "sq", "var", "sd", "rs", "xh", "xn", "add",
                                               "addsq")}

            def tile(i, j):
                return src[:, j, ds(i * BLK, BLK)]

            def act_a(act, i):
                for j in range(J):
                    scale(act, i, j).then_inc(q["in"], 1)

            def pool_sum(pool, i, first):
                mean, there = value(pool, i + 0), value(pool, i * J + J)
                pool.wait_ge(s_k0, 2)
                pool.wait_ge(q["in"], there)
                if not first:
                    pool.wait_ge(q["mean"], mean)
                nc.gpsimd.tensor_tensor(sums[0], tile(i, 0), tile(i, 1), ALU.add).then_inc(q["add"], 1)

            def pool_sum_squares(pool, i, first):
                var, there = value(pool, i + 0), value(pool, i * J + J)
                pool.wait_ge(s_k0, 2)
                pool.wait_ge(q["sq"], there)
                if not first:
                    pool.wait_ge(q["var"], var)
                nc.gpsimd.tensor_tensor(sums[1], sq[:, 0, :], sq[:, 1, :], ALU.add).then_inc(q["addsq"], 1)

            def pe_mean(pe, i, first):
                if not first:
                    pe.wait_ge(q["xc"], i * J)
                if sums:
                    pe.wait_ge(q["add"], i + 1)
                    nc.tensor.matmul(PS[:, 0, :], mean_c, sums[0], start=True, stop=True
                                     ).then_inc(q["mean"], 1)
                    return
                pe.wait_ge(ready or q["in"], i * J + J)
                for j in range(J):
                    m = nc.tensor.matmul(PS[:, 0, :], mean_c, tile(i, j), start=(j == 0), stop=(j == J - 1))
                m.then_inc(q["mean"], 1)

            def dve_center(dve, i):
                dve.wait_ge(q["mean"], i + 1)
                for j in range(J):
                    nc.vector.tensor_tensor(tile(i, j), tile(i, j), PS[:, 0, :], ALU.subtract
                                            ).then_inc(q["xc"], 1)

            def act_square(act, i, first):
                if not first:
                    act.wait_ge(q["addsq" if sums else "var"], i + 0)
                for j in range(J):
                    act.wait_ge(s_k0, 2)
                    act.wait_ge(q["xc"], i * J + j + 1)
                    nc.scalar.activation(sq[:, j, :], tile(i, j), ACT.Square).then_inc(q["sq"], 1)

            def pe_var(pe, i, first):
                if not first:
                    pe.wait_ge(q["sd"], i + 0)
                if sums:
                    pe.wait_ge(q["addsq"], i + 1)
                    nc.tensor.matmul(PS[:, 1, :], mean_c, sums[1], start=True, stop=True
                                     ).then_inc(q["var"], 1)
                    return
                pe.wait_ge(q["sq"], i * J + J)
                for j in range(J):
                    m = nc.tensor.matmul(PS[:, 1, :], mean_c, sq[:, j, :], start=(j == 0), stop=(j == J - 1))
                m.then_inc(q["var"], 1)

            def act_sd(act, i, first):
                act.wait_ge(q["var"], i + 1)
                if not first:
                    act.wait_ge(q["xh"], i * J)
                nc.scalar.activation(sd, PS[:, 1, :], ACT.Sqrt, bias=eps).then_inc(q["sd"], 1)

            def dve_scale(dve, i):
                dve.wait_ge(q["sd"], i + 1)
                nc.vector.reciprocal(sd, sd).then_inc(q["rs"], 1)
                dve.wait_ge(q["rs"], i + 1)
                for j in range(J):
                    nc.vector.tensor_tensor(tile(i, j), tile(i, j), sd, ALU.mult).then_inc(q["xh"], 1)

            def act_affine(act, i):
                for j in range(J):
                    act.wait_ge(s_k0, 2)
                    act.wait_ge(q["xh"], i * J + j + 1)
                    nc.scalar.activation(tile(i, j), tile(i, j), ACT.Identity, scale=pcol(w, j),
                                         bias=pcol(b, j)).then_inc(q["xn"], 1)

            return q, tile, act_a, pe_mean, dve_center, act_square, pe_var, act_sd, dve_scale, act_affine, \
                pool_sum, pool_sum_squares

        ga8 = sb("ga8", [P, 2, J, NBLK])

        def spread_gn(dve, s):
            for k, src in enumerate((gn_a, gn_c)):
                for j in range(J):
                    nc.vector.tensor_copy(
                        ga8[:, k, j, :].rearrange("p (b h) -> p b h", h=PER),
                        src.rearrange("p (b j) -> p b j", j=J)[:, :, j].unsqueeze(2).broadcast_to([P, B, PER])
                    ).then_inc(s, 1)

        s_sp, s_qperm = sem("gn_spread"), sem("qperm")
        with nc.Block() as block:
            q1, xt, act_a, pe_mean, dve_center, act_square, pe_var, act_sd, dve_scale, act_affine, pool_sum, \
                pool_sum_squares = \
                layer_norm("ln1", X, sq, sd, eps5, "ln_w", "ln_b",
                           lambda act, i, j: nc.scalar.activation(
                               X[:, j, ds(i * BLK, BLK)], X[:, j, ds(i * BLK, BLK)], ACT.Identity,
                               scale=ga8[:, 0, j, ds(i, 1)], bias=ga8[:, 1, j, ds(i, 1)]),
                           sums=(sum_x, sum_sq))
            s_proj, s_kc, s_ksw, s_ksin, s_rope, s_tt, s_lr, s_kperm, s_ttf, s_tr, s_sig, s_spread, s_lrh = (
                sem(n) for n in ("proj", "kc", "ksw", "ksin", "rope", "tt", "lr", "kperm", "ttf", "lr_tr", "sig",
                                 "lr_spread", "lr_h"))
            NPJ = 7

            @block.sync
            def _(sp):

                def permute(i, first):
                    if not first:
                        sp.wait_ge(s_kperm, i * 128)
                    sp.wait_ge(s_rope, i * 2 * J + J)
                    for k in range(J):
                        for a2 in range(2):
                            for e in range(E):
                                a = 2 * k + a2
                                r = 2 * HD * a2 + HD * e
                                sp.dma_start(KN[HD * a:HD * a + HD, e, ds(i * BLK, BLK)],
                                             KP[r:r + HD, k, ds(i * BLK, BLK)]).then_inc(s_kperm, 16)
                permute(0, True)
                with sp.Fori(1, NBLK) as i:
                    permute(i, False)
                sp.wait_ge(s_kperm, NBLK * 128)
                sp.wait_ge(s_sp2, 16)

            @block.tensor
            def _(pe):
                pe.wait_ge(s_w, 64)

                def proj(i, m, first):
                    if m < 2 * J:
                        lhs = lambda j: wkv[:, j, m * P:(m + 1) * P]
                    elif m < 3 * J:
                        lhs = lambda j: wvw[:, j, (m - 2 * J) * P:(m - 2 * J + 1) * P]
                    else:
                        lhs = lambda j: wl[:, j, :]
                    if m == NPJ - 1:
                        first_tile = value(pe, i * (2 * J) + 1)
                        pe.wait_ge(s_w, 64)
                        pe.wait_ge(s_ksw, first_tile)
                        o = PS[0:NH, 2, :]
                    else:
                        o = PS[:, 2 + m, :]
                        if not first:
                            if m < 2 * J:
                                pe.wait_ge(s_ksw, (i - 1) * (2 * J) + m + 1)
                            else:
                                pe.wait_ge(s_tt, (i - 1) * J + m - 2 * J + 1)
                            if m == 0:
                                pe.wait_ge(s_lr, i + 0)
                    for j in range(J):
                        mm = nc.tensor.matmul(o, lhs(j), xt(i, j), start=(j == 0), stop=(j == J - 1))
                    mm.then_inc(s_proj, 1)

                def body(i, first):
                    if has(i, 2):
                        pe_mean(pe, i + 2, False)
                    if has(i, 1):
                        pe_var(pe, i + 1, False)
                    pe.wait_ge(q1["xn"], i * J + J)
                    for m in range(NPJ):
                        proj(i, m, first)

                pe_mean(pe, 0, True)
                pe_mean(pe, 1, False)
                pe_var(pe, 0, True)
                body(0, True)
                with pe.Fori(1, NBLK - 2) as i:
                    body(i, False)
                body(NBLK - 2, False)
                body(NBLK - 1, False)
                pe.wait_ge(s_lr, NBLK)
                pe.wait_ge(q1["sd"], NBLK)
                for b in range(B):
                    for s in range(8):
                        tr = nc.tensor.transpose(PS[:, 1, (s * B + b) * NH:(s * B + b + 1) * NH],
                                                 X[0:NH, 0, b * N + s * P:b * N + (s + 1) * P],
                                                 ident[0:NH, 0:NH])
                tr.then_inc(s_tr, 1)
                pe.wait_ge(s_sig, 1)
                pe.wait_ge(s_sp2, 16)
                pe.wait_ge(q1["xc"], NBLK * J)
                for n in range(8):
                    for e in range(E):
                        for a in range(4):
                            mm = nc.tensor.matmul(
                                PS[HD * a:HD * a + HD, 0, n * 8 * B:(n + 1) * 8 * B],
                                ccol("spread", (n * E + e) * HD, HD),
                                lrt.rearrange("p (k h) -> p k h", h=NH)[:, :, 4 * e + a],
                                start=(e == 0), stop=(e == E - 1))
                mm.then_inc(s_spread, 1)

            @block.vector
            def _(dve):
                def rope_in(i, m, first):
                    t = m % 2
                    dve.wait_ge(s_proj, i * NPJ + m + 1)
                    if not (first and m < 2):
                        dve.wait_ge(s_rope, i * (2 * J) + m - 1)
                    h = ds((i % PER) * BLK, BLK)
                    nc.vector.tensor_tensor(kc[:, t, :], PS[:, 2 + m, :], cosT[:, h], ALU.mult).then_inc(s_kc, 1)
                    nc.vector.stream_shuffle(ksw[:, t, :], PS[:, 2 + m, :], swap).then_inc(s_ksw, 1)

                def finish_target(i):
                    dve.wait_ge(s_kperm, i * 128 + 128)
                    for j in range(J):
                        dve.wait_ge(s_tt, i * J + j + 1)
                        nc.vector.scalar_tensor_tensor(TT[:, j, ds(i * BLK, BLK)], KN[:, j, ds(i * BLK, BLK)],
                                                       pcol("g", j), TT[:, j, ds(i * BLK, BLK)],
                                                       ALU.mult, ALU.add).then_inc(s_ttf, 1)

                def body(i, first):
                    if has(i, 2):
                        dve_center(dve, i + 2)
                    if has(i, 1):
                        dve_scale(dve, i + 1)
                    for m in range(2 * J):
                        rope_in(i, m, first)
                    if not first:
                        finish_target(i - 1)

                spread_gn(dve, s_sp)
                m4 = mask2.rearrange("p (b s m) -> p b s m", b=B, s=2)
                nc.vector.tensor_copy(m4[:, :, 0, :], amask.unsqueeze(1).broadcast_to([P, B, E * CS]))
                nc.vector.tensor_copy(m4[:, :, 1, :].rearrange("p b (e t) -> p b e t", e=E),
                                      upd_mask.unsqueeze(1).unsqueeze(3).broadcast_to([P, B, E, CS]))
                dve.wait_ge(s_rt, 32)
                dve_center(dve, 0)
                dve_center(dve, 1)
                dve_scale(dve, 0)
                body(0, True)
                with dve.Fori(1, NBLK - 2) as i:
                    body(i, False)
                body(NBLK - 2, False)
                body(NBLK - 1, False)
                dve.wait_ge(s_spread, 1)
                nc.vector.tensor_copy(lrh.rearrange("p (s n) b -> p n s b", n=8),
                                      PS[:, 0, 0:8 * 8 * B].rearrange("p (n s b) -> p n s b", n=8, b=B)
                                      ).then_inc(s_lrh, 1)
                finish_target(NBLK - 1)

            @block.gpsimd
            def _(pool):
                def rope_out(i, m):
                    t = m % 2
                    dst = (KP if m < J else QP)[:, m % J, ds(i * BLK, BLK)]
                    h = ds((i % PER) * BLK, BLK)
                    done = value(pool, i * (2 * J) + (m + 1))
                    pool.wait_ge(s_rt, 32)
                    pool.wait_ge(s_ksw, done)
                    nc.gpsimd.tensor_tensor(ksw[:, t, :], ksw[:, t, :], sinT[:, h], ALU.mult).then_inc(s_ksin, 1)
                    pool.wait_ge(s_rt, 32)
                    pool.wait_ge(s_ksin, done)
                    nc.gpsimd.tensor_tensor(dst, ksw[:, t, :], kc[:, t, :], ALU.add).then_inc(s_rope, 1)

                def body(i):
                    if has(i, 3):
                        pool_sum(pool, i + 3, False)
                    if has(i, 2):
                        pool_sum_squares(pool, i + 2, False)
                    for m in range(2 * J):
                        rope_out(i, m)

                pool.wait_ge(s_rt, 32)
                pool_sum(pool, 0, True)
                pool_sum(pool, 1, False)
                pool_sum_squares(pool, 0, True)
                pool_sum(pool, 2, False)
                pool_sum_squares(pool, 1, False)
                with pool.Fori(0, NBLK - 3) as i:
                    body(i)
                for i in range(NBLK - 3, NBLK):
                    body(i)

            @block.scalar
            def _(act):
                def v_out(i, j):
                    act.wait_ge(s_proj, i * NPJ + 2 * J + j + 1)
                    nc.scalar.activation(TT[:, j, ds(i * BLK, BLK)], PS[:, 2 + 2 * J + j, :], ACT.Identity,
                                         scale=neg_g[:, j:j + 1], bias=bbg[:, j:j + 1]).then_inc(s_tt, 1)

                def lr_out(i):
                    act.wait_ge(s_proj, i * NPJ + NPJ)
                    nc.scalar.activation(X[0:NH, 0, ds(i * BLK, BLK)], PS[0:NH, 2, :], ACT.Identity,
                                         bias=pcol("lr_b", rows=NH)).then_inc(s_lr, 1)

                def body(i):
                    if has(i, 1):
                        act_sd(act, i + 1, False)
                    if has(i, 3):
                        act_a(act, i + 3)
                    if has(i, 2):
                        act_square(act, i + 2, False)
                    if has(i, 1):
                        act_affine(act, i + 1)
                    for j in range(J):
                        v_out(i, j)
                    lr_out(i)

                act.wait_ge(s_sp, 2 * J)
                act_a(act, 0)
                act_a(act, 1)
                act_square(act, 0, True)
                act_a(act, 2)
                act_sd(act, 0, True)
                act_square(act, 1, False)
                act_affine(act, 0)
                with act.Fori(0, NBLK - 3) as i:
                    body(i)
                for i in range(NBLK - 3, NBLK):
                    body(i)
                act.wait_ge(s_tr, 1)
                nc.scalar.activation(lrt[:, :], PS[:, 1, 0:8 * B * NH], ACT.Sigmoid).then_inc(s_sig, 1)

        carve = Carve()
        KT2 = [carve(J * B, E, CS) for _ in range(2)]
        QT2 = [carve(J * B, E, CS) for _ in range(2)]
        R = [carve(J, B, HD + 2 * CS) for _ in range(2)]
        TK = [carve(2, B, E, CS) for _ in range(2)]
        TKH = [carve(2, B, HD) for _ in range(2)]
        KHX = [carve(E, B, HD) for _ in range(2)]
        S1 = [carve(B * 2, CS) for _ in range(2)]
        AM = [carve(B, 2, E, CS) for _ in range(2)]
        Bs = [carve(B, HD) for _ in range(2)]
        ZP, XP = carve(2, B, HD), carve(2, B, HD)
        SQ, Y0, Y1, YL, WX = (carve(B, HD) for _ in range(5))
        GL = [carve(B, HD) for _ in range(2)]
        ZQ = [carve(B, HD) for _ in range(2)]
        SQQ, ZN, ZT = (carve(B, HD) for _ in range(3))
        sz = carve(2 * B)
        ss, ssq, rl, m2, m2r, sT = (carve(B) for _ in range(6))
        sds = carve(2 * B)
        sd1, sdq = sds[:, 0:B], sds[:, B:2 * B]

        def bc(v, n=HD):
            return v.unsqueeze(2).broadcast_to([P, v.shape[1], n])

        WB, BB, ZB, QB = 0, 2, (3, 4), (5, 6)
        ZW = HD + 2 * CS

        with nc.Block() as block:
            names = ("init wcopy bcopy kt2 qt2 qr kr stage tkh khx base qbase corr s1 am z p sq sz st tc zc ss sd "
                     "r xp y yl yp m mr w rl gl upd attn zq sqq ssq sdq rq zn zt ot").split()
            q = {n: sem(f"scan_{n}") for n in names}

            def chunk(t, c):
                return t.rearrange("p j (b n) -> p (j b) n", b=B)[:, :, ds(c * CS, CS)]

            def past(c, n):
                return c >= n if isinstance(c, int) else n <= 2

            def run_chunks(eng, body):
                body(0, 0)
                body(1, 1)
                with eng.Fori(1, NC // 2 - 2) as pair:
                    c = pair * 2
                    body(c, 0)
                    body(c + 1, 1)
                for c in range(NC - 4, NC):
                    body(c, c % 2)

            is_last = lambda c: isinstance(c, int) and c == NC - 1
            near_end = lambda c: isinstance(c, int) and c >= NC - 2

            @block.tensor
            def _(pe):
                for k in range(J):
                    nc.tensor.matmul(PS[:, WB + k, 0:B * HD].rearrange("p (b d) -> p b d", b=B), ident,
                                     w0[:, k * HD:(k + 1) * HD].unsqueeze(1).broadcast_to([P, B, HD]),
                                     start=True, stop=True, skip_group_check=True)
                nc.tensor.matmul(PS[:, BB, 0:B * HD].rearrange("p (b d) -> p b d", b=B), ident,
                                 b0.unsqueeze(1).broadcast_to([P, B, HD]), start=True, stop=True,
                                 skip_group_check=True).then_inc(q["init"], 1)

                def base(n, p, ready, state):
                    pe.wait_ge(q["init"], 1)
                    pe.wait_ge(q["kt2"], ready)
                    pe.wait_ge(q["qr"], ready)
                    pe.wait_ge(q["kr"], min(n + 1, NC - 1) if isinstance(n, int) else ready)
                    pe.wait_ge(q["wcopy"], state)
                    for b in range(B):
                        for k in range(J):
                            for a2 in range(2):
                                r, a = 2 * HD * a2, 2 * k + a2
                                mm = nc.tensor.matmul(
                                    PS[HD * a:HD * a + HD, ZB[p], b * ZW:b * ZW + ZW],
                                    KT2[p][r:r + 64, k * B + b, :, :].rearrange("p e t -> p (e t)"),
                                    R[p][r:r + 64, k, b, :], start=(b == 0), stop=False,
                                    skip_group_check=True)
                    mm.then_inc(q["base"], 1)

                def grads(width, bank, p, part):
                    for a in range(4):
                        for b in range(B):
                            mm = nc.tensor.matmul(PS[HD * a:HD * a + HD, bank, b * width:b * width + HD],
                                                  AM[p][HD * a:HD * a + HD, b, part, :, :].rearrange(
                                                      "p e t -> p (e t)"),
                                                  GL[p][HD * a:HD * a + HD, b, :],
                                                  start=False, stop=True, skip_group_check=True)
                    return mm

                def update(p):
                    for k in range(J):
                        for a2 in range(2):
                            a = 2 * k + a2
                            for e in range(E):
                                o = 2 * HD * a2 + HD * e
                                for b in range(B):
                                    nc.tensor.matmul(PS[o:o + HD, WB + k, b * HD:b * HD + HD],
                                                     KHX[p][HD * a:HD * a + HD, e, b, :],
                                                     GL[p][HD * a:HD * a + HD, b, :],
                                                     start=False, stop=True, skip_group_check=True)
                    nc.tensor.matmul(PS[:, BB, 0:B * HD], ones_blk[:, :], GL[p].rearrange("p b d -> p (b d)"),
                                     start=False, stop=True, skip_group_check=True).then_inc(q["upd"], 1)

                def body(c, p):
                    o = 1 - p
                    done, now, nxt = value(pe, c), value(pe, c + 1), value(pe, c + 2)
                    before = value(pe, c - 1) if past(c, 2) else None
                    if past(c, 1):
                        pe.wait_ge(q["init"], 1)
                        pe.wait_ge(q["gl"], done)
                        pe.wait_ge(q["am"], done)
                        pe.wait_ge(q["s1"], now)
                        grads(ZW, ZB[p], o, 1).then_inc(q["corr"], 1)
                        pe.wait_ge(q["init"], 1)
                        pe.wait_ge(q["khx"], done)
                        pe.wait_ge(q["bcopy"], done)
                        update(o)
                        grads(HD, QB[o], o, 0).then_inc(q["attn"], 1)
                    else:
                        base(0, 0, 1, 1)
                    if not is_last(c):
                        base(c + 1, o, nxt, now)
                    pe.wait_ge(q["init"], 1)
                    pe.wait_ge(q["qt2"], now)
                    pe.wait_ge(q["wcopy"], now)
                    if past(c, 2):
                        pe.wait_ge(q["zq"], before)
                    for b in range(B):
                        for k in range(J):
                            for a2 in range(2):
                                r, a = 2 * HD * a2, 2 * k + a2
                                mm = nc.tensor.matmul(
                                    PS[HD * a:HD * a + HD, QB[p], b * HD:b * HD + HD],
                                    QT2[p][r:r + 64, k * B + b, :, :].rearrange("p e t -> p (e t)"),
                                    R[o][r:r + 64, k, b, 0:HD], start=(b == 0), stop=False,
                                    skip_group_check=True)
                    mm.then_inc(q["qbase"], 1)

                run_chunks(pe, body)
                pe.wait_ge(q["gl"], NC)
                pe.wait_ge(q["am"], NC)
                grads(HD, QB[1], 1, 0).then_inc(q["attn"], 1)

            @block.vector
            def _(dve):
                def rows_of(c, p):
                    dve.wait_ge(q["stage"], c + 1)
                    if past(c, 2):
                        dve.wait_ge(q["khx"], c - 1)
                    nc.vector.transpose(TKH[p].rearrange("p s b d -> p (s b d)"),
                                        TK[p].rearrange("p s b e t -> p (s b e t)")).then_inc(q["tkh"], 1)

                def target_sum(c, p):
                    dve.wait_ge(q["tkh"], c + 1)
                    nc.vector.tensor_reduce(sT, TKH[p][:, 0, :, :], AX.X, ALU.add).then_inc(q["st"], 1)

                def target_center(c, p):
                    dve.wait_ge(q["st"], c + 1)
                    T = TKH[p][:, 0, :, :]
                    nc.vector.scalar_tensor_tensor(T, bc(sT), -1.0 / HD, T, ALU.mult, ALU.add
                                                   ).then_inc(q["tc"], 1)

                def out_rows(c, p):
                    dve.wait_ge(q["attn"], c + 1)
                    nc.vector.tensor_tensor(ZQ[p], PS[:, QB[p], 0:B * HD].rearrange("p (b d) -> p b d", b=B),
                                            Bs[p], ALU.add).then_inc(q["zq"], 1)

                def out_var(c):
                    dve.wait_ge(q["sqq"], c + 1)
                    nc.vector.tensor_reduce(ssq, SQQ, AX.X, ALU.add).then_inc(q["ssq"], 1)

                def out_r(c):
                    dve.wait_ge(q["sdq"], c + 1)
                    nc.vector.reciprocal(sdq, sdq).then_inc(q["rq"], 1)

                def out_turn(c):
                    dve.wait_ge(q["zn"], c + 1)
                    nc.vector.transpose(ZT.rearrange("p b d -> p (b d)"), ZN.rearrange("p b d -> p (b d)")
                                        ).then_inc(q["zt"], 1)

                def body(c, p):
                    zb = PS[:, ZB[p], 0:B * ZW].rearrange("p (b n) -> p b n", b=B)[:, :, 0:HD]
                    flat2 = lambda v: v.rearrange("p s b d -> p (s b) d")
                    if past(c, 1):
                        dve.wait_ge(q["corr"], c + 0)
                    else:
                        dve.wait_ge(q["s1"], 1)
                    dve.wait_ge(q["bcopy"], max(c, 1) if isinstance(c, int) else c + 0)
                    nc.vector.tensor_tensor(ZP[:, 0, :, :], zb, Bs[1 - p] if past(c, 1) else Bs[0], ALU.add
                                            ).then_inc(q["z"], 1)
                    dve.wait_ge(q["z"], c + 1)
                    nc.vector.tensor_tensor(ZP[:, 1, :, :], ZP[:, 0, :, :],
                                            g2row.unsqueeze(1).broadcast_to([P, B, HD]), ALU.mult
                                            ).then_inc(q["p"], 1)
                    dve.wait_ge(q["sq"], c + 1)
                    nc.vector.tensor_reduce(ss, SQ, AX.X, ALU.add).then_inc(q["ss"], 1)
                    dve.wait_ge(q["p"], c + 1)
                    nc.vector.tensor_reduce(sz, flat2(ZP), AX.X, ALU.add).then_inc(q["sz"], 1)
                    dve.wait_ge(q["sd"], c + 1)
                    if past(c, 2):
                        dve.wait_ge(q["sdq"], c - 1)
                        nc.vector.reciprocal(sds, sds).then_inc(q["r"], 1)
                    else:
                        nc.vector.reciprocal(sd1, sd1).then_inc(q["r"], 1)
                    dve.wait_ge(q["sz"], c + 1)
                    nc.vector.scalar_tensor_tensor(
                        flat2(ZP), sz.unsqueeze(2).broadcast_to([P, 2 * B, HD]), -1.0 / HD, flat2(ZP),
                        ALU.mult, ALU.add).then_inc(q["zc"], 1)
                    dve.wait_ge(q["r"], c + 1)
                    dve.wait_ge(q["zc"], c + 1)
                    nc.vector.tensor_tensor(XP, ZP, sd1.unsqueeze(1).unsqueeze(3).broadcast_to([P, 2, B, HD]),
                                            ALU.mult).then_inc(q["xp"], 1)
                    dve.wait_ge(q["xp"], c + 1)
                    dve.wait_ge(q["tc"], c + 1)
                    nc.vector.tensor_tensor(Y0, XP[:, 1, :, :], TKH[p][:, 0, :, :], ALU.add).then_inc(q["y"], 1)
                    dve.wait_ge(q["y"], c + 1)
                    nc.vector.tensor_tensor(Y1, Y0, XP[:, 0, :, :], ALU.mult).then_inc(q["yp"], 1)
                    dve.wait_ge(q["yp"], c + 1)
                    nc.vector.tensor_reduce(m2, Y1, AX.X, ALU.add).then_inc(q["m"], 1)
                    dve.wait_ge(q["m"], c + 1)
                    dve.wait_ge(q["rl"], c + 1)
                    nc.vector.scalar_tensor_tensor(m2r, m2, -1.0 / HD, rl, ALU.mult, ALU.mult
                                                   ).then_inc(q["mr"], 1)
                    dve.wait_ge(q["mr"], c + 1)
                    nc.vector.tensor_tensor(WX, XP[:, 0, :, :], bc(m2r), ALU.mult).then_inc(q["w"], 1)
                    dve.wait_ge(q["w"], c + 1)
                    dve.wait_ge(q["yl"], c + 1)
                    nc.vector.tensor_tensor(GL[p], WX, YL, ALU.add).then_inc(q["gl"], 1)
                    if past(c, 1):
                        out_rows(c - 1, 1 - p)
                    if past(c, 2):
                        out_turn(c - 2)
                    if not is_last(c):
                        rows_of(c + 1, 1 - p)
                        target_sum(c + 1, 1 - p)
                    if past(c, 1):
                        out_var(c - 1)
                    if not is_last(c):
                        target_center(c + 1, 1 - p)

                rows_of(0, 0)
                target_sum(0, 0)
                target_center(0, 0)
                run_chunks(dve, body)
                out_rows(NC - 1, 1)
                out_r(NC - 2)
                dve.wait_ge(q["ot"], NC - 2)
                out_turn(NC - 2)
                out_var(NC - 1)
                out_r(NC - 1)
                dve.wait_ge(q["ot"], NC - 1)
                out_turn(NC - 1)

            @block.gpsimd
            def _(pool):
                def prepare(c, p):
                    if past(c, 2):
                        pool.wait_ge(q["base"], c - 1)
                    nc.gpsimd.tensor_tensor(
                        KT2[p], chunk(KP, c).unsqueeze(2).broadcast_to([P, J * B, E, CS]),
                        ccol("emask_k").unsqueeze(1).unsqueeze(3).broadcast_to([P, J * B, E, CS]),
                        ALU.mult).then_inc(q["kt2"], 1)
                    nc.gpsimd.tensor_copy(R[p].rearrange("p k b n -> p (k b) n")[:, :, HD:HD + CS],
                                          chunk(QP, c)).then_inc(q["qr"], 1)
                    if past(c, 2):
                        pool.wait_ge(q["tkh"], c - 1)
                    nc.gpsimd.tensor_copy(TK[p][:, 0, :, :, :].rearrange("p b e t -> p e b t"),
                                          TT.rearrange("p e (b n) -> p e b n", b=B)[:, :, :, ds(c * CS, CS)])
                    nc.gpsimd.tensor_copy(TK[p][:, 1, :, :, :].rearrange("p b e t -> p e b t"),
                                          KN.rearrange("p e (b n) -> p e b n", b=B)[:, :, :, ds(c * CS, CS)]
                                          ).then_inc(q["stage"], 1)

                def khx(c, p):
                    pool.wait_ge(q["tkh"], c + 1)
                    if past(c, 2):
                        pool.wait_ge(q["upd"], c - 1)
                    nc.gpsimd.tensor_tensor(
                        KHX[p], TKH[p][:, 1, :, :].unsqueeze(1).broadcast_to([P, E, B, HD]),
                        upd_mask.unsqueeze(2).unsqueeze(3).broadcast_to([P, E, B, HD]), ALU.mult
                    ).then_inc(q["khx"], 1)

                def masks(c, p):
                    pool.wait_ge(q["s1"], c + 1)
                    if past(c, 2):
                        pool.wait_ge(q["attn"], c - 1)
                    nc.gpsimd.tensor_tensor(
                        AM[p].rearrange("p b s e t -> p (b s) e t"),
                        S1[p].unsqueeze(2).broadcast_to([P, 2 * B, E, CS]),
                        mask2.rearrange("p (k e t) -> p k e t", e=E, t=CS), ALU.mult).then_inc(q["am"], 1)

                def out_norm(c, p):
                    nc.gpsimd.tensor_tensor(ZN, ZQ[p], bc(sdq), ALU.mult).then_inc(q["zn"], 1)

                def body(c, p):
                    if not near_end(c):
                        prepare(c + 2, p)
                    pool.wait_ge(q["r"], c + 1)
                    nc.gpsimd.tensor_tensor(rl, sd1, lrh[:, ds(c, 1), :].squeeze(1), ALU.mult
                                            ).then_inc(q["rl"], 1)
                    pool.wait_ge(q["rl"], c + 1)
                    pool.wait_ge(q["y"], c + 1)
                    nc.gpsimd.tensor_tensor(YL, Y0, bc(rl), ALU.mult).then_inc(q["yl"], 1)
                    if past(c, 2):
                        out_norm(c - 2, p)
                    khx(c, p)
                    if not is_last(c):
                        masks(c + 1, 1 - p)

                prepare(0, 0)
                prepare(1, 1)
                masks(0, 0)
                run_chunks(pool, body)
                for c in (NC - 2, NC - 1):
                    pool.wait_ge(q["rq"], c - NC + 3)
                    out_norm(c, c % 2)

            @block.scalar
            def _(act):
                wb = PS[:, WB:WB + J, 0:B * HD].rearrange("p k (b d) -> p k b d", b=B)

                def state_w(p):
                    for k in range(J):
                        w = nc.scalar.activation(R[p][:, k, :, 0:HD], wb[:, k, :, :], ACT.Copy)
                    return w

                def state_b(p):
                    nc.scalar.activation(Bs[p], PS[:, BB, 0:B * HD].rearrange("p (b d) -> p b d", b=B),
                                         ACT.Copy).then_inc(q["bcopy"], 1)

                def next_k(c, p):
                    if past(c, 2):
                        act.wait_ge(q["base"], c - 1)
                    nc.scalar.activation(R[p].rearrange("p k b n -> p (k b) n")[:, :, HD + CS:ZW],
                                         chunk(KP, c + 1), ACT.Copy).then_inc(q["kr"], 1)

                def qt2(c, p):
                    if past(c, 2):
                        act.wait_ge(q["qbase"], c - 1)
                    for e in range(E):
                        a = nc.scalar.activation(QT2[p][:, :, e, :], chunk(QP, c), ACT.Copy,
                                                 scale=ccol("emask_k", e, 1))
                    a.then_inc(q["qt2"], 1)

                def products(c, p):
                    act.wait_ge(q["base"], c + 1)
                    nc.scalar.activation(
                        S1[p].rearrange("p (b s) t -> p b (s t)", b=B),
                        PS[:, ZB[p], 0:B * ZW].rearrange("p (b n) -> p b n", b=B)[:, :, HD:ZW],
                        ACT.Identity, bias=one).then_inc(q["s1"], 1)

                def out_square(c, p):
                    act.wait_ge(q["zq"], c + 1)
                    nc.scalar.activation(SQQ, ZQ[p], ACT.Square).then_inc(q["sqq"], 1)

                def out_sd(c):
                    act.wait_ge(q["ssq"], c + 1)
                    nc.scalar.activation(sdq, ssq, ACT.Sqrt, bias=eps6, scale=1.0 / HD).then_inc(q["sdq"], 1)

                def out_store(c):
                    act.wait_ge(q["zt"], c + 1)
                    nc.scalar.activation(
                        TT.rearrange("p e (b n) -> p e b n", b=B)[:, :, :, ds(c * CS, CS)],
                        ZT.rearrange("p b (e t) -> p e b t", e=E), ACT.Copy).then_inc(q["ot"], 1)

                def body(c, p):
                    act.wait_ge(q["z"], c + 1)
                    nc.scalar.activation(SQ, ZP[:, 0, :, :], ACT.Square).then_inc(q["sq"], 1)
                    act.wait_ge(q["ss"], c + 1)
                    nc.scalar.activation(sd1, ss, ACT.Sqrt, bias=eps6, scale=1.0 / HD).then_inc(q["sd"], 1)
                    if past(c, 1):
                        act.wait_ge(q["upd"], c + 0)
                        state_w(1 - p).then_inc(q["wcopy"], 1)
                        state_b(p)
                    if not is_last(c):
                        products(c + 1, 1 - p)
                        qt2(c + 1, 1 - p)
                    if not isinstance(c, int) or c + 3 < NC:
                        next_k(c + 2, p)
                    if past(c, 1):
                        out_square(c - 1, 1 - p)
                        out_sd(c - 1)
                    if past(c, 2):
                        out_store(c - 2)

                next_k(0, 0)
                next_k(1, 1)
                act.wait_ge(q["init"], 1)
                state_w(0)
                state_w(1).then_inc(q["wcopy"], 1)
                state_b(0)
                products(0, 0)
                qt2(0, 0)
                run_chunks(act, body)
                out_square(NC - 1, 1)
                out_sd(NC - 1)
                out_store(NC - 2)
                out_store(NC - 1)

            @block.sync
            def _(sp):
                for k in range(J):
                    for a2 in range(2):
                        for e in range(E):
                            a = 2 * k + a2
                            r = 2 * HD * a2 + HD * e
                            sp.dma_start(X[HD * a:HD * a + HD, e, :], QP[r:r + HD, k, :]).then_inc(s_qperm, 16)
                sp.wait_ge(s_qperm, 16 * 2 * J * E)

        carve = Carve()
        sq, sd = carve(J, BLK), carve(BLK)
        with nc.Block() as block:
            s_pre, s_wo, s_o, s_oc, s_x1, s_st2 = (sem(n) for n in ("pre", "wo", "o", "oc", "x1", "stats2"))
            s_xr = [sem(f"xr{b}") for b in range(B)]

            def gain(act, i, j):
                return nc.scalar.activation(blk_of(TT[:, j, :], i), blk_of(TT[:, j, :], i), ACT.Identity,
                                            scale=pcol("g", j), bias=pcol("bb", j))

            q2, ot, act_a, pe_mean, dve_center, act_square, pe_var, act_sd, dve_scale, act_affine, _, _ = \
                layer_norm("ln2", TT, sq, sd, eps6, "post_w", "post_b", gain,
                           ready=s_pre)

            @block.sync
            def _(sp):
                sp.dma_start(wsm[:, :, :], wo).then_inc(s_wo, 16)
                for b in range(B):
                    sp.dma_start(KN[:, :, b * N:(b + 1) * N], xv[:, :, b, :]).then_inc(s_xr[b], 16)

            @block.tensor
            def _(pe):
                pe.wait_ge(s_wo, 16)

                def body(i, first):
                    if has(i, 2):
                        pe_mean(pe, i + 2, False)
                    if has(i, 1):
                        pe_var(pe, i + 1, False)
                    pe.wait_ge(q2["xn"], i * J + J)
                    for m in range(J):
                        if not first:
                            pe.wait_ge(s_oc, (i - 1) * J + m + 1)
                        for j in range(J):
                            mm = nc.tensor.matmul(PS[:, 2 + m, :], wsm[:, j, m * P:(m + 1) * P], ot(i, j),
                                                  start=(j == 0), stop=(j == J - 1))
                        mm.then_inc(s_o, 1)

                pe_mean(pe, 0, True)
                pe_mean(pe, 1, False)
                pe_var(pe, 0, True)
                body(0, True)
                with pe.Fori(1, NBLK - 2) as i:
                    body(i, False)
                body(NBLK - 2, False)
                body(NBLK - 1, False)

            @block.vector
            def _(dve):
                dve_center(dve, 0)
                dve_center(dve, 1)
                dve_scale(dve, 0)
                def statistics(i):
                    for m in range(J):
                        dve.wait_ge(s_x1, i * J + m + 1)
                        nc.vector.bn_stats(stat.rearrange("p (k s) -> p k s", s=6)[:, ds(i * J + m, 1), :].squeeze(1),
                                           blk_of(KN[:, m, :], i)).then_inc(s_st2, 1)

                dve_center(dve, 2)
                dve_scale(dve, 1)
                with dve.Fori(1, NBLK - 2) as i:
                    dve_center(dve, i + 2)
                    dve_scale(dve, i + 1)
                    statistics(i - 1)
                dve_scale(dve, NBLK - 1)
                for i in range(NBLK - 3, NBLK):
                    statistics(i)

            @block.gpsimd
            def _(pool):
                def pre(i):
                    for j in range(J):
                        gained = value(pool, i * J + (j + 1))
                        pool.wait_ge(s_k0, 2)
                        pool.wait_ge(q2["in"], gained)
                        nc.gpsimd.tensor_tensor(blk_of(TT[:, j, :], i), blk_of(TT[:, j, :], i),
                                                blk_of(X[:, j, :], i), ALU.add).then_inc(s_pre, 1)

                for i in range(4):
                    pre(i)
                for b in range(B):
                    pool.wait_ge(s_xr[b], 16)
                def residual(i):
                    for m in range(J):
                        made = value(pool, i * J + (m + 1))
                        pool.wait_ge(s_k0, 2)
                        pool.wait_ge(s_oc, made)
                        nc.gpsimd.tensor_tensor(blk_of(KN[:, m, :], i), blk_of(X[:, m, :], i),
                                                blk_of(KN[:, m, :], i), ALU.add).then_inc(s_x1, 1)

                with pool.Fori(0, NBLK - 4) as i:
                    pre(i + 4)
                    residual(i)
                for i in range(NBLK - 4, NBLK):
                    residual(i)

            @block.scalar
            def _(act):
                def output(i):
                    for m in range(J):
                        act.wait_ge(s_o, i * J + m + 1)
                        nc.scalar.activation(blk_of(X[:, m, :], i), PS[:, 2 + m, :], ACT.Copy
                                             ).then_inc(s_oc, 1)

                def body(i):
                    if not isinstance(i, int) or i > 0:
                        output(i - 1)
                    if has(i, 1):
                        act_sd(act, i + 1, False)
                    if has(i, 2):
                        act_square(act, i + 2, False)
                    if has(i, 4):
                        act_a(act, i + 4)
                    if has(i, 1):
                        act_affine(act, i + 1)

                for i in range(4):
                    act_a(act, i)
                act_square(act, 0, True)
                act_sd(act, 0, True)
                act_square(act, 1, False)
                act_affine(act, 0)
                body(0)
                with act.Fori(1, NBLK - 4) as i:
                    body(i)
                for i in range(NBLK - 4, NBLK):
                    body(i)
                output(NBLK - 1)

        with nc.Block() as block:
            group_norm(block, KN, "gn2", have_stats=True)

        flat = lambda t: t[:, :, :].rearrange("p j n -> p (j n)")
        NXP = J * XW * W_
        XP = [flat(KP)[:, s * NXP:(s + 1) * NXP].rearrange("p (j r x) -> p j r x", j=J, x=W_)
              for s in range(3)]
        NG = NRB * RW * XW
        G = flat(QP)[:, 0:NG]
        STAGES = [(NRB, RW * XW, 2 * XW, (RW - 2) * XW), (NRB, (RW - 2) * XW, XW, KS * XW),
                  (NRB * KS, XW, 16, 20), (NRB * KS, 20, 8, 12), (NRB * KS, 12, 4, 8),
                  (NRB * KS, 8, 2, 6), (NRB * KS, 6, 1, KS)]
        carve = Carve()
        DST, SRC = [], [G.rearrange("p (r w) -> p r w", w=RW * XW)]
        at = [flat(QP), NG]
        for k, (r, w, _, kept) in enumerate(STAGES):
            n = r * kept
            if at[1] + n > J * NT:
                at = [flat(TT), 0]
            DST.append(at[0][:, at[1]:at[1] + n].rearrange("p (r w) -> p r w", w=kept))
            if k + 1 < len(STAGES):
                SRC.append(at[0][:, at[1]:at[1] + n].rearrange("p (r w) -> p r w", w=STAGES[k + 1][1]))
            at[1] += n
        TMP = [flat(X)[:, k * 2048:k * 2048 + r * kept].rearrange("p (r w) -> p r w", w=kept)
               for k, (r, w, _, kept) in zip((0, 1, 2, 0, 1, 2, 0), STAGES)]
        YB = [flat(TT)[:, 4096 + s * 2048:4096 + (s + 1) * 2048].rearrange("p (k n) -> p k n", k=PER * J)
              for s in range(2)]
        DN = carve(NRB, S)
        DSQ = carve(NRB, S)
        nrm = carve(NRB)
        DT = carve(N)
        wsw = carve(C)
        ov = out.rearrange("b (j p) n -> p j b n", p=P)

        with nc.Block() as block:
            (s_w2, s_pad, s_xg, s_gram, s_gs, s_tmp, s_st, s_dsq, s_dss, s_dsd, s_dr, s_dn, s_dt, s_dtc,
             s_conv, s_relu, s_y) = (
                sem(n) for n in ("w2", "pad", "xg", "gram", "gs", "btmp", "bstage", "dsq", "dss", "dsd", "dr",
                                 "dn", "dt", "dtc", "conv", "relu", "yfin"))
            s_out = [sem(f"out{s}") for s in range(2)]
            NS = len(STAGES)
            CV = PER * J
            CB = (2, 3, 6, 7)

            @block.sync
            def _(sp):
                sp.dma_start(wsm[:, :, :], wx).then_inc(s_w2, 16)
                sp.dma_start(wsw[0:S, :], ws).then_inc(s_w2, 16)

                def store(b, p, h):
                    sp.wait_ge(s_y, b * CV + (h + 1) * J)
                    for o in range(J):
                        sp.dma_start(ov[:, o, ds(b, 1), h * BLK:(h + 1) * BLK].rearrange("p b n -> p (b n)"),
                                     YB[p][:, h * J + o, :]).then_inc(s_out[p], 16)
                with sp.Fori(0, B // 2) as pair:
                    b = pair * 2
                    for p in range(2):
                        for h in range(PER):
                            store(b + p, p, h)
                for p in range(2):
                    sp.wait_ge(s_out[p], 16 * CV * B // 2)

            @block.gpsimd
            def _(pool):
                for p in range(3):
                    nc.gpsimd.memset(XP[p][:, :, 0:PAD, :], 0.0)
                    nc.gpsimd.memset(XP[p][:, :, XW - PAD:XW, :], 0.0)
                g3 = G.rearrange("p (r x) -> p r x", x=XW)
                nc.gpsimd.memset(g3[:, :, 0:PAD], 0.0)
                nc.gpsimd.memset(g3[:, :, XW - PAD:XW], 0.0).then_inc(s_pad, 1)

                def fin(b, p, k):
                    h, o = divmod(k, J)
                    pool.wait_ge(s_relu, b * CV + k + 1)
                    nc.gpsimd.tensor_tensor(YB[p][:, k, :], YB[p][:, k, :],
                                            KN[:, o, ds(b * N + h * BLK, BLK)], ALU.add).then_inc(s_y, 1)
                with pool.Fori(0, B // 2) as pair:
                    b = pair * 2
                    for p in range(2):
                        for k in range(CV):
                            fin(b + p, p, k)

            @block.tensor
            def _(pe):
                pe.wait_ge(s_w2, 32)
                pe.wait_ge(s_pad, 1)

                def gram(b):
                    pe.wait_ge(s_xg, b * J + J)
                    for rb in range(NRB):
                        if b or rb >= 2:
                            pe.wait_ge(s_gs, b * NRB + rb - 1)
                        for j in range(J):
                            mm = nc.tensor.matmul(
                                PS[:, rb % 2, 0:RW * W_],
                                XP[b % 3][:, j, PAD + RB * rb:PAD + RB * rb + RB, :].rearrange("p r x -> p (r x)"),
                                XP[b % 3][:, j, RB * rb:RB * rb + RW, :].rearrange("p r x -> p (r x)"),
                                start=(j == 0), stop=(j == J - 1))
                        mm.then_inc(s_gram, 1)

                def conv(b):
                    for k in range(CV):
                        h, o = divmod(k, J)
                        if b:
                            pe.wait_ge(s_relu, (b - 1) * CV + k + 1)
                        for j in range(J):
                            nc.tensor.matmul(PS[:, CB[k], :], wsm[:, j, o * P:(o + 1) * P],
                                             XP[b % 3][:, j, PAD + 16 * h:PAD + 16 * h + 16, :].rearrange(
                                                 "p r x -> p (r x)"), start=(j == 0), stop=False)
                    pe.wait_ge(s_dn, b + 1)
                    if b:
                        pe.wait_ge(s_dtc, b * 2)
                    for rb in range(NRB):
                        tr = nc.tensor.transpose(PS[0:S, 4 + rb // 4, (rb % 4) * P:(rb % 4 + 1) * P],
                                                 DN[:, rb, :], ident)
                        if rb % 4 == 3:
                            tr.then_inc(s_dt, 1)
                    for k in range(CV):
                        h, o = divmod(k, J)
                        pe.wait_ge(s_dtc, b * 2 + h + 1)
                        nc.tensor.matmul(PS[:, CB[k], :], wsw[0:S, o * P:(o + 1) * P],
                                         DT[0:S, h * BLK:(h + 1) * BLK], start=False, stop=True
                                         ).then_inc(s_conv, 1)

                gram(0)
                for b in range(B):
                    if b + 1 < B:
                        gram(b + 1)
                    conv(b)

            @block.vector
            def _(dve):
                def body(b, first):
                    for k, (r, w, sh, kept) in enumerate(STAGES):
                        if k == 0:
                            dve.wait_ge(s_gs, b * NRB + NRB)
                        else:
                            dve.wait_ge(s_st, b * NS + k)
                        nc.vector.tensor_scalar(TMP[k], SRC[k][:, :, sh:sh + kept], ccol("shift_on", k, 1), None,
                                                ALU.mult).then_inc(s_tmp, 1)
                        dve.wait_ge(s_tmp, b * NS + k + 1)
                        nc.vector.scalar_tensor_tensor(DST[k], SRC[k][:, :, 0:kept], ccol("shift_off", k, 1),
                                                       TMP[k], ALU.mult, ALU.add).then_inc(s_st, 1)
                    dve.wait_ge(s_st, b * NS + NS)
                    D = DST[-1].rearrange("p (a r) w -> p a (r w)", r=KS)
                    nc.vector.tensor_tensor(DSQ, D, D, ALU.mult).then_inc(s_dsq, 1)
                    dve.wait_ge(s_dsq, b + 1)
                    nc.vector.tensor_reduce(nrm, DSQ, AX.X, ALU.add).then_inc(s_dss, 1)
                    dve.wait_ge(s_dsd, b + 1)
                    nc.vector.reciprocal(nrm, nrm).then_inc(s_dr, 1)
                    dve.wait_ge(s_dr, b + 1)
                    if not first:
                        dve.wait_ge(s_dt, b * 2)
                    nc.vector.tensor_tensor(DN, D, nrm.unsqueeze(2).broadcast_to([P, NRB, S]), ALU.mult
                                            ).then_inc(s_dn, 1)

                body(0, True)
                with dve.Fori(1, B) as b:
                    body(b, False)

            @block.scalar
            def _(act):
                def scale(b):
                    if b >= 3:
                        act.wait_ge(s_conv, (b - 2) * CV)
                    for j in range(J):
                        nc.scalar.activation(
                            XP[b % 3][:, j, PAD:PAD + H, :].rearrange("p r x -> p (r x)"),
                            KN[:, j, b * N:(b + 1) * N], ACT.Identity, scale=gn_a[:, b * J + j:b * J + j + 1],
                            bias=gn_c[:, b * J + j:b * J + j + 1]).then_inc(s_xg, 1)

                def evacuate(b):
                    if b:
                        act.wait_ge(s_st, (b - 1) * NS + 1)
                    for rb in range(NRB):
                        act.wait_ge(s_gram, b * NRB + rb + 1)
                        nc.scalar.activation(
                            G.rearrange("p (a r x) -> p a r x", a=NRB, x=XW)[:, rb, :, PAD:PAD + W_],
                            PS[:, rb % 2, 0:RW * W_].rearrange("p (r x) -> p r x", x=W_), ACT.Copy
                        ).then_inc(s_gs, 1)

                def norm(b):
                    act.wait_ge(s_dss, b + 1)
                    nc.scalar.activation(nrm, nrm, ACT.Sqrt, bias=eps6).then_inc(s_dsd, 1)

                def descriptor(b):
                    if b:
                        act.wait_ge(s_conv, b * CV)
                    for h in range(2):
                        act.wait_ge(s_dt, b * 2 + h + 1)
                        nc.scalar.activation(DT[0:S, h * BLK:(h + 1) * BLK], PS[0:S, 4 + h, :], ACT.Copy
                                             ).then_inc(s_dtc, 1)

                def relu(b):
                    p = b % 2
                    if b >= 2:
                        act.wait_ge(s_out[p], (b // 2) * 16 * CV)
                    for k in range(CV):
                        h, o = divmod(k, J)
                        act.wait_ge(s_conv, b * CV + k + 1)
                        nc.scalar.activation(YB[p][:, k, :], PS[:, CB[k], :], ACT.Relu,
                                             bias=pcol("conv_b", o)).then_inc(s_relu, 1)

                scale(0)
                scale(1)
                evacuate(0)
                scale(2)
                for b in range(B):
                    if b + 1 < B:
                        evacuate(b + 1)
                    norm(b)
                    if 3 <= b + 2 < B:
                        scale(b + 2)
                    descriptor(b)
                    relu(b)


def constants():
    p = np.arange(P)
    row_e, row_t = (p // CS) % E, p % CS
    c = {}
    c["ident"] = np.eye(P)
    c["mean_c"] = np.full((P, P), 1.0 / C)
    c["mean_g"] = (p[:, None] // GROUP == p[None, :] // GROUP) / GROUP
    c["chunk_ones"] = p[:, None] // CS == p[None, :] // CS
    c["emask"] = row_e[:, None] == np.arange(E)
    c["emask_k"] = ((p // HD) % E)[:, None] == np.arange(E)
    col_e, col_t = np.divmod(np.arange(E * CS), CS)
    c["causal"] = (row_e[:, None] == col_e) & (row_t[:, None] <= col_t)
    c["inv_t"] = np.broadcast_to((1.0 / np.arange(1, CS + 1, dtype=np.float32)), (P, CS))
    r, xx = np.divmod(p, W_)
    bits = np.stack([(r >> 1) & 1, r & 1] + [(xx >> k) & 1 for k in (4, 3, 2, 1, 0)], 1)
    c["shift_on"], c["shift_off"] = bits, 1 - bits
    c["spread"] = np.concatenate([(p[:, None] == n * CS + col_t[None, :]) * (col_e == e) / HD
                                  for n in range(8) for e in range(E)], 1)
    table = np.concatenate([np.asarray(c[k], np.float32).reshape(P, w) for k, w in CONST.items()], 1)
    inv = (1.0 / 10000.0 ** (np.arange(0, HD, 2, dtype=np.float32) / np.float32(HD))).astype(np.float32)
    angle = np.arange(N, dtype=np.float32)[None, :] * inv[:, None]
    cos, sin = np.cos(angle), np.sin(angle)
    rope = np.stack([np.tile(np.concatenate([cos, cos]), (P // HD, 1)),
                     np.tile(np.concatenate([-sin, sin]), (P // HD, 1))], 1)
    return np.ascontiguousarray(table), np.ascontiguousarray(rope.astype(np.float32))


def kernel(x, L0_conv_ln_w, L0_conv_ln_b, L0_conv_q_w, L0_conv_k_w, L0_conv_v_w, L0_conv_o_w, L0_conv_W1,
           L0_conv_b1, L0_conv_ttt_ln_w, L0_conv_ttt_ln_b, L0_conv_lr_w, L0_conv_lr_b,
           L0_conv_tok_idx_delta, L0_conv_post_w, L0_conv_post_b, L1_conv_W, L1_conv_bias):
    import concourse.bacc as bacc
    from concourse.bass_utils import run_bass_kernel_spmd

    a = np.asarray
    paired = [4 * e + 2 * k + a2 for k in range(J) for a2 in range(2) for e in range(E)]
    rows = [4 * e + g for g in range(4) for e in range(E)]

    def stationary(w):
        return np.ascontiguousarray(a(w).T.reshape(J, P, -1).transpose(1, 0, 2))

    def by_head(w):
        return a(w).reshape(NH, HD, C)[paired].reshape(C, C)

    def channels(v):
        return a(v).reshape(J, P).T

    pars = dict(
        ln_w=channels(L0_conv_ln_w), ln_b=channels(L0_conv_ln_b), post_w=channels(L0_conv_post_w),
        post_b=channels(L0_conv_post_b), conv_b=channels(L1_conv_bias),
        g=channels(a(L0_conv_ttt_ln_w).reshape(C)), bb=channels(a(L0_conv_ttt_ln_b).reshape(C)),
        g_row=np.repeat(a(L0_conv_ttt_ln_w)[rows], CS, 0),
        b1_row=np.repeat(a(L0_conv_b1).reshape(NH, HD)[rows], CS, 0),
        delta=np.tile(a(L0_conv_tok_idx_delta)[None], (P, 1)),
        lr_b=np.tile(a(L0_conv_lr_b).reshape(NH, 1), (P // NH, 1)),
        w1=a(L0_conv_W1)[paired].reshape(J, P, HD).transpose(1, 0, 2).reshape(P, J * HD),
    )
    table, rope = constants()
    arrays = dict(
        x=np.ascontiguousarray(a(x).reshape(B, C, N)),
        wq=stationary(by_head(L0_conv_q_w)), wk=stationary(by_head(L0_conv_k_w)),
        wv=stationary(L0_conv_v_w), wo=stationary(L0_conv_o_w),
        wlr=stationary(a(L0_conv_lr_w).reshape(NH, C)),
        wx=stationary(a(L1_conv_W)[:, :C]), ws=np.ascontiguousarray(a(L1_conv_W)[:, C:].T),
        params=np.ascontiguousarray(np.concatenate([pars[k] for k in PARAM], 1)),
        consts=table, rope=rope)

    nc = bacc.Bacc("TRN2", target_bir_lowering=False, num_devices=1)
    order = ["x", "wq", "wk", "wv", "wo", "wlr", "wx", "ws", "params", "consts", "rope"]
    aps = {k: nc.dram_tensor(f"in_{k}", arrays[k].shape, F32, kind="ExternalInput").ap() for k in order}
    o = nc.dram_tensor("out_0", (B, C, N), F32, kind="ExternalOutput").ap()
    build(nc, aps["x"], o, aps["wq"], aps["wk"], aps["wv"], aps["wo"], aps["wlr"], aps["wx"], aps["ws"],
          aps["params"], aps["consts"], aps["rope"])
    r = run_bass_kernel_spmd(nc, [{f"in_{k}": arrays[k] for k in order}], core_ids=[0])
    return r.results[0]["out_0"].reshape(B, C, H, W_)
```
